# Optimizing a Trainium2 kernel written in Bass

```python
import numpy as np
import jax
import jax.numpy as jnp

def _softmax(x, axis=-1):
    return jax.nn.softmax(x, axis=axis)

def _gelu(x):
    return jax.nn.gelu(x, approximate=True)

def _silu(x):
    return jax.nn.silu(x)

def _sigmoid(x):
    return jax.nn.sigmoid(x)

def _layernorm(x, axis=-1, eps=1e-05):
    m = jnp.mean(x, axis=axis, keepdims=True)
    v = jnp.var(x, axis=axis, keepdims=True)
    return (x - m) / jnp.sqrt(v + eps)

def _scatter_add(tgt, idx, src, axis=0):
    return tgt.at[idx].add(src)

def _segment_sum(src, seg, n):
    return jax.ops.segment_sum(src, seg, n)
kernel_name = 'mk_flamingo_gated_d2_seqx_r8_6e9077'

def setup_inputs(seed: int=0):
    np.random.seed(seed)
    _w = jnp.asarray

    def _rec_inputs():
        import jax
        import jax.numpy as jnp
        _rk = jax.random.key(seed)
        x = -0.0003929 + 0.9999 * jax.random.normal(jax.random.fold_in(_rk, 1), (8, 128, 128), jnp.float32)
        _lenS = 128 - jax.random.randint(jax.random.fold_in(_rk, 7), (8,), 0, max(1, 128 // 4) + 1, jnp.int32)
        _lenS2 = 128 - jax.random.randint(jax.random.fold_in(_rk, 8), (8,), 0, max(1, 128 // 4) + 1, jnp.int32)
        _ctx_768P = jax.random.normal(jax.random.fold_in(_rk, 11), (8, 16, 96), jnp.float32)
        _ctx_768c = jax.random.dirichlet(jax.random.fold_in(_rk, 511), 0.3 * jnp.ones((16,), jnp.float32), (8, 128))
        _ctx_768t = jnp.einsum('bsk,bkd->bsd', _ctx_768c, _ctx_768P)
        _ctx_768t = _ctx_768t * jax.lax.rsqrt(jnp.mean(jnp.square(_ctx_768t)) + 1e-12) * 0.953939
        ctx_768 = -7.36909e-05 + 0.999899 * (_ctx_768t + 0.3 * jax.random.normal(jax.random.fold_in(_rk, 611), (8, 128, 96), jnp.float32))
        _g = jax.random.normal(jax.random.fold_in(_rk, 9001), (2, 2), jnp.float32)
        _g = jnp.sign(_g) * jnp.maximum(jnp.abs(_g), 1.0) + (_g == 0) * 1.0
        g_xattn = _g[0]
        g_ffn = _g[1]
        return (x, ctx_768, g_xattn, g_ffn)
    x, ctx_768, g_xattn, g_ffn = _rec_inputs()

    def _L0_xattn_setup():
        import jax, jax.numpy as jnp
        import numpy as np
        EPS = 1e-08
        key = jax.random.key(seed)
        kv, kt, k1, k2, k3, k4 = jax.random.split(key, 6)
        B, S = (16, 128)
        VD, TD, H = (128, 96, 64)
        visual_features = jax.random.normal(kv, (B, S, VD), dtype=jnp.float32)
        text_features = jax.random.normal(kt, (B, S, TD), dtype=jnp.float32)
        Wv = jax.random.normal(k1, (H, VD), dtype=jnp.float32) * (1.0 / np.sqrt(VD))
        bv = jax.random.normal(k2, (H,), dtype=jnp.float32) * 0.01
        Wt = jax.random.normal(k3, (H, TD), dtype=jnp.float32) * (1.0 / np.sqrt(TD))
        bt = jax.random.normal(k4, (H,), dtype=jnp.float32) * 0.01
        return {'visual_features': visual_features, 'text_features': text_features, 'Wv': Wv, 'bv': bv, 'Wt': Wt, 'bt': bt}
    _L0_xattn_all = _L0_xattn_setup()
    _L0_xattn_in = {k: v for k, v in _L0_xattn_all.items() if k in ('Wv', 'bv', 'Wt', 'bt')}
    del _L0_xattn_all

    def _L0_ffn_setup():
        import jax, jax.numpy as jnp
        import numpy as np
        DIM = 128
        DEPTH = 6
        HEADS = 16
        DIM_HEAD = 64
        WINDOW = 32
        INNER = HEADS * DIM_HEAD
        DIM_INNER = int(DIM * 4 * 2 / 3)
        QK_SCALE = 8.0

        def shift_tokens(t):
            a, s = jnp.split(t, 2, -1)
            s = jnp.pad(s, ((0, 0), (1, 0), (0, 0)))[:, :-1]
            return jnp.concatenate([a, s], -1)

        def l2norm(t):
            return t / jnp.maximum(jnp.linalg.norm(t, axis=-1, keepdims=True), 1e-12)

        def rotate_half(x):
            x1, x2 = jnp.split(x, 2, -1)
            return jnp.concatenate([-x2, x1], -1)

        def rotary_tables(n):
            half = jnp.arange(0, DIM_HEAD, 2, dtype=jnp.float32)
            inv_freq = 1.0 / 10000.0 ** (half / DIM_HEAD)
            t = jnp.arange(n, dtype=jnp.float32)
            freqs = t[:, None] * inv_freq[None, :]
            freqs = jnp.concatenate([freqs, freqs], -1)
            base_scale = (half + 0.4 * DIM_HEAD) / (1.4 * DIM_HEAD)
            power = (t - n // 2) / (WINDOW // 2)
            scale = base_scale[None, :] ** power[:, None]
            scale = jnp.concatenate([scale, scale], -1)
            return (freqs, scale)

        def local_attention(q, k, v):
            b, h, n, d = q.shape
            w = WINDOW
            nw = n // w
            bq = q.reshape(b, h, nw, w, d)
            bk = k.reshape(b, h, nw, w, d)
            bv = v.reshape(b, h, nw, w, d)

            def look(t):
                p = jnp.pad(t, ((0, 0), (0, 0), (1, 0), (0, 0), (0, 0)))
                return jnp.concatenate([p[:, :, :nw], p[:, :, 1:]], axis=3)
            bk2, bv2 = (look(bk), look(bv))
            seq = jnp.arange(n).reshape(nw, w)
            seq_p = jnp.pad(seq, ((1, 0), (0, 0)), constant_values=-1)
            jt = jnp.concatenate([seq_p[:nw], seq_p[1:]], axis=1)
            it = seq[:, :, None]
            jb = jt[:, None, :]
            mask = (it < jb) | (it > jb + w) | (jb == -1)
            sim = jnp.einsum('bhwie,bhwje->bhwij', bq, bk2) * QK_SCALE
            sim = jnp.where(mask, -jnp.finfo(sim.dtype).max, sim)
            attn = jax.nn.softmax(sim, -1)
            out = jnp.einsum('bhwij,bhwje->bhwie', attn, bv2)
            return out.reshape(b, h, n, d)

        def attn_layer(x, Wqkv, qs, ksc, Wo):
            b, n, _ = x.shape
            qkv = x @ Wqkv
            q, k, v = jnp.split(qkv, 3, -1)
            sh = lambda t: t.reshape(b, n, HEADS, DIM_HEAD).transpose(0, 2, 1, 3)
            q, k, v = (sh(q), sh(k), sh(v))
            q = l2norm(q) * qs
            k = l2norm(k) * ksc
            freqs, scale = rotary_tables(n)
            cos, sin = (jnp.cos(freqs), jnp.sin(freqs))
            q = q * cos * scale + rotate_half(q) * sin * scale
            inv = 1.0 / scale
            k = k * cos * inv + rotate_half(k) * sin * inv
            out = local_attention(q, k, v)
            out = out.transpose(0, 2, 1, 3).reshape(b, n, INNER)
            return out @ Wo

        def ffn_layer(x, g, bln, W1, b1, W2, b2):
            mu = x.mean(-1, keepdims=True)
            var = ((x - mu) ** 2).mean(-1, keepdims=True)
            xn = (x - mu) / jnp.sqrt(var + 1e-05) * g + bln
            hg = xn @ W1 + b1
            a, gate = jnp.split(hg, 2, -1)
            return a * jax.nn.gelu(gate, approximate=False) @ W2 + b2
        key = jax.random.key(seed)
        ks = jax.random.split(key, 8)
        B, N = (2, 256)
        init = lambda k, shape: jax.random.normal(k, shape, jnp.float32) * 0.02
        return {'x': jax.random.normal(ks[0], (B, N, DIM), jnp.float32), 'Wqkv': init(ks[1], (DEPTH, DIM, 3 * INNER)), 'q_scale': jnp.ones((DEPTH, DIM_HEAD), jnp.float32), 'k_scale': jnp.ones((DEPTH, DIM_HEAD), jnp.float32), 'Wo': init(ks[2], (DEPTH, INNER, DIM)), 'ln_g': jnp.ones((DEPTH, DIM), jnp.float32), 'ln_b': jnp.zeros((DEPTH, DIM), jnp.float32), 'W1': init(ks[3], (DEPTH, DIM, 2 * DIM_INNER)), 'b1': jnp.zeros((DEPTH, 2 * DIM_INNER), jnp.float32), 'W2': init(ks[4], (DEPTH, DIM_INNER, DIM)), 'b2': jnp.zeros((DEPTH, DIM), jnp.float32)}
    _L0_ffn_all = _L0_ffn_setup()
    _L0_ffn_in = {k: v for k, v in _L0_ffn_all.items() if k in ('Wqkv', 'q_scale', 'k_scale', 'Wo', 'ln_g', 'ln_b', 'W1', 'b1', 'W2', 'b2')}
    del _L0_ffn_all

    def _L1_xattn_setup():
        import jax, jax.numpy as jnp
        import numpy as np
        HEADS = 16
        DIM_HEAD = 64
        key = jax.random.key(seed)
        ks = jax.random.split(key, 8)
        B, S, D = (16, 512, 128)
        K, DE = (77, 96)
        inner = HEADS * DIM_HEAD
        hidden_states = jax.random.normal(ks[0], (B, S, D), dtype=jnp.float32)
        encoder_hidden_states = jax.random.normal(ks[1], (B, K, DE), dtype=jnp.float32)
        sc_q = 1.0 / np.sqrt(D)
        sc_kv = 1.0 / np.sqrt(DE)
        sc_o = 1.0 / np.sqrt(inner)
        Wq = jax.random.normal(ks[2], (D, inner), dtype=jnp.float32) * sc_q
        Wk = jax.random.normal(ks[3], (DE, inner), dtype=jnp.float32) * sc_kv
        Wv = jax.random.normal(ks[4], (DE, inner), dtype=jnp.float32) * sc_kv
        Wo = jax.random.normal(ks[5], (inner, D), dtype=jnp.float32) * sc_o
        bo = jax.random.normal(ks[6], (D,), dtype=jnp.float32) * 0.01
        return {'hidden_states': hidden_states, 'encoder_hidden_states': encoder_hidden_states, 'Wq': Wq, 'Wk': Wk, 'Wv': Wv, 'Wo': Wo, 'bo': bo}
    _L1_xattn_all = _L1_xattn_setup()
    _L1_xattn_in = {k: v for k, v in _L1_xattn_all.items() if k in ('Wq', 'Wk', 'Wv', 'Wo', 'bo')}
    del _L1_xattn_all

    def _L1_ffn_setup():
        import jax, jax.numpy as jnp
        import numpy as np
        B, S, D = (2, 128, 128)
        H = 64
        E = 16
        K = 2
        HS = 2 * H
        ROUTE_SCALE = 1.0

        def _gated_mlp_act(y):
            u, g = jnp.split(y, 2, axis=-1)
            return u * jax.nn.silu(g)
        key = jax.random.key(seed)
        ks = jax.random.split(key, 6)
        s = 0.02
        return {'x': jax.random.normal(ks[0], (B, S, D), dtype=jnp.float32), 'Wg': jax.random.normal(ks[1], (E, D), dtype=jnp.float32) * s, 'W1': jax.random.normal(ks[2], (E, D, 2 * H), dtype=jnp.float32) * s, 'W2': jax.random.normal(ks[3], (E, H, D), dtype=jnp.float32) * s, 'Ws1': jax.random.normal(ks[4], (D, 2 * HS), dtype=jnp.float32) * s, 'Ws2': jax.random.normal(ks[5], (HS, D), dtype=jnp.float32) * s}
    _L1_ffn_all = _L1_ffn_setup()
    _L1_ffn_in = {k: v for k, v in _L1_ffn_all.items() if k in ('Wg', 'W1', 'W2', 'Ws1', 'Ws2')}
    del _L1_ffn_all
    return {'x': x, 'ctx_768': ctx_768, 'g_xattn': g_xattn, 'g_ffn': g_ffn, 'L0_xattn_Wv': _L0_xattn_in['Wv'], 'L0_xattn_bv': _L0_xattn_in['bv'], 'L0_xattn_Wt': _L0_xattn_in['Wt'], 'L0_xattn_bt': _L0_xattn_in['bt'], 'L0_ffn_Wqkv': _L0_ffn_in['Wqkv'], 'L0_ffn_q_scale': _L0_ffn_in['q_scale'], 'L0_ffn_k_scale': _L0_ffn_in['k_scale'], 'L0_ffn_Wo': _L0_ffn_in['Wo'], 'L0_ffn_ln_g': _L0_ffn_in['ln_g'], 'L0_ffn_ln_b': _L0_ffn_in['ln_b'], 'L0_ffn_W1': _L0_ffn_in['W1'], 'L0_ffn_b1': _L0_ffn_in['b1'], 'L0_ffn_W2': _L0_ffn_in['W2'], 'L0_ffn_b2': _L0_ffn_in['b2'], 'L1_xattn_Wq': _L1_xattn_in['Wq'], 'L1_xattn_Wk': _L1_xattn_in['Wk'], 'L1_xattn_Wv': _L1_xattn_in['Wv'], 'L1_xattn_Wo': _L1_xattn_in['Wo'], 'L1_xattn_bo': _L1_xattn_in['bo'], 'L1_ffn_Wg': _L1_ffn_in['Wg'], 'L1_ffn_W1': _L1_ffn_in['W1'], 'L1_ffn_W2': _L1_ffn_in['W2'], 'L1_ffn_Ws1': _L1_ffn_in['Ws1'], 'L1_ffn_Ws2': _L1_ffn_in['Ws2']}

def reference(x, ctx_768, g_xattn, g_ffn, L0_xattn_Wv, L0_xattn_bv, L0_xattn_Wt, L0_xattn_bt, L0_ffn_Wqkv, L0_ffn_q_scale, L0_ffn_k_scale, L0_ffn_Wo, L0_ffn_ln_g, L0_ffn_ln_b, L0_ffn_W1, L0_ffn_b1, L0_ffn_W2, L0_ffn_b2, L1_xattn_Wq, L1_xattn_Wk, L1_xattn_Wv, L1_xattn_Wo, L1_xattn_bo, L1_ffn_Wg, L1_ffn_W1, L1_ffn_W2, L1_ffn_Ws1, L1_ffn_Ws2):
    import jax
    import jax.numpy as jnp

    def _L0_xattn_ref(visual_features, text_features, Wv, bv, Wt, bt):
        import jax, jax.numpy as jnp
        import numpy as np
        EPS = 1e-08
        v = jnp.einsum('bsd,hd->bsh', visual_features, Wv) + bv
        t = jnp.einsum('bsd,hd->bsh', text_features, Wt) + bt
        dots = jnp.einsum('bih,bjh->bij', v, t)
        vn = jnp.linalg.norm(v, axis=-1)
        tn = jnp.linalg.norm(t, axis=-1)
        denom = jnp.maximum(vn[:, :, None] * tn[:, None, :], EPS)
        return dots / denom

    def _L0_ffn_ref(x, Wqkv, q_scale, k_scale, Wo, ln_g, ln_b, W1, b1, W2, b2):
        import jax, jax.numpy as jnp
        import numpy as np
        DIM = 128
        DEPTH = 6
        HEADS = 16
        DIM_HEAD = 64
        WINDOW = 32
        INNER = HEADS * DIM_HEAD
        DIM_INNER = int(DIM * 4 * 2 / 3)
        QK_SCALE = 8.0

        def shift_tokens(t):
            a, s = jnp.split(t, 2, -1)
            s = jnp.pad(s, ((0, 0), (1, 0), (0, 0)))[:, :-1]
            return jnp.concatenate([a, s], -1)

        def l2norm(t):
            return t / jnp.maximum(jnp.linalg.norm(t, axis=-1, keepdims=True), 1e-12)

        def rotate_half(x):
            x1, x2 = jnp.split(x, 2, -1)
            return jnp.concatenate([-x2, x1], -1)

        def rotary_tables(n):
            half = jnp.arange(0, DIM_HEAD, 2, dtype=jnp.float32)
            inv_freq = 1.0 / 10000.0 ** (half / DIM_HEAD)
            t = jnp.arange(n, dtype=jnp.float32)
            freqs = t[:, None] * inv_freq[None, :]
            freqs = jnp.concatenate([freqs, freqs], -1)
            base_scale = (half + 0.4 * DIM_HEAD) / (1.4 * DIM_HEAD)
            power = (t - n // 2) / (WINDOW // 2)
            scale = base_scale[None, :] ** power[:, None]
            scale = jnp.concatenate([scale, scale], -1)
            return (freqs, scale)

        def local_attention(q, k, v):
            b, h, n, d = q.shape
            w = WINDOW
            nw = n // w
            bq = q.reshape(b, h, nw, w, d)
            bk = k.reshape(b, h, nw, w, d)
            bv = v.reshape(b, h, nw, w, d)

            def look(t):
                p = jnp.pad(t, ((0, 0), (0, 0), (1, 0), (0, 0), (0, 0)))
                return jnp.concatenate([p[:, :, :nw], p[:, :, 1:]], axis=3)
            bk2, bv2 = (look(bk), look(bv))
            seq = jnp.arange(n).reshape(nw, w)
            seq_p = jnp.pad(seq, ((1, 0), (0, 0)), constant_values=-1)
            jt = jnp.concatenate([seq_p[:nw], seq_p[1:]], axis=1)
            it = seq[:, :, None]
            jb = jt[:, None, :]
            mask = (it < jb) | (it > jb + w) | (jb == -1)
            sim = jnp.einsum('bhwie,bhwje->bhwij', bq, bk2) * QK_SCALE
            sim = jnp.where(mask, -jnp.finfo(sim.dtype).max, sim)
            attn = jax.nn.softmax(sim, -1)
            out = jnp.einsum('bhwij,bhwje->bhwie', attn, bv2)
            return out.reshape(b, h, n, d)

        def attn_layer(x, Wqkv, qs, ksc, Wo):
            b, n, _ = x.shape
            qkv = x @ Wqkv
            q, k, v = jnp.split(qkv, 3, -1)
            sh = lambda t: t.reshape(b, n, HEADS, DIM_HEAD).transpose(0, 2, 1, 3)
            q, k, v = (sh(q), sh(k), sh(v))
            q = l2norm(q) * qs
            k = l2norm(k) * ksc
            freqs, scale = rotary_tables(n)
            cos, sin = (jnp.cos(freqs), jnp.sin(freqs))
            q = q * cos * scale + rotate_half(q) * sin * scale
            inv = 1.0 / scale
            k = k * cos * inv + rotate_half(k) * sin * inv
            out = local_attention(q, k, v)
            out = out.transpose(0, 2, 1, 3).reshape(b, n, INNER)
            return out @ Wo

        def ffn_layer(x, g, bln, W1, b1, W2, b2):
            mu = x.mean(-1, keepdims=True)
            var = ((x - mu) ** 2).mean(-1, keepdims=True)
            xn = (x - mu) / jnp.sqrt(var + 1e-05) * g + bln
            hg = xn @ W1 + b1
            a, gate = jnp.split(hg, 2, -1)
            return a * jax.nn.gelu(gate, approximate=False) @ W2 + b2
        for i in range(DEPTH):
            x = attn_layer(shift_tokens(x), Wqkv[i], q_scale[i], k_scale[i], Wo[i]) + x
            x = ffn_layer(shift_tokens(x), ln_g[i], ln_b[i], W1[i], b1[i], W2[i], b2[i]) + x
        return x

    def _L1_xattn_ref(hidden_states, encoder_hidden_states, Wq, Wk, Wv, Wo, bo):
        import jax, jax.numpy as jnp
        import numpy as np
        HEADS = 16
        DIM_HEAD = 64
        B, S, D = hidden_states.shape
        K = encoder_hidden_states.shape[1]
        H, Dh = (HEADS, DIM_HEAD)
        scale = 1.0 / np.sqrt(Dh)
        q = hidden_states @ Wq
        k = encoder_hidden_states @ Wk
        v = encoder_hidden_states @ Wv
        q = q.reshape(B, S, H, Dh).transpose(0, 2, 1, 3)
        k = k.reshape(B, K, H, Dh).transpose(0, 2, 1, 3)
        v = v.reshape(B, K, H, Dh).transpose(0, 2, 1, 3)
        scores = jnp.einsum('bhsd,bhkd->bhsk', q, k) * scale
        probs = jax.nn.softmax(scores, axis=-1)
        out = jnp.einsum('bhsk,bhkd->bhsd', probs, v)
        out = out.transpose(0, 2, 1, 3).reshape(B, S, H * Dh)
        out = out @ Wo + bo
        return out

    def _L1_ffn_ref(x, Wg, W1, W2, Ws1, Ws2):
        import jax, jax.numpy as jnp
        import numpy as np
        B, S, D = (2, 128, 128)
        H = 64
        E = 16
        K = 2
        HS = 2 * H
        ROUTE_SCALE = 1.0

        def _gated_mlp_act(y):
            u, g = jnp.split(y, 2, axis=-1)
            return u * jax.nn.silu(g)
        x_shape = x.shape
        xf = x.reshape(-1, D)
        scores = jax.nn.softmax(xf @ Wg.T, axis=-1)
        wk, idx = jax.lax.top_k(scores, K)
        wk = wk * ROUTE_SCALE
        cw = jnp.sum(jax.nn.one_hot(idx, E, dtype=xf.dtype) * wk[..., None], axis=1)
        h = _gated_mlp_act(jnp.einsum('td,edh->teh', xf, W1))
        z = jnp.einsum('te,teh,ehd->td', cw, h, W2)
        ys = _gated_mlp_act(xf @ Ws1) @ Ws2
        return (z + ys).reshape(x_shape)
    x = x + jnp.tanh(g_xattn[0]) * _L0_xattn_ref(_layernorm(x, axis=-1), ctx_768, L0_xattn_Wv, L0_xattn_bv, L0_xattn_Wt, L0_xattn_bt)
    x = x + jnp.tanh(g_ffn[0]) * _L0_ffn_ref(_layernorm(x, axis=-1), L0_ffn_Wqkv, L0_ffn_q_scale, L0_ffn_k_scale, L0_ffn_Wo, L0_ffn_ln_g, L0_ffn_ln_b, L0_ffn_W1, L0_ffn_b1, L0_ffn_W2, L0_ffn_b2)
    x = x + jnp.tanh(g_xattn[1]) * _L1_xattn_ref(_layernorm(x, axis=-1), ctx_768, L1_xattn_Wq, L1_xattn_Wk, L1_xattn_Wv, L1_xattn_Wo, L1_xattn_bo)
    x = x + jnp.tanh(g_ffn[1]) * _L1_ffn_ref(_layernorm(x, axis=-1), L1_ffn_Wg, L1_ffn_W1, L1_ffn_W2, L1_ffn_Ws1, L1_ffn_Ws2)
    return x

_drawn_inputs = setup_inputs


def setup_inputs(seed=0):
    import zlib

    import numpy as np

    out = dict(_drawn_inputs(seed))
    spreads = {'g_ffn': (-1.0, 0.6),
     'L0_ffn_q_scale': (1.0, 0.6),
     'L0_ffn_k_scale': (1.0, 0.6),
     'L0_ffn_ln_g': (1.0, 0.6),
     'L0_ffn_ln_b': (0.0, 0.8),
     'L0_ffn_b1': (0.0, 0.311),
     'L0_ffn_b2': (0.0, 0.1)}
    factors = {'L0_xattn_bv': 22.436,
     'L0_xattn_bt': 52.286,
     'L1_xattn_bo': 3.517,
     'L1_ffn_Wg': 8.0,
     'L1_ffn_W1': 8.0,
     'L1_ffn_W2': 8.0,
     'L1_ffn_Ws1': 6.853,
     'L1_ffn_Ws2': 7.179}
    for name, (base, spread) in spreads.items():
        noise = np.random.default_rng([zlib.crc32(name.encode()), seed]).standard_normal(out[name].shape)
        drawn = base * np.exp(spread * noise) if base else spread * noise
        out[name] = jnp.asarray(drawn.astype(out[name].dtype))
    for name, factor in factors.items():
        out[name] = (out[name] * factor).astype(out[name].dtype)
    return out
```

```python
from contextlib import ExitStack

import numpy as np

import concourse.bass as bass
from concourse import mybir

ALU = mybir.AluOpType
ACT = mybir.ActivationFunctionType
AX = mybir.AxisListType
F32 = mybir.dt.float32
BF16 = mybir.dt.bfloat16
I32 = mybir.dt.int32

B = 8
T = 128
D = 128
DC = 96
HEADS = 16
DH = 64
INNER = HEADS * DH
WINDOW = 32
DEPTH = 6
DFF = int(D * 4 * 2 / 3)
HSIM = 64
E = 16
HE = 64
HG = 4
GPB = HEADS // HG
GPL = B * GPB
LAG = 6
UNROLL = 8
GW = HG * DH
FCH = [(c, min(128, DFF - c)) for c in range(0, DFF, 128)]
NF = len(FCH)
NP = 2 + 2 * NF
RSQRT_SEED = float(0x5F3759DF)
NEWTON = 3
RS_OPS = 1 + 3 * NEWTON
LN_OPS = 5 + RS_OPS
C_ID, C_SH, C_MASK, C_COS, C_SIN, C_IOTA, C_END = 0, 128, 256, 384, 512, 640, 656


def shape_constants():
    c = np.zeros((T, C_END), np.float32)
    c[:, C_ID:C_ID + T] = np.eye(T)
    c[:, C_SH:C_SH + T] = np.eye(T, k=1)
    i, j = np.arange(T)[:, None], np.arange(T)[None, :]
    seen = (j // WINDOW >= i // WINDOW - 1) & (j <= i) & (i <= j + WINDOW)
    c[:, C_MASK:C_MASK + T] = np.where(seen, 0.0, -1e30)
    half = np.arange(0, DH, 2, dtype=np.float32)
    inv = (1.0 / 10000.0 ** (half / DH)).astype(np.float32)
    t = np.arange(T, dtype=np.float32)
    freqs = (t[:, None] * inv[None, :]).astype(np.float32)
    base = ((half + 0.4 * DH) / (1.4 * DH)).astype(np.float32)
    power = ((t - T // 2) / (WINDOW // 2)).astype(np.float32)
    scale = (base[None, :] ** power[:, None]).astype(np.float32)
    cos, sin = np.cos(freqs), np.sin(freqs)
    for n, s in enumerate((8.0 * scale, 1.0 / scale)):
        c[:, C_COS + n * DH:C_COS + (n + 1) * DH] = np.concatenate([cos * s, cos * s], 1)
        c[:, C_SIN + n * DH:C_SIN + (n + 1) * DH] = np.concatenate([-sin * s, sin * s], 1)
    c[:, C_IOTA:C_IOTA + E] = np.arange(E)
    return c


class Steps:

    def __init__(self, sem, credit=0):
        self.sem, self.credit = sem, credit

    def done(self, eng, step):
        eng.wait_ge(self.sem, step + 1 + self.credit)

    def free(self, eng, step, ring):
        assert self.credit >= ring
        eng.wait_ge(self.sem, step + 1 - ring + self.credit)


def build(nc, x, ctx, g_xattn, g_ffn, s_Wv, s_bv, s_Wt, s_bt, Wqkv, q_scale, k_scale, Wo, ln_g, ln_b, W1, b1,
          W2, b2, x_Wq, x_Wk, x_Wv, x_Wo, x_bo, m_Wg, m_W1, m_W2, m_Ws1, m_Ws2, consts, out):
    with ExitStack() as stack:
        def sb(name, shape, dt=F32):
            return stack.enter_context(nc.sbuf_tensor(name, shape, dt))

        def sem(name):
            return stack.enter_context(nc.semaphore(name))

        def steps(name, credit=0):
            return Steps(sem(name), credit)

        cst = sb("cst", [T, C_END])
        ident = cst[:, C_ID:C_ID + T]
        shift = cst[:, C_SH:C_SH + T]
        ident_b = sb("ident_b", [T, T], BF16)
        masks = sb("masks", [T, 2, T], BF16)
        ones = sb("ones", [T, T])
        xbase = sb("xbase", [T, B, D])
        xres = sb("xres", [T, B, D])
        xsh = sb("xsh", [T, B, D])
        xn = sb("xn", [T, B, D])
        xT = sb("xT", [D, B, T])
        xfT = sb("xfT", [D, B, T])
        xcur = sb("xcur", [D, 2, T])
        ctx_sb = sb("ctx_sb", [T, B, DC])
        cT = sb("cT", [DC, B, T])
        ccur = sb("ccur", [DC, 2, T])
        gates = sb("gates", [T, 4])
        tg = sb("tg", [T, 4])
        wv_n = sb("wv_n", [HSIM, D])
        wt_n = sb("wt_n", [HSIM, DC])
        wvT = sb("wvT", [D, HSIM])
        wtT = sb("wtT", [DC, HSIM])
        bvt = sb("bvt", [HSIM, 2])
        vT = sb("vT", [HSIM, B * T])
        tT = sb("tT", [HSIM, B * T])
        vsq = sb("vsq", [HSIM, B * T])
        tsq = sb("tsq", [HSIM, B * T])
        vn2 = sb("vn2", [T, B])
        den = sb("den", [T, B, T])
        wqkv = sb("wqkv", [D, 3 * INNER])
        wo = sb("wo", [D, INNER // 128, D])
        scales = sb("scales", [T, DEPTH, 2, DH])
        tab_cos = sb("tab_cos", [T, 2, DH])
        tab_sin = sb("tab_sin", [T, 2, DH])
        sq = sb("sq", [T, 2, 512])
        rot_a = sb("rot_a", [T, 2, 512])
        rot_b = sb("rot_b", [T, 2, 512])
        rot = sb("rot", [T, 512])
        n2 = sb("n2", [T, 2, 8])
        nt = sb("nt", [T, 8])
        rn = sb("rn", [T, 2, 8])
        q_n = sb("q_n", [T, 2, GW])
        k_z = sb("k_z", [T, 2, 6 * DH])
        qT = sb("qT", [T, 2, 2, T])
        kT = sb("kT", [T, 2, HG, T])
        v_n = sb("v_n", [T, UNROLL, GW])
        negm = sb("negm", [T, 2, HG], BF16)
        probs = sb("probs", [T, 2, HG, T])
        sums = sb("sums", [T, 2, HG])
        rsum = sb("rsum", [T, 2, HG])
        pT = sb("pT", [T, 2, HG, T])
        oT = sb("oT", [T, 2, INNER // 128, T])
        w1 = sb("w1", [D, 2 * DFF])
        w2 = sb("w2", [128, NF, D])
        par_rows = sb("par_rows", [NP * DEPTH, 128])
        lpar_all = sb("lpar_all", [D, NP, DEPTH])
        lpar = sb("lpar", [D, NP])
        b2_all = sb("b2_all", [T, DEPTH, D])
        bo_b = sb("bo_b", [T, D])
        stats = sb("stats", [T, B, 6])
        mean = sb("mean", [T, B])
        lvar = sb("lvar", [T, B])
        lt = sb("lt", [T, B])
        lr = sb("lr", [T, B])
        gact = sb("gact", [128, NF, 512])
        hT = sb("hT", [128, 2, NF, 512])
        wg_n = sb("wg_n", [E, D])
        wgT = sb("wgT", [D, E])
        mw1 = sb("mw1", [D, E, 2 * HE])
        mw2 = sb("mw2", [128, E * HE // 128, D])
        ws1 = sb("ws1", [D, 4 * HE])
        ws2 = sb("ws2", [2 * HE, D])
        sc = sb("sc", [T, B, E])
        scm = sb("scm", [T, B])
        scs = sb("scs", [T, B])
        sc2 = sb("sc2", [T, B, E])
        top = sb("top", [T, B, 8])
        tidx = sb("tidx", [T, B, 8], mybir.dt.uint32)
        tidf = sb("tidf", [T, B, 2])
        cw = sb("cw", [T, B, E])
        NCH = E // 4 + 1
        sg = sb("sg", [T, 2, NCH, 256])
        mh = sb("mh", [T, 2, NCH, 256])
        mhT = sb("mhT", [128, 2, 12, T])

        bank = {n: stack.enter_context(nc.psum_tensor("ps_" + n, [128, 512], F32))
                for n in ("qk", "v", "kt", "qt", "s", "pt", "ot", "y")}
        by_head = {n: b[:, :].rearrange("p (h t) -> p h t", t=128) for n, b in bank.items()}

        in_const, in_x, in_sim, in_par, in_moe = (sem("in_" + n) for n in ("const", "x", "sim", "par", "moe"))
        in_qkv, in_wo, in_ffn = sem("in_qkv"), sem("in_wo"), sem("in_ffn")
        out_done = sem("out_done")
        setup, par_clear = sem("setup"), sem("par_clear")
        pe_v, pe_qk, pe_T, pe_S, pe_neg, pe_PT, pe_PV, pe_Y = (
            steps(n, c) for n, c in (("pe_v", 0), ("pe_qk", 2), ("pe_T", 2), ("pe_S", 2), ("pe_neg", 2),
                                     ("pe_PT", 2), ("pe_PV", 2), ("pe_Y", 2)))
        act_qk, act_T, act_v, act_exp, act_PT, act_OT = (
            steps(n, 1) for n in ("act_qk", "act_T", "act_v", "act_exp", "act_PT", "act_OT"))
        dve_qk, dve_y, dve_n2 = steps("dve_qk", 1), steps("dve_y", 1), steps("dve_n2", 2)
        dve_max, dve_rs, dve_rn = steps("dve_max"), steps("dve_rs"), sem("dve_rn")
        pool_add, pool_norm, pool_pn = steps("pool_add", 2), steps("pool_norm", 2), steps("pool_pn")
        pool_cur = steps("pool_cur")
        x_ready, pe_xt, xT_ready, tab_ready = steps("x_ready"), steps("pe_xt"), steps("xT_ready"), steps("tab_ready")
        xn_ready = steps("xn_ready")
        ln = sem("ln")
        pe_sh, act_half, pool_b2 = steps("pe_sh"), steps("act_half"), steps("pool_b2")
        dve_sh, pe_nt, act_nt = steps("dve_sh"), steps("pe_nt"), steps("act_nt")
        pe_g, pe_a, act_g, dve_h, pe_f, dve_f = (steps(n, c) for n, c in (
            ("pe_g", 0), ("pe_a", 0), ("act_g", NF), ("dve_h", NF), ("pe_f", 0), ("dve_f", 0)))
        sim_pe, sim_act, sim_dve = sem("sim_pe"), sem("sim_act"), sem("sim_dve")
        moe_pe, moe_act, moe_dve, moe_self = sem("moe_pe"), sem("moe_act"), sem("moe_dve"), sem("moe_self")
        m_cur, m_h, m_silu, m_u, m_w, m_T, m_ev, m_y, m_out = (steps(n, c) for n, c in (
            ("m_cur", 0), ("m_h", 2), ("m_silu", 1), ("m_u", 2), ("m_w", 0), ("m_T", 6), ("m_ev", 2), ("m_y", 2),
            ("m_out", 1)))

        block = stack.enter_context(nc.Block())


        def pipeline(eng, base, run, first=LAG):
            for s in range(first):
                run(base, 0, s, lambda lag, s=s: s - lag >= 0)
            rounds = GPL // UNROLL - 1
            with eng.Fori(0, rounds) as it:
                for s in range(first, first + UNROLL):
                    run(base + it * UNROLL, it * (UNROLL // GPB), s, lambda lag: True)
            for s in range(first + rounds * UNROLL, GPL + LAG):
                run(base, 0, s, lambda lag, s=s: s - lag < GPL)

        def rsqrt_step(dve, k, r, v, t, sig, at):
            if k == 0:
                i = nc.vector.tensor_scalar(r.bitcast(I32), v.bitcast(I32), -0.5, RSQRT_SEED, ALU.mult, ALU.add)
            else:
                dve.wait_ge(sig, at + k)
                if k % 3 == 1:
                    i = nc.vector.tensor_tensor(t, r, r, ALU.mult)
                elif k % 3 == 2:
                    i = nc.vector.scalar_tensor_tensor(out=t, in0=t, scalar=-0.5, in1=v, op0=ALU.mult, op1=ALU.mult)
                else:
                    i = nc.vector.scalar_tensor_tensor(out=r, in0=t, scalar=1.5, in1=r, op0=ALU.add, op1=ALU.mult)
            i.then_inc(sig, 1)

        def layernorm(dve, dst, src, call, done):
            at = call * LN_OPS
            for b in range(B):
                i = nc.vector.bn_stats(stats[:, b, :], src[:, b, :])
            i.then_inc(ln, 1)
            dve.wait_ge(ln, at + 1)
            me, ve, mo, vo = (stats[:, :, k] for k in (1, 2, 4, 5))
            nc.vector.tensor_tensor(mean[:, :], me, mo, ALU.add)
            nc.vector.tensor_tensor(lt[:, :], me, mo, ALU.subtract)
            nc.vector.tensor_tensor(lvar[:, :], ve, vo, ALU.add).then_inc(ln, 1)
            dve.wait_ge(ln, at + 2)
            nc.vector.tensor_scalar(mean[:, :], mean[:, :], 0.5, None, ALU.mult)
            nc.vector.tensor_tensor(lt[:, :], lt[:, :], lt[:, :], ALU.mult).then_inc(ln, 1)
            dve.wait_ge(ln, at + 3)
            nc.vector.tensor_scalar(lt[:, :], lt[:, :], 0.25, 1e-5, ALU.mult, ALU.add).then_inc(ln, 1)
            dve.wait_ge(ln, at + 4)
            nc.vector.scalar_tensor_tensor(out=lvar[:, :], in0=lvar[:, :], scalar=1.0 / D, in1=lt[:, :],
                                           op0=ALU.mult, op1=ALU.add).then_inc(ln, 1)
            dve.wait_ge(ln, at + 5)
            for k in range(RS_OPS):
                rsqrt_step(dve, k, lr[:, :], lvar[:, :], lt[:, :], ln, at + 5)
            dve.wait_ge(ln, at + LN_OPS)
            for b in range(B):
                i = nc.vector.tensor_scalar(dst[:, b, :], src[:, b, :], mean[:, b:b + 1], lr[:, b:b + 1],
                                            ALU.subtract, ALU.mult)
            i.then_inc(done.sem, 1)

        @block.sync
        def _(sp):
            sp.dma_start(cst[:, :], consts).then_inc(in_const, 16)
            sp.dma_start(xbase[:, :, :], x.rearrange("b t d -> t b d")).then_inc(in_x, 16)
            sp.dma_start(ctx_sb[:, :, :], ctx.rearrange("b t d -> t b d")).then_inc(in_sim, 16)
            sp.dma_start(wv_n[:, :], s_Wv).then_inc(in_sim, 16)
            sp.dma_start(wt_n[:, :], s_Wt).then_inc(in_sim, 16)
            sp.dma_start(bvt[:, 0:1], s_bv.rearrange("(h o) -> h o", o=1)).then_inc(in_sim, 16)
            sp.dma_start(bvt[:, 1:2], s_bt.rearrange("(h o) -> h o", o=1)).then_inc(in_sim, 16)
            sp.dma_start(gates[:, 0:2], g_xattn.rearrange("(o n) -> o n", o=1).to_broadcast([T, 2])).then_inc(in_sim, 16)
            sp.dma_start(gates[:, 2:4], g_ffn.rearrange("(o n) -> o n", o=1).to_broadcast([T, 2])).then_inc(in_sim, 16)
            for m in range(3):
                sp.dma_start(wqkv[:, m * INNER:(m + 1) * INNER], Wqkv[0, :, m * INNER:(m + 1) * INNER]).then_inc(in_qkv, 16)
            for m, s in enumerate((q_scale, k_scale)):
                sp.dma_start(scales[:, :, m, :], s.rearrange("(o l) d -> o l d", o=1).to_broadcast([T, DEPTH, DH])).then_inc(in_par, 16)
            sp.dma_start(wo[:, :, :], Wo[0].rearrange("(c p) d -> p c d", p=128)).then_inc(in_wo, 16)

            def load_ffn(l):
                sp.dma_start(w1[:, :], W1[l]).then_inc(in_ffn, 16)
                sp.dma_start(w2[:, 0:NF - 1, :], W2[l, 0:128 * (NF - 1), :].rearrange("(c p) d -> p c d", p=128)).then_inc(in_ffn, 16)
                sp.dma_start(w2[0:FCH[-1][1], NF - 1, :], W2[l, FCH[-1][0]:DFF, :]).then_inc(in_ffn, 16)

            load_ffn(0)
            sp.wait_ge(par_clear, 1)
            for m, s in enumerate((ln_g, ln_b)):
                sp.dma_start(par_rows[m * DEPTH:(m + 1) * DEPTH, :], s).then_inc(in_par, 16)
            for m in range(2):
                for c, (f0, fn) in enumerate(FCH):
                    k = 2 + m * NF + c
                    sp.dma_start(par_rows[k * DEPTH:(k + 1) * DEPTH, 0:fn],
                                 b1[:, m * DFF + f0:m * DFF + f0 + fn]).then_inc(in_par, 16)
            sp.dma_start(b2_all[:, :, :], b2.rearrange("(o l) d -> o l d", o=1).to_broadcast([T, DEPTH, D])).then_inc(in_par, 16)
            sp.dma_start(bo_b[:, :], x_bo.rearrange("(o d) -> o d", o=1).to_broadcast([T, D])).then_inc(in_par, 16)
            sp.dma_start(wg_n[:, :], m_Wg).then_inc(in_moe, 16)
            sp.dma_start(mw1[:, :, :], m_W1.rearrange("e d h -> d e h")).then_inc(in_moe, 16)
            sp.dma_start(mw2[:, :, :], m_W2.rearrange("(c e) h d -> (e h) c d", e=2)).then_inc(in_moe, 16)
            sp.dma_start(ws1[:, :], m_Ws1).then_inc(in_moe, 16)
            sp.dma_start(ws2[:, :], m_Ws2).then_inc(in_moe, 16)
            with sp.Fori(0, DEPTH - 1) as l:
                pe_qk.done(sp, l * GPL + GPL - 1)
                for m in range(3):
                    sp.dma_start(wqkv[:, m * INNER:(m + 1) * INNER], Wqkv[l + 1, :, m * INNER:(m + 1) * INNER]).then_inc(in_qkv, 16)
                pe_Y.done(sp, l * B + B - 1)
                sp.dma_start(wo[:, :, :], Wo[l + 1].rearrange("(c p) d -> p c d", p=128)).then_inc(in_wo, 16)
                pe_f.done(sp, l * 2 + 1)
                load_ffn(l + 1)
            pe_qk.done(sp, DEPTH * GPL - 1)
            sp.dma_start(wqkv[:, 0:INNER], x_Wq).then_inc(in_qkv, 16)
            sp.dma_start(wqkv[0:DC, INNER:2 * INNER], x_Wk).then_inc(in_qkv, 16)
            sp.dma_start(wqkv[0:DC, 2 * INNER:3 * INNER], x_Wv).then_inc(in_qkv, 16)
            pe_Y.done(sp, DEPTH * B - 1)
            sp.dma_start(wo[:, :, :], x_Wo.rearrange("(c p) d -> p c d", p=128)).then_inc(in_wo, 16)
            m_out.done(sp, B - 1)
            sp.dma_start(out.rearrange("b t d -> t b d"), xbase[:, :, :]).then_inc(out_done, 16)
            sp.wait_ge(out_done, 16)

        PAR = 16 * (4 + 2 * NF + 2)

        @block.tensor
        def _(pe):
            for s in (pe_v, pe_qk, pe_T, pe_S, pe_neg, pe_PT, pe_PV, pe_Y, m_h, m_T, m_y):
                if s.credit:
                    pe.sem_inc(s.sem, s.credit)

            def tiles_T(src, done):
                for h, bk in enumerate(("kt", "qt")):
                    for j in range(4):
                        i = nc.tensor.transpose(by_head[bk][:, j, :], src[:, 4 * h + j, :], ident)
                    i.then_inc(done.sem, 1)

            pe.wait_ge(in_const, 16)
            pe.wait_ge(in_sim, 16 * 7)
            nc.tensor.transpose(bank["v"][:, 0:HSIM], wv_n[:, :], ident[0:HSIM, 0:HSIM])
            nc.tensor.transpose(bank["v"][0:DC, HSIM:2 * HSIM], wt_n[:, :], ident[0:HSIM, 0:HSIM])
            pe.wait_ge(in_par, PAR)
            nc.tensor.transpose(bank["v"][:, 128:128 + NP * DEPTH], par_rows[:, :], ident[0:NP * DEPTH, 0:NP * DEPTH])
            for h, bk in enumerate(("s", "pt")):
                for j in range(4):
                    i = nc.tensor.transpose(by_head[bk][0:DC, j, :], ctx_sb[:, 4 * h + j, :], ident)
            i.then_inc(sim_pe, 1)
            x_ready.done(pe, 0)
            tiles_T(xn, pe_xt)
            pe.wait_ge(sim_act, 2)
            xT_ready.done(pe, 0)
            for h, bk in enumerate(("qk", "v")):
                nc.tensor.matmul(bank[bk][0:HSIM, :], wvT[:, :], xfT[:, 4 * h:4 * h + 4, :], start=True, stop=True)
            for h, bk in enumerate(("s", "pt")):
                i = nc.tensor.matmul(bank[bk][0:HSIM, :], wtT[:, :], cT[:, 4 * h:4 * h + 4, :], start=True, stop=True)
            i.then_inc(sim_pe, 1)
            pe.wait_ge(sim_act, 6)
            pe.wait_ge(setup, 1)
            for h, bk in enumerate(("kt", "qt")):
                i = nc.tensor.matmul(bank[bk][:, :], ones[0:HSIM, :], tsq[:, 512 * h:512 * h + 512], start=True, stop=True)
            for b in range(B):
                i = nc.tensor.matmul(bank["y"][:, b:b + 1], vsq[:, b * T:b * T + T], ones[0:HSIM, 0:1], start=True, stop=True)
            i.then_inc(sim_pe, 1)
            for b in range(B):
                i = nc.tensor.matmul(by_head["ot" if b < 4 else "qk"][:, b % 4, :], vT[:, b * T:b * T + T],
                                     tT[:, b * T:b * T + T], start=True, stop=True)
            i.then_inc(sim_pe, 1)

            def attention(base, kind, seq0):
                window = kind == "local"

                def run(g0, b0, s, on):
                    gi, bs = s % GPB, s // GPB
                    lhs = xcur[:, bs % 2, :] if window else ccur[:, bs % 2, :]
                    rows = D if window else DC
                    if on(3):
                        g, r = g0 + s - 3, (s - 3) % 2
                        if window:
                            pool_norm.done(pe, g)
                        else:
                            act_qk.done(pe, g)
                            dve_qk.done(pe, g)
                        act_T.free(pe, g, 1)
                        for h in range(HG):
                            o = (0, 1, 3, 4)[h] * DH
                            nc.tensor.transpose(by_head["kt"][:, h, :], k_z[:, r, o:o + 128], ident)
                        for p in range(2):
                            i = nc.tensor.transpose(by_head["qt"][:, p, :], q_n[:, r, p * 128:p * 128 + 128], ident)
                        i.then_inc(pe_T.sem, 1)
                    if on(0):
                        g = g0 + s
                        if gi == 0:
                            pool_cur.done(pe, seq0 + b0 + bs)
                        act_v.free(pe, g, 1)
                        nc.tensor.matmul(bank["v"][:, 0:GW], lhs, wqkv[0:rows, 2 * INNER + gi * GW:2 * INNER + (gi + 1) * GW],
                                         start=True, stop=True).then_inc(pe_v.sem, 1)
                    if on(6) and (s - 6) % GPB == GPB - 1:
                        ys = (s - 6) // GPB
                        act_OT.done(pe, g0 + s - 6)
                        dve_y.free(pe, seq0 + b0 + ys, 1)
                        for c in range(INNER // 128):
                            i = nc.tensor.matmul(bank["y"][:, 0:D], oT[:, ys % 2, c, :], wo[:, c, :],
                                                 start=(c == 0), stop=(c == INNER // 128 - 1))
                        i.then_inc(pe_Y.sem, 1)
                    if on(5):
                        g, r = g0 + s - 5, (s - 5) % 2
                        act_PT.done(pe, g)
                        act_OT.free(pe, g, 1)
                        vs = v_n[:, (s - 5) % UNROLL, :]
                        for h in range(HG):
                            i = nc.tensor.matmul(by_head["ot"][64 * (h % 2):64 * (h % 2) + 64, h // 2, :],
                                                 vs[:, h * DH:(h + 1) * DH], pT[:, r, h, :], start=True, stop=True)
                        i.then_inc(pe_PV.sem, 1)
                    if on(3):
                        g, r = g0 + s - 3, (s - 3) % 2
                        act_T.done(pe, g)
                        act_exp.free(pe, g, 1)
                        nc.tensor.matmul(by_head["s"], ident_b[:, :],
                                         masks[:, 0 if window else 1, :].unsqueeze(1).to_broadcast([T, HG, T]),
                                         start=True, stop=False, skip_group_check=True)
                        for h in range(HG):
                            i = nc.tensor.matmul(by_head["s"][:, h, :], qT[:, r, h // 2, :], kT[:, r, h, :],
                                                 start=False, stop=False, skip_group_check=True)
                        i.then_inc(pe_S.sem, 1)
                    if on(0):
                        g = g0 + s
                        act_qk.free(pe, g, 1)
                        dve_qk.free(pe, g, 1)
                        nc.tensor.matmul(bank["qk"][:, 0:GW], xcur[:, bs % 2, :], wqkv[:, gi * GW:(gi + 1) * GW], start=True, stop=True)
                        nc.tensor.matmul(bank["qk"][:, GW:2 * GW], lhs, wqkv[0:rows, INNER + gi * GW:INNER + (gi + 1) * GW],
                                         start=True, stop=True).then_inc(pe_qk.sem, 1)
                    if on(4):
                        g, r = g0 + s - 4, (s - 4) % 2
                        pool_pn.done(pe, g)
                        act_PT.free(pe, g, 1)
                        for h in range(HG):
                            i = nc.tensor.transpose(by_head["pt"][:, h, :], probs[:, r, h, :], ident)
                        i.then_inc(pe_PT.sem, 1)
                    if on(3):
                        g, r = g0 + s - 3, (s - 3) % 2
                        dve_max.done(pe, g)
                        nc.tensor.matmul(by_head["s"], ident_b[:, :], negm[:, r, :].unsqueeze(2).to_broadcast([T, HG, T]),
                                         start=False, stop=True, skip_group_check=True).then_inc(pe_neg.sem, 1)

                pipeline(pe, base, run)

            with pe.Fori(0, DEPTH) as l:
                x_ready.done(pe, l + 1)
                tiles_T(xres, pe_xt)
                pe.wait_ge(in_qkv, l * 48 + 48)
                pe.wait_ge(in_wo, l * 16 + 16)
                attention(l * GPL, "local", l * B)
                dve_y.done(pe, l * B + B - 1)
                nc.tensor.matmul(bank["qk"][:, :], shift, xres[:, :, D // 2:D], start=True, stop=True).then_inc(pe_sh.sem, 1)
                xn_ready.done(pe, l)
                tiles_T(xn, pe_nt)
                pe.wait_ge(in_ffn, l * 48 + 48)
                gate_banks, a_banks = ("v", "s", "pt"), ("ot", "y", "qk")
                for h in range(2):
                    act_nt.done(pe, l * 2 + h)
                    for c, (f0, fn) in enumerate(FCH):
                        n = l * 2 * NF + h * NF + c
                        act_g.free(pe, n, NF)
                        nc.tensor.matmul(bank[gate_banks[c]][0:fn, :], w1[:, DFF + f0:DFF + f0 + fn],
                                         xfT[:, 4 * h:4 * h + 4, :], start=True, stop=True).then_inc(pe_g.sem, 1)
                        dve_h.free(pe, n, NF)
                        nc.tensor.matmul(bank[a_banks[c]][0:fn, :], w1[:, f0:f0 + fn],
                                         xfT[:, 4 * h:4 * h + 4, :], start=True, stop=True).then_inc(pe_a.sem, 1)
                for h, bk in enumerate(("kt", "qt")):
                    dve_h.done(pe, l * 2 * NF + h * NF + NF - 1)
                    for j in range(4):
                        for c, (f0, fn) in enumerate(FCH):
                            i = nc.tensor.matmul(by_head[bk][:, j, :], hT[0:fn, h, c, j * T:j * T + T], w2[0:fn, c, :],
                                                 start=(c == 0), stop=(c == NF - 1))
                    i.then_inc(pe_f.sem, 1)

            x_ready.done(pe, DEPTH + 2)
            tiles_T(xn, pe_xt)
            pe.wait_ge(in_qkv, DEPTH * 48 + 48)
            pe.wait_ge(in_wo, DEPTH * 16 + 16)
            attention(DEPTH * GPL, "cross", DEPTH * B)

            pe.wait_ge(in_moe, 16 * 5)
            nc.tensor.transpose(bank["v"][:, 0:E], wg_n[:, :], ident[0:E, 0:E]).then_inc(moe_pe, 1)
            x_ready.done(pe, DEPTH + 3)
            tiles_T(xn, pe_xt)
            pe.wait_ge(moe_act, 1)
            xT_ready.done(pe, DEPTH + 2)
            for b in range(B):
                i = nc.tensor.matmul(bank["s"][:, b * E:(b + 1) * E], xfT[:, b, :], wgT[:, :], start=True, stop=True)
            i.then_inc(moe_pe, 1)
            pe.wait_ge(moe_dve, 1)
            h_banks = ("qk", "v", "s", "pt", "ot")

            def hidden(t, r):
                m_cur.done(pe, t)
                m_silu.free(pe, t, 1)
                m_u.free(pe, t, 1)
                for c in range(E // 4):
                    nc.tensor.matmul(bank[h_banks[c]][:, :], xcur[:, r, :], mw1[:, 4 * c:4 * c + 4, :], start=True, stop=True)
                nc.tensor.matmul(bank[h_banks[-1]][:, 0:4 * HE], xcur[:, r, :], ws1[:, :], start=True, stop=True).then_inc(m_h.sem, 1)

            def project(t, r):
                m_w.done(pe, t)
                for c in range(3):
                    n = t * 3 + c
                    bk = ("kt", "qt")[c % 2] if r == 0 else ("qt", "kt")[c % 2]
                    m_ev.free(pe, n, 2)
                    for j in range(4 if c < 2 else 1):
                        k = 4 * c + j
                        i = nc.tensor.transpose(by_head[bk][:, j, :], mh[:, r, k // 2, 128 * (k % 2):128 * (k % 2) + 128], ident)
                    i.then_inc(m_T.sem, 1)
                m_out.free(pe, t, 1)
                for c in range(3):
                    m_ev.done(pe, t * 3 + c)
                    for k in range(4 * c, min(4 * c + 4, 9)):
                        i = nc.tensor.matmul(bank["y"][:, 0:D], mhT[:, r, k, :], mw2[:, k, :] if k < 8 else ws2[:, :],
                                             start=(k == 0), stop=(k == 8))
                i.then_inc(m_y.sem, 1)

            hidden(0, 0)
            with pe.Fori(0, B // 2 - 1) as p:
                hidden(p * 2 + 1, 1)
                project(p * 2, 0)
                hidden(p * 2 + 2, 0)
                project(p * 2 + 1, 1)
            hidden(B - 1, 1)
            project(B - 2, 0)
            project(B - 1, 1)

        @block.scalar
        def _(act):
            for s in (act_qk, act_T, act_v, act_exp, act_PT, act_OT, act_g, m_silu, m_ev):
                act.sem_inc(s.sem, s.credit)

            def copy(dst, src, **kw):
                return nc.scalar.activation(dst, src, ACT.Copy, **kw)

            def tiles_out(first, shifted, done):
                for h, bk in enumerate(("kt", "qt")):
                    pe_xt.done(act, first + h)
                    dst = (xT if shifted else xfT)[:, 4 * h:4 * h + 4, :]
                    if shifted:
                        copy(dst[0:D // 2], by_head[bk][0:D // 2])
                        i = copy(dst[D // 2:D, :, 1:T], by_head[bk][D // 2:D, :, 0:T - 1])
                    else:
                        i = copy(dst, by_head[bk])
                i.then_inc(done.sem, 1)

            act.wait_ge(in_sim, 16 * 7)
            nc.scalar.activation(tg[:, :], gates[:, :], ACT.Tanh).then_inc(sim_act, 1)
            act.wait_ge(sim_pe, 1)
            copy(wvT[:, :], bank["v"][:, 0:HSIM])
            copy(wtT[:, :], bank["v"][0:DC, HSIM:2 * HSIM])
            copy(lpar_all[:, :, :], bank["v"][:, 128:128 + NP * DEPTH].rearrange("p (k l) -> p k l", k=NP))
            copy(cT[:, 0:4, :], by_head["s"][0:DC])
            copy(cT[:, 4:8, :], by_head["pt"][0:DC]).then_inc(sim_act, 1)
            tiles_out(0, False, xT_ready)
            act.wait_ge(sim_pe, 2)
            for h, (vb, tb) in enumerate((("qk", "s"), ("v", "pt"))):
                nc.scalar.activation(vT[:, 512 * h:512 * h + 512], bank[vb][0:HSIM, :], ACT.Identity, bias=bvt[:, 0:1])
                nc.scalar.activation(tT[:, 512 * h:512 * h + 512], bank[tb][0:HSIM, :], ACT.Identity, bias=bvt[:, 1:2])
                nc.scalar.activation(vsq[:, 512 * h:512 * h + 512], bank[vb][0:HSIM, :], ACT.Square, bias=bvt[:, 0:1]).then_inc(sim_act, 1)
                nc.scalar.activation(tsq[:, 512 * h:512 * h + 512], bank[tb][0:HSIM, :], ACT.Square, bias=bvt[:, 1:2]).then_inc(sim_act, 1)
            act.wait_ge(sim_dve, 2)
            nc.scalar.activation(den[:, :, :], den[:, :, :], ACT.Sqrt).then_inc(sim_act, 1)

            def attention(base, kind, seq0):
                window = kind == "local"

                def run(g0, b0, s, on):
                    if on(3):
                        g, r = g0 + s - 3, (s - 3) % 2
                        pe_T.done(act, g)
                        pe_S.free(act, g, 2)
                        copy(kT[:, r], by_head["kt"])
                        copy(qT[:, r], by_head["qt"][:, 0:2, :]).then_inc(act_T.sem, 1)
                    if on(0):
                        g = g0 + s
                        pe_v.done(act, g)
                        copy(v_n[:, s % UNROLL, :], bank["v"][:, 0:GW]).then_inc(act_v.sem, 1)
                    if on(5):
                        g, gi, bs = g0 + s - 5, (s - 5) % GPB, (s - 5) // GPB
                        pe_PV.done(act, g)
                        if gi == 0:
                            pe_Y.free(act, seq0 + b0 + bs, 2)
                        copy(oT[:, bs % 2, 2 * gi:2 * gi + 2, :], by_head["ot"][:, 0:2, :]).then_inc(act_OT.sem, 1)
                    if on(0):
                        g, r = g0 + s, s % 2
                        pe_qk.done(act, g)
                        if window:
                            dve_n2.free(act, g, 2)
                            nc.scalar.activation(sq[:, r, :], bank["qk"][:, :], ACT.Square).then_inc(act_qk.sem, 1)
                        else:
                            pe_T.free(act, g, 2)
                            copy(q_n[:, r, :], bank["qk"][:, 0:GW], scale=DH ** -0.5).then_inc(act_qk.sem, 1)
                    if on(4):
                        g, r = g0 + s - 4, (s - 4) % 2
                        pe_PT.done(act, g)
                        pe_PV.free(act, g, 2)
                        copy(pT[:, r], by_head["pt"]).then_inc(act_PT.sem, 1)
                    if on(3):
                        g, r = g0 + s - 3, (s - 3) % 2
                        pe_neg.done(act, g)
                        pe_PT.free(act, g, 2)
                        for h in range(HG):
                            i = nc.scalar.activation(probs[:, r, h, :], by_head["s"][:, h, :], ACT.Exp,
                                                     accum_out=sums[:, r, h:h + 1])
                        i.then_inc(act_exp.sem, 1)

                pipeline(act, base, run)

            with act.Fori(0, DEPTH) as l:
                tiles_out(l * 2 + 2, True, xT_ready)
                attention(l * GPL, "local", l * B)
                dve_y.done(act, l * B + B - 1)
                copy(xsh[:, :, 0:D // 2], xres[:, :, 0:D // 2]).then_inc(act_half.sem, 1)
                for h, bk in enumerate(("kt", "qt")):
                    pe_nt.done(act, l * 2 + h)
                    tab_ready.done(act, l)
                    nc.scalar.activation(xfT[:, 4 * h:4 * h + 4, :], by_head[bk], ACT.Identity,
                                         scale=lpar[:, 0:1], bias=lpar[:, 1:2]).then_inc(act_nt.sem, 1)
                for h in range(2):
                    for c, (f0, fn) in enumerate(FCH):
                        n = l * 2 * NF + h * NF + c
                        pe_g.done(act, n)
                        dve_h.free(act, n, NF)
                        nc.scalar.activation(gact[0:fn, c, :], bank[("v", "s", "pt")[c]][0:fn, :], ACT.Gelu,
                                             bias=lpar[0:fn, 2 + NF + c:3 + NF + c]).then_inc(act_g.sem, 1)

            tiles_out(DEPTH * 2 + 2, False, xT_ready)
            attention(DEPTH * GPL, "cross", DEPTH * B)

            act.wait_ge(moe_pe, 1)
            copy(wgT[:, :], bank["v"][:, 0:E]).then_inc(moe_act, 1)
            tiles_out(DEPTH * 2 + 4, False, xT_ready)
            act.wait_ge(moe_dve, 2)
            nc.scalar.activation(sc[:, :, :], sc[:, :, :], ACT.Exp).then_inc(moe_act, 1)

            def silu(t, r):
                m_h.done(act, t)
                m_u.free(act, t, 2)
                for c in range(E // 4):
                    bk = ("qk", "v", "s", "pt")[c]
                    nc.scalar.activation(sg[:, r, c, :].rearrange("p (e h) -> p e h", h=HE),
                                         bank[bk][:, :].rearrange("p (e u h) -> p e u h", u=2, h=HE)[:, :, 1, :], ACT.Silu)
                nc.scalar.activation(sg[:, r, NCH - 1, 0:2 * HE], bank["ot"][:, 2 * HE:4 * HE], ACT.Silu).then_inc(m_silu.sem, 1)

            def evict(t, r):
                for c in range(3):
                    n = t * 3 + c
                    bk = ("kt", "qt")[c % 2] if r == 0 else ("qt", "kt")[c % 2]
                    k = 4 if c < 2 else 1
                    m_T.done(act, n)
                    if c == 0:
                        m_y.free(act, t, 2)
                    copy(mhT[:, r, 4 * c:4 * c + k, :], by_head[bk][:, 0:k, :]).then_inc(m_ev.sem, 1)

            silu(0, 0)
            with act.Fori(0, B // 2 - 1) as p:
                silu(p * 2 + 1, 1)
                evict(p * 2, 0)
                silu(p * 2 + 2, 0)
                evict(p * 2 + 1, 1)
            silu(B - 1, 1)
            evict(B - 2, 0)
            evict(B - 1, 1)

        @block.vector
        def _(dve):
            for s in (dve_qk, dve_y, dve_n2, dve_h, m_u, m_out):
                dve.sem_inc(s.sem, s.credit)
            nc.vector.memset(par_rows[:, :], 0.0).then_inc(par_clear, 1)
            nc.vector.memset(ones[:, :], 1.0).then_inc(setup, 1)
            nc.vector.memset(masks[:, 1, :], 0.0)
            nc.vector.memset(xT[D // 2:D, :, 0:1], 0.0)
            dve.wait_ge(in_const, 16)
            nc.vector.tensor_copy(ident_b[:, :], ident)
            nc.vector.tensor_copy(masks[:, 0, :], cst[:, C_MASK:C_MASK + T])
            dve.wait_ge(in_x, 16)
            dve.wait_ge(in_par, PAR)
            layernorm(dve, xn, xbase, 0, x_ready)
            dve.wait_ge(sim_pe, 3)
            nc.vector.tensor_copy(vn2[:, :], bank["y"][:, 0:B]).then_inc(sim_dve, 1)
            dve.wait_ge(sim_dve, 1)
            for b in range(B):
                i = nc.vector.tensor_scalar(den[:, b, :], by_head["kt" if b < 4 else "qt"][:, b % 4, :], vn2[:, b:b + 1], 1e-16,
                                            ALU.mult, ALU.max)
            i.then_inc(sim_dve, 1)
            dve.wait_ge(sim_act, 7)
            nc.vector.reciprocal(den[:, :, :], den[:, :, :]).then_inc(sim_dve, 1)
            dve.wait_ge(sim_dve, 3)
            dve.wait_ge(sim_pe, 4)
            for h, bk in enumerate(("ot", "qk")):
                i = nc.vector.tensor_tensor(den[:, 4 * h:4 * h + 4, :], by_head[bk], den[:, 4 * h:4 * h + 4, :], ALU.mult)
            i.then_inc(sim_dve, 1)
            dve.wait_ge(sim_dve, 4)
            nc.vector.scalar_tensor_tensor(out=xbase[:, :, :], in0=den[:, :, :], scalar=tg[:, 0:1], in1=xbase[:, :, :],
                                           op0=ALU.mult, op1=ALU.add).then_inc(sim_dve, 1)
            dve.wait_ge(sim_dve, 5)
            layernorm(dve, xres, xbase, 1, x_ready)

            def attention(base, kind, seq0):
                window = kind == "local"

                def run(g0, b0, s, on):
                    def norms(*ks):
                        if not (window and on(1)):
                            return
                        g, r = g0 + s - 1, (s - 1) % 2
                        at = g * (RS_OPS + 1)
                        for k in ks:
                            if k < 0:
                                dve_n2.done(dve, g)
                                pool_norm.free(dve, g, 2)
                                nc.vector.tensor_scalar(n2[:, r, :], n2[:, r, :], 1e-24, None, ALU.max).then_inc(dve_rn, 1)
                            else:
                                if k == 0:
                                    dve.wait_ge(dve_rn, at + 1)
                                rsqrt_step(dve, k, rn[:, r, :], n2[:, r, :], nt[:, :], dve_rn, at + 1)

                    norms(-1, 0)
                    if on(3):
                        g, r = g0 + s - 3, (s - 3) % 2
                        pe_S.done(dve, g)
                        pe_neg.free(dve, g, 2)
                        nc.vector.tensor_reduce(negm[:, r, :], by_head["s"], AX.X, ALU.max, negate=True).then_inc(dve_max.sem, 1)
                    norms(1, 2)
                    if on(6) and (s - 6) % GPB == GPB - 1:
                        bs = (s - 6) // GPB
                        pe_Y.done(dve, seq0 + b0 + bs)
                        if window:
                            xb = xres[:, b0 + bs, :]
                            nc.vector.tensor_tensor(xb, bank["y"][:, 0:D], xb, ALU.add).then_inc(dve_y.sem, 1)
                        else:
                            xb = xbase[:, b0 + bs, :]
                            nc.vector.scalar_tensor_tensor(out=xb, in0=bank["y"][:, 0:D], scalar=tg[:, 1:2], in1=xb,
                                                           op0=ALU.mult, op1=ALU.add).then_inc(dve_y.sem, 1)
                    if on(0):
                        g, r = g0 + s, s % 2
                        norms(3)
                        pe_qk.done(dve, g)
                        act_qk.done(dve, g)
                        if window:
                            pool_add.free(dve, g, 2)
                            qk = bank["qk"][:, :].rearrange("p (m h d) -> p m h d", m=2, d=DH)
                            ra = rot_a[:, r, :].rearrange("p (m h d) -> p m h d", m=2, d=DH)
                            rb = rot_b[:, r, :].rearrange("p (m h d) -> p m h d", m=2, d=DH)
                            H = DH // 2

                            def table(t, a, b):
                                return t[:, :, a:b].unsqueeze(2).to_broadcast([T, 2, HG, b - a])

                            nc.vector.tensor_tensor(ra, qk, table(tab_cos, 0, DH), ALU.mult)
                            norms(4)
                            nc.vector.tensor_tensor(rb[:, :, :, 0:H], qk[:, :, :, H:DH], table(tab_sin, 0, H), ALU.mult)
                            norms(5)
                            nc.vector.tensor_tensor(rb[:, :, :, H:DH], qk[:, :, :, 0:H], table(tab_sin, H, DH),
                                                    ALU.mult).then_inc(dve_qk.sem, 1)
                            norms(6)
                            nc.vector.tensor_reduce(n2[:, r, :], sq[:, r, :].rearrange("p (h d) -> p h d", d=DH), AX.X,
                                                    ALU.add).then_inc(dve_n2.sem, 1)
                        else:
                            pe_T.free(dve, g, 2)
                            kd = k_z[:, r, :].rearrange("p (a z) -> p a z", a=2)
                            kd = [kd[:, :, 0:DH], kd[:, :, 2 * DH:3 * DH]]
                            ks = bank["qk"][:, GW:2 * GW].rearrange("p (a o d) -> p a o d", a=2, d=DH)
                            nc.vector.tensor_copy(kd[0], ks[:, :, 0, :])
                            nc.vector.tensor_copy(kd[1], ks[:, :, 1, :]).then_inc(dve_qk.sem, 1)
                    else:
                        norms(3, 4, 5, 6)
                    norms(7)
                    if on(3):
                        g, r = g0 + s - 3, (s - 3) % 2
                        act_exp.done(dve, g)
                        nc.vector.reciprocal(rsum[:, r, :], sums[:, r, :]).then_inc(dve_rs.sem, 1)
                    norms(8, 9)

                pipeline(dve, base, run)

            with dve.Fori(0, DEPTH) as l:
                tab_ready.done(dve, l)
                attention(l * GPL, "local", l * B)
                pe_sh.done(dve, l)
                nc.vector.tensor_copy(xsh[:, :, D // 2:D], bank["qk"][:, :].rearrange("p (b d) -> p b d", b=B)).then_inc(dve_sh.sem, 1)
                dve_sh.done(dve, l)
                act_half.done(dve, l)
                layernorm(dve, xn, xsh, l + 2, xn_ready)
                for h in range(2):
                    for c, (f0, fn) in enumerate(FCH):
                        n = l * 2 * NF + h * NF + c
                        act_g.done(dve, n)
                        pe_a.done(dve, n)
                        nc.vector.scalar_tensor_tensor(out=hT[0:fn, h, c, :], in0=bank[("ot", "y", "qk")[c]][0:fn, :],
                                                       scalar=lpar[0:fn, 2 + c:3 + c], in1=gact[0:fn, c, :],
                                                       op0=ALU.add, op1=ALU.mult).then_inc(dve_h.sem, 1)
                pool_b2.done(dve, l)
                for h, bk in enumerate(("kt", "qt")):
                    pe_f.done(dve, l * 2 + h)
                    xb = xres[:, 4 * h:4 * h + 4, :]
                    i = nc.vector.tensor_tensor(xb, by_head[bk], xb, ALU.add)
                i.then_inc(x_ready.sem, 1)

            x_ready.done(dve, DEPTH + 1)
            nc.vector.scalar_tensor_tensor(out=xbase[:, :, :], in0=xres[:, :, :], scalar=tg[:, 2:3], in1=xbase[:, :, :],
                                           op0=ALU.mult, op1=ALU.add).then_inc(sim_dve, 1)
            dve.wait_ge(sim_dve, 6)
            layernorm(dve, xn, xbase, DEPTH + 2, x_ready)
            for b in range(B):
                i = nc.vector.scalar_tensor_tensor(out=xbase[:, b, :], in0=bo_b[:, :], scalar=tg[:, 1:2], in1=xbase[:, b, :],
                                                   op0=ALU.mult, op1=ALU.add)
            i.then_inc(sim_dve, 1)
            dve.wait_ge(sim_dve, 7)
            attention(DEPTH * GPL, "cross", DEPTH * B)
            dve_y.done(dve, (DEPTH + 1) * B - 1)
            layernorm(dve, xn, xbase, DEPTH + 3, x_ready)

            dve.wait_ge(moe_pe, 2)
            nc.vector.tensor_copy(sc[:, :, :], bank["s"][:, 0:B * E].rearrange("p (b e) -> p b e", e=E)).then_inc(moe_dve, 1)
            n = 1
            dve.wait_ge(moe_dve, n)
            nc.vector.tensor_reduce(scm[:, :], sc[:, :, :], AX.X, ALU.max).then_inc(moe_self, 1)
            dve.wait_ge(moe_self, 1)
            nc.vector.tensor_tensor(sc[:, :, :], sc[:, :, :], scm[:, :].unsqueeze(2).to_broadcast([T, B, E]),
                                    ALU.subtract).then_inc(moe_dve, 1)
            dve.wait_ge(moe_act, 2)
            nc.vector.tensor_reduce(scs[:, :], sc[:, :, :], AX.X, ALU.add).then_inc(moe_self, 1)
            dve.wait_ge(moe_self, 2)
            nc.vector.reciprocal(scm[:, :], scs[:, :]).then_inc(moe_self, 1)
            dve.wait_ge(moe_self, 3)
            nc.vector.tensor_tensor(sc[:, :, :], sc[:, :, :], scm[:, :].unsqueeze(2).to_broadcast([T, B, E]),
                                    ALU.mult).then_inc(moe_self, 1)
            dve.wait_ge(moe_self, 4)
            for b in range(B):
                i = nc.vector.max(top[:, b, :], sc[:, b, :])
            i.then_inc(moe_self, 1)
            dve.wait_ge(moe_self, 5)
            for b in range(B):
                i = nc.vector.max_index(tidx[:, b, :], top[:, b, :], sc[:, b, :])
            i.then_inc(moe_self, 1)
            dve.wait_ge(moe_self, 6)
            nc.vector.tensor_copy(tidf[:, :, :], tidx[:, :, 0:2]).then_inc(moe_self, 1)
            dve.wait_ge(moe_self, 7)
            experts = cst[:, C_IOTA:C_IOTA + E].unsqueeze(1).to_broadcast([T, B, E])
            for k, hot in enumerate((cw, sc2)):
                i = nc.vector.tensor_tensor(hot[:, :, :], experts, tidf[:, :, k:k + 1].to_broadcast([T, B, E]), ALU.is_equal)
            i.then_inc(moe_self, 1)
            dve.wait_ge(moe_self, 8)
            nc.vector.tensor_tensor(cw[:, :, :], cw[:, :, :], sc2[:, :, :], ALU.add).then_inc(moe_self, 1)
            dve.wait_ge(moe_self, 9)
            nc.vector.tensor_tensor(cw[:, :, :], cw[:, :, :], sc[:, :, :], ALU.mult).then_inc(moe_dve, 1)

            def gated(t, r):
                m_silu.done(dve, t)
                m_T.free(dve, t * 3 + 2, 6)
                for c in range(E // 4):
                    bk = ("qk", "v", "s", "pt")[c]
                    nc.vector.tensor_tensor(mh[:, r, c, :].rearrange("p (e h) -> p e h", h=HE),
                                            bank[bk][:, :].rearrange("p (e u h) -> p e u h", u=2, h=HE)[:, :, 0, :],
                                            sg[:, r, c, :].rearrange("p (e h) -> p e h", h=HE), ALU.mult)
                nc.vector.tensor_tensor(mh[:, r, NCH - 1, 0:2 * HE], bank["ot"][:, 0:2 * HE], sg[:, r, NCH - 1, 0:2 * HE],
                                        ALU.mult).then_inc(m_u.sem, 1)

            def add_out(t):
                m_y.done(dve, t)
                xb = xbase[:, t, :]
                nc.vector.scalar_tensor_tensor(out=xb, in0=bank["y"][:, 0:D], scalar=tg[:, 3:4], in1=xb,
                                               op0=ALU.mult, op1=ALU.add).then_inc(m_out.sem, 1)

            gated(0, 0)
            with dve.Fori(0, B // 2 - 1) as p:
                gated(p * 2 + 1, 1)
                add_out(p * 2)
                gated(p * 2 + 2, 0)
                add_out(p * 2 + 1)
            gated(B - 1, 1)
            add_out(B - 2)
            add_out(B - 1)

        @block.gpsimd
        def _(pool):
            for s in (pool_add, pool_norm):
                pool.sem_inc(s.sem, s.credit)
            nc.gpsimd.memset(k_z[:, :, :], 0.0)
            pool.wait_ge(in_const, 16)
            pool.wait_ge(in_par, PAR)

            def stage(cross, b, r, step):
                i = nc.gpsimd.tensor_copy(xcur[:, r, :], (xfT if cross else xT)[:, b, :])
                if cross:
                    i = nc.gpsimd.tensor_copy(ccur[:, r, :], cT[:, b, :])
                i.then_inc(step, 1)

            def attention(base, kind, seq0):
                window = kind == "local"

                def run(g0, b0, s, on):
                    if on(3):
                        g, r = g0 + s - 3, (s - 3) % 2
                        dve_rs.done(pool, g)
                        nc.gpsimd.tensor_tensor(probs[:, r], probs[:, r], rsum[:, r, :].unsqueeze(2).to_broadcast([T, HG, T]),
                                                ALU.mult).then_inc(pool_pn.sem, 1)
                    if on(1) and window:
                        g, r = g0 + s - 1, (s - 1) % 2
                        pool.wait_ge(dve_rn, (g + 1) * (RS_OPS + 1))
                        pool_add.done(pool, g)
                        pe_T.free(pool, g, 2)
                        u = rot[:, :].rearrange("p (m h d) -> p m h d", m=2, d=DH)
                        n = rn[:, r, :].rearrange("p (m h) -> p m h", m=2).unsqueeze(3).to_broadcast([T, 2, HG, DH])
                        nc.gpsimd.tensor_tensor(q_n[:, r, :].rearrange("p (h d) -> p h d", d=DH), u[:, 0], n[:, 0], ALU.mult)
                        kd = k_z[:, r, :].rearrange("p (a z) -> p a z", a=2)
                        for o in range(2):
                            uk = u[:, 1].rearrange("p (a o) d -> p a o d", o=2)[:, :, o, :]
                            nk = rn[:, r, HG + o:2 * HG:2].unsqueeze(2).to_broadcast([T, 2, DH])
                            i = nc.gpsimd.tensor_tensor(kd[:, :, 2 * DH * o:2 * DH * o + DH], uk, nk, ALU.mult)
                        i.then_inc(pool_norm.sem, 1)
                    if on(0) and window:
                        g, r = g0 + s, s % 2
                        dve_qk.done(pool, g)
                        pool_norm.free(pool, g, 1)
                        nc.gpsimd.tensor_tensor(rot[:, :], rot_a[:, r, :], rot_b[:, r, :], ALU.add).then_inc(pool_add.sem, 1)
                    if on(0) and s % GPB == 1 and s // GPB + 1 < B:
                        stage(not window, b0 + s // GPB + 1, (s // GPB + 1) % 2, pool_cur.sem)

                pipeline(pool, base, run, first=LAG - 1)

            with pool.Fori(0, DEPTH) as l:
                xT_ready.done(pool, l + 1)
                H = DH // 2
                nc.gpsimd.tensor_tensor(tab_cos[:, :, :], cst[:, C_COS:C_COS + 2 * DH].rearrange("p (m d) -> p m d", m=2),
                                        scales[:, l, :, :], ALU.mult)
                stage(False, 0, 0, pool_cur.sem)
                nc.gpsimd.tensor_copy(lpar[:, :], lpar_all[:, :, l])
                sin = cst[:, C_SIN:C_SIN + 2 * DH].rearrange("p (m d) -> p m d", m=2)
                nc.gpsimd.tensor_tensor(tab_sin[:, :, 0:H], sin[:, :, 0:H], scales[:, l, :, H:DH], ALU.mult)
                nc.gpsimd.tensor_tensor(tab_sin[:, :, H:DH], sin[:, :, H:DH], scales[:, l, :, 0:H], ALU.mult).then_inc(tab_ready.sem, 1)
                attention(l * GPL, "local", l * B)
                act_half.done(pool, l)
                pe_sh.done(pool, l)
                nc.gpsimd.tensor_tensor(xres[:, :, :], xres[:, :, :],
                                        b2_all[:, l, :].unsqueeze(1).to_broadcast([T, B, D]), ALU.add).then_inc(pool_b2.sem, 1)
            xT_ready.done(pool, DEPTH + 1)
            stage(True, 0, 0, pool_cur.sem)
            attention(DEPTH * GPL, "cross", DEPTH * B)

            def weigh(t, r):
                m_u.done(pool, t)
                nc.gpsimd.tensor_tensor(mh[:, r, 0:E // 4, :].rearrange("p c (e h) -> p (c e) h", h=HE),
                                        mh[:, r, 0:E // 4, :].rearrange("p c (e h) -> p (c e) h", h=HE),
                                        cw[:, t, :].unsqueeze(2).to_broadcast([T, E, HE]), ALU.mult).then_inc(m_w.sem, 1)

            def stage_tile(t, r):
                nc.gpsimd.tensor_copy(xcur[:, r, :], xfT[:, t, :]).then_inc(m_cur.sem, 1)

            xT_ready.done(pool, DEPTH + 2)
            pool.wait_ge(moe_dve, 3)
            stage_tile(0, 0)
            stage_tile(1, 1)
            weigh(0, 0)
            with pool.Fori(0, B // 2 - 1) as p:
                stage_tile(p * 2 + 2, 0)
                weigh(p * 2 + 1, 1)
                stage_tile(p * 2 + 3, 1)
                weigh(p * 2 + 2, 0)
            weigh(B - 1, 1)


_IN = ['x', 'ctx_768', 'g_xattn', 'g_ffn', 'L0_xattn_Wv', 'L0_xattn_bv', 'L0_xattn_Wt', 'L0_xattn_bt', 'L0_ffn_Wqkv',
       'L0_ffn_q_scale', 'L0_ffn_k_scale', 'L0_ffn_Wo', 'L0_ffn_ln_g', 'L0_ffn_ln_b', 'L0_ffn_W1', 'L0_ffn_b1', 'L0_ffn_W2',
       'L0_ffn_b2', 'L1_xattn_Wq', 'L1_xattn_Wk', 'L1_xattn_Wv', 'L1_xattn_Wo', 'L1_xattn_bo', 'L1_ffn_Wg', 'L1_ffn_W1',
       'L1_ffn_W2', 'L1_ffn_Ws1', 'L1_ffn_Ws2']


def kernel(**inputs):
    import concourse.bacc as bacc
    from concourse.bass_utils import run_bass_kernel_spmd

    nc = bacc.Bacc("TRN2", target_bir_lowering=False, num_devices=1)
    arrays = {f"in_{n}": np.ascontiguousarray(inputs[n]) for n in _IN}
    arrays["in_consts"] = shape_constants()
    args = [nc.dram_tensor(n, a.shape, mybir.dt.from_np(a.dtype), kind="ExternalInput").ap() for n, a in arrays.items()]
    res = nc.dram_tensor("out", (B, T, D), F32, kind="ExternalOutput").ap()
    build(nc, *args, res)
    r = run_bass_kernel_spmd(nc, [arrays], core_ids=[0])
    return r.results[0]["out"]
```

```python
from contextlib import ExitStack

import numpy as np

import concourse.bass as bass
from concourse import mybir

ALU = mybir.AluOpType
ACT = mybir.ActivationFunctionType
AX = mybir.AxisListType
F32 = mybir.dt.float32
BF16 = mybir.dt.bfloat16
I32 = mybir.dt.int32

B = 8
T = 128
D = 128
DC = 96
HEADS = 16
DH = 64
INNER = HEADS * DH
WINDOW = 32
DEPTH = 6
DFF = int(D * 4 * 2 / 3)
HSIM = 64
E = 16
HE = 64
HG = 4
GPB = HEADS // HG
GPL = B * GPB
LAG = 7
UNROLL = 8
GW = HG * DH
FCH = [(c, min(128, DFF - c)) for c in range(0, DFF, 128)]
NF = len(FCH)
NP = 2 + 2 * NF
RSQRT_SEED = float(0x5F3759DF)
NEWTON = 3
RS_OPS = 1 + 3 * NEWTON
LN_OPS = 5 + RS_OPS
C_ID, C_SH, C_MASK, C_COS, C_SIN, C_IOTA, C_END = 0, 128, 256, 384, 512, 640, 656


def shape_constants():
    c = np.zeros((T, C_END), np.float32)
    c[:, C_ID:C_ID + T] = np.eye(T)
    c[:, C_SH:C_SH + T] = np.eye(T, k=1)
    i, j = np.arange(T)[:, None], np.arange(T)[None, :]
    seen = (j // WINDOW >= i // WINDOW - 1) & (j <= i) & (i <= j + WINDOW)
    c[:, C_MASK:C_MASK + T] = np.where(seen, 0.0, -1e30)
    half = np.arange(0, DH, 2, dtype=np.float32)
    inv = (1.0 / 10000.0 ** (half / DH)).astype(np.float32)
    t = np.arange(T, dtype=np.float32)
    freqs = (t[:, None] * inv[None, :]).astype(np.float32)
    base = ((half + 0.4 * DH) / (1.4 * DH)).astype(np.float32)
    power = ((t - T // 2) / (WINDOW // 2)).astype(np.float32)
    scale = (base[None, :] ** power[:, None]).astype(np.float32)
    cos, sin = np.cos(freqs), np.sin(freqs)
    for n, s in enumerate((8.0 * scale, 1.0 / scale)):
        c[:, C_COS + n * DH:C_COS + (n + 1) * DH] = np.concatenate([cos * s, cos * s], 1)
        c[:, C_SIN + n * DH:C_SIN + (n + 1) * DH] = np.concatenate([-sin * s, sin * s], 1)
    c[:, C_IOTA:C_IOTA + E] = np.arange(E)
    return c


class Steps:

    def __init__(self, sem, credit=0):
        self.sem, self.credit = sem, credit

    def done(self, eng, step):
        eng.wait_ge(self.sem, step + 1 + self.credit)

    def free(self, eng, step, ring):
        assert self.credit >= ring
        eng.wait_ge(self.sem, step + 1 - ring + self.credit)


def build(nc, x, ctx, g_xattn, g_ffn, s_Wv, s_bv, s_Wt, s_bt, Wqkv, q_scale, k_scale, Wo, ln_g, ln_b, W1, b1,
          W2, b2, x_Wq, x_Wk, x_Wv, x_Wo, x_bo, m_Wg, m_W1, m_W2, m_Ws1, m_Ws2, consts, out):
    with ExitStack() as stack:
        def sb(name, shape, dt=F32):
            return stack.enter_context(nc.sbuf_tensor(name, shape, dt))

        def sem(name):
            return stack.enter_context(nc.semaphore(name))

        def steps(name, credit=0):
            return Steps(sem(name), credit)

        cst = sb("cst", [T, C_END])
        ident = cst[:, C_ID:C_ID + T]
        shift = cst[:, C_SH:C_SH + T]
        ident_b = sb("ident_b", [T, T], BF16)
        masks = sb("masks", [T, 2, T], BF16)
        ones = sb("ones", [T, T])
        xbase = sb("xbase", [T, B, D])
        xres = sb("xres", [T, B, D])
        xsh = sb("xsh", [T, B // 2, D])
        xn = sb("xn", [T, B, D])
        xT = sb("xT", [D, B, T])
        xfT = sb("xfT", [D, B, T])
        xcur = sb("xcur", [D, 2, T])
        ctx_sb = sb("ctx_sb", [T, B, DC])
        cT = sb("cT", [DC, B, T])
        ccur = sb("ccur", [DC, 2, T])
        gates = sb("gates", [T, 4])
        tg = sb("tg", [T, 4])
        wv_n = sb("wv_n", [HSIM, D])
        wt_n = sb("wt_n", [HSIM, DC])
        wvT = sb("wvT", [D, HSIM])
        wtT = sb("wtT", [DC, HSIM])
        bvt = sb("bvt", [HSIM, 2])
        vT = sb("vT", [HSIM, B * T])
        tT = sb("tT", [HSIM, B * T])
        vsq = sb("vsq", [HSIM, B * T])
        tsq = sb("tsq", [HSIM, B * T])
        vn2 = sb("vn2", [T, B])
        den = sb("den", [T, B, T])
        wqkv = sb("wqkv", [D, 2, 3 * INNER])
        wo = sb("wo", [D, INNER // 128, D])
        scales = sb("scales", [T, DEPTH, 2, DH])
        tab_cos = sb("tab_cos", [T, 2, DH])
        tab_sin = sb("tab_sin", [T, 2, DH])
        sq = sb("sq", [T, 2, 512])
        rot_a = sb("rot_a", [T, 2, 512])
        rot_b = sb("rot_b", [T, 2, 512])
        rot = sb("rot", [T, 512])
        n2 = sb("n2", [T, 2, 8])
        nt = sb("nt", [T, 8])
        rn = sb("rn", [T, 2, 8])
        q_n = sb("q_n", [T, 2, GW])
        k_n = sb("k_n", [T, 2, GW])
        qT = sb("qT", [T, 2, 2, T])
        kT = sb("kT", [T, 2, HG, T])
        v_n = sb("v_n", [T, UNROLL, GW])
        negm = sb("negm", [T, 2, HG])
        probs = sb("probs", [T, 2, HG, T])
        sums = sb("sums", [T, 2, HG])
        rsum = sb("rsum", [T, 2, HG])
        pT = sb("pT", [T, 2, HG, T])
        oT = sb("oT", [T, 2, INNER // 128, T])
        w1 = sb("w1", [D, 2 * DFF])
        w2 = sb("w2", [128, NF, D])
        par_rows = sb("par_rows", [NP * DEPTH, 128])
        lpar_all = sb("lpar_all", [D, NP, DEPTH])
        lpar = sb("lpar", [D, NP])
        b2_all = sb("b2_all", [T, DEPTH, D])
        bo_b = sb("bo_b", [T, D])
        stats = sb("stats", [T, B, 6])
        mean = sb("mean", [T, B])
        lvar = sb("lvar", [T, B])
        lt = sb("lt", [T, B])
        lr = sb("lr", [T, B])
        gact = sb("gact", [128, NF, 512])
        hT = sb("hT", [128, NF, 512])
        wg_n = sb("wg_n", [E, D])
        wgT = sb("wgT", [D, E])
        mw1 = sb("mw1", [D, E, 2 * HE])
        mw2 = sb("mw2", [128, E * HE // 128, D])
        ws1 = sb("ws1", [D, 4 * HE])
        ws2 = sb("ws2", [2 * HE, D])
        sc = sb("sc", [T, B, E])
        scm = sb("scm", [T, B])
        scs = sb("scs", [T, B])
        sc2 = sb("sc2", [T, B, E])
        top = sb("top", [T, B, 8])
        tidx = sb("tidx", [T, B, 8], mybir.dt.uint32)
        tidf = sb("tidf", [T, B, 2])
        cw = sb("cw", [T, B, E])
        NCH = E // 4 + 1
        sg = sb("sg", [T, 2, NCH, 256])
        mh = sb("mh", [T, 2, NCH, 256])
        mhT = sb("mhT", [128, 2, 12, T])

        bank = {n: stack.enter_context(nc.psum_tensor("ps_" + n, [128, 512], F32))
                for n in ("qk", "v", "qkt", "s", "pt", "ot", "f0", "f1")}
        by_head = {n: b[:, :].rearrange("p (h t) -> p h t", t=128) for n, b in bank.items()}

        in_const, in_x, in_sim, in_par, in_moe = (sem("in_" + n) for n in ("const", "x", "sim", "par", "moe"))
        in_qkv, in_wo, in_ffn = sem("in_qkv"), sem("in_wo"), sem("in_ffn")
        out_done = sem("out_done")
        setup, par_clear = sem("setup"), sem("par_clear")
        pe_v, pe_qk, pe_T, pe_S, pe_PT, pe_PV, pe_Y = (
            steps(n, c) for n, c in (("pe_v", 0), ("pe_qk", 2), ("pe_T", 2), ("pe_S", 2), 
                                     ("pe_PT", 2), ("pe_PV", 2), ("pe_Y", 2)))
        act_qk, act_T, act_v, act_exp, act_PT, act_OT = (
            steps(n, c) for n, c in (("act_qk", 1), ("act_T", 1), ("act_v", 1), ("act_exp", 2), ("act_PT", 1), ("act_OT", 1)))
        dve_qk, dve_y, dve_n2 = steps("dve_qk", 1), steps("dve_y", 1), steps("dve_n2", 2)
        dve_max, dve_rs, dve_rn = steps("dve_max"), steps("dve_rs"), sem("dve_rn")
        pool_add, pool_norm, pool_pn = steps("pool_add", 2), steps("pool_norm", 2), steps("pool_pn")
        pool_cur = steps("pool_cur")
        x_ready, pe_xt, xf_ready = steps("x_ready"), steps("pe_xt"), steps("xf_ready")
        tab_ready, lpar_ready = steps("tab_ready"), steps("lpar_ready")
        ln = sem("ln")
        pe_sh, dve_sh, xn_ready, pe_nt, act_nt = (steps(n) for n in ("pe_sh", "dve_sh", "xn_ready", "pe_nt", "act_nt"))
        pe_gate, act_gate, act_gelu, pe_a, dve_h, pe_f, pool_b2, x_half = (steps(n) for n in (
            "pe_gate", "act_gate", "act_gelu", "pe_a", "dve_h", "pe_f", "pool_b2", "x_half"))
        pe_xh, xh_ready = steps("pe_xh"), steps("xh_ready")
        sim_pe, sim_act, sim_dve = sem("sim_pe"), sem("sim_act"), sem("sim_dve")
        moe_pe, moe_act, moe_dve, moe_self = sem("moe_pe"), sem("moe_act"), sem("moe_dve"), sem("moe_self")
        m_cur, m_h, m_silu, m_u, m_w, m_T, m_ev, m_y, m_out = (steps(n, c) for n, c in (
            ("m_cur", 0), ("m_h", 2), ("m_silu", 1), ("m_u", 2), ("m_w", 0), ("m_T", 6), ("m_ev", 2), ("m_y", 2),
            ("m_out", 1)))

        block = stack.enter_context(nc.Block())


        def local_layers(run):
            def layers(eng):
                for s in range(GPL // 2):
                    run(0, 0, 0, s, lambda lag, s=s: s - lag >= 0, False)
                with eng.Fori(0, DEPTH - 1) as l:
                    for s in range(GPL // 2, GPL // 2 + GPL):
                        run(l * GPL, l, 0, s, lambda lag: True, False)
                for s in range(GPL // 2, GPL // 2 + GPL):
                    run((DEPTH - 1) * GPL, DEPTH - 1, 0, s, lambda lag, s=s: s - lag < GPL, True)
            return layers

        def cross_layer(run, first=LAG):
            def layer(eng):
                base = DEPTH * GPL
                for s in range(first):
                    run(base, DEPTH, 0, s, lambda lag, s=s: s - lag >= 0, True)
                rounds = GPL // UNROLL - 1
                with eng.Fori(0, rounds) as it:
                    for s in range(first, first + UNROLL):
                        run(base + it * UNROLL, DEPTH, it * (UNROLL // GPB), s, lambda lag: True, True)
                for s in range(first + rounds * UNROLL, GPL + LAG):
                    run(base, DEPTH, 0, s, lambda lag, s=s: s - lag < GPL, True)
            return layer

        def ffn_step(window, s):
            for h in range(2):
                f = s - (GPL // 2 * (h + 1) + LAG - 1)
                if window and 0 <= f <= GPL // 2 - LAG:
                    return h, f
            return None, None

        def rsqrt_step(dve, k, r, v, t, sig, at):
            if k == 0:
                i = nc.vector.tensor_scalar(r.bitcast(I32), v.bitcast(I32), -0.5, RSQRT_SEED, ALU.mult, ALU.add)
            else:
                dve.wait_ge(sig, at + k)
                if k % 3 == 1:
                    i = nc.vector.tensor_tensor(t, r, r, ALU.mult)
                elif k % 3 == 2:
                    i = nc.vector.scalar_tensor_tensor(out=t, in0=t, scalar=-0.5, in1=v, op0=ALU.mult, op1=ALU.mult)
                else:
                    i = nc.vector.scalar_tensor_tensor(out=r, in0=t, scalar=1.5, in1=r, op0=ALU.add, op1=ALU.mult)
            i.then_inc(sig, 1)

        def layernorm_step(dve, k, dst, src, tiles, call, done):
            at = call * LN_OPS
            if k:
                dve.wait_ge(ln, at + k)
            if k == 0:
                for b in range(tiles):
                    i = nc.vector.bn_stats(stats[:, b, :], src[:, b, :])
                i.then_inc(ln, 1)
                return
            me, ve, mo, vo = (stats[:, 0:tiles, j] for j in (1, 2, 4, 5))
            m, v, t, r = (z[:, 0:tiles] for z in (mean, lvar, lt, lr))
            if k == 1:
                nc.vector.tensor_tensor(m, me, mo, ALU.add)
                nc.vector.tensor_tensor(t, me, mo, ALU.subtract)
                nc.vector.tensor_tensor(v, ve, vo, ALU.add).then_inc(ln, 1)
            elif k == 2:
                nc.vector.tensor_scalar(m, m, 0.5, None, ALU.mult)
                nc.vector.tensor_tensor(t, t, t, ALU.mult).then_inc(ln, 1)
            elif k == 3:
                nc.vector.tensor_scalar(t, t, 0.25, 1e-5, ALU.mult, ALU.add).then_inc(ln, 1)
            elif k == 4:
                nc.vector.scalar_tensor_tensor(out=v, in0=v, scalar=1.0 / D, in1=t, op0=ALU.mult, op1=ALU.add).then_inc(ln, 1)
            elif k < LN_OPS:
                rsqrt_step(dve, k - 5, r, v, t, ln, at + 5)
            else:
                for b in range(tiles):
                    i = nc.vector.tensor_scalar(dst[:, b, :], src[:, b, :], m[:, b:b + 1], r[:, b:b + 1],
                                                ALU.subtract, ALU.mult)
                i.then_inc(done.sem, 1)

        def layernorm(dve, dst, src, call, done):
            for k in range(LN_OPS + 1):
                layernorm_step(dve, k, dst, src, B, call, done)

        @block.sync
        def _(sp):
            sp.dma_start(cst[:, :], consts).then_inc(in_const, 16)
            sp.dma_start(xbase[:, :, :], x.rearrange("b t d -> t b d")).then_inc(in_x, 16)
            sp.dma_start(ctx_sb[:, :, :], ctx.rearrange("b t d -> t b d")).then_inc(in_sim, 16)
            sp.dma_start(wv_n[:, :], s_Wv).then_inc(in_sim, 16)
            sp.dma_start(wt_n[:, :], s_Wt).then_inc(in_sim, 16)
            sp.dma_start(bvt[:, 0:1], s_bv.rearrange("(h o) -> h o", o=1)).then_inc(in_sim, 16)
            sp.dma_start(bvt[:, 1:2], s_bt.rearrange("(h o) -> h o", o=1)).then_inc(in_sim, 16)
            sp.dma_start(gates[:, 0:2], g_xattn.rearrange("(o n) -> o n", o=1).to_broadcast([T, 2])).then_inc(in_sim, 16)
            sp.dma_start(gates[:, 2:4], g_ffn.rearrange("(o n) -> o n", o=1).to_broadcast([T, 2])).then_inc(in_sim, 16)
            for m in range(3):
                sp.dma_start(wqkv[:, 0, m * INNER:(m + 1) * INNER], Wqkv[0, :, m * INNER:(m + 1) * INNER]).then_inc(in_qkv, 16)
            for m, s in enumerate((q_scale, k_scale)):
                sp.dma_start(scales[:, :, m, :], s.rearrange("(o l) d -> o l d", o=1).to_broadcast([T, DEPTH, DH])).then_inc(in_par, 16)
            sp.dma_start(wo[:, :, :], Wo[0].rearrange("(c p) d -> p c d", p=128)).then_inc(in_wo, 16)

            def load_ffn(l):
                sp.dma_start(w1[:, :], W1[l]).then_inc(in_ffn, 16)
                sp.dma_start(w2[:, 0:NF - 1, :], W2[l, 0:128 * (NF - 1), :].rearrange("(c p) d -> p c d", p=128)).then_inc(in_ffn, 16)
                sp.dma_start(w2[0:FCH[-1][1], NF - 1, :], W2[l, FCH[-1][0]:DFF, :]).then_inc(in_ffn, 16)

            load_ffn(0)
            sp.wait_ge(par_clear, 1)
            for m, s in enumerate((ln_g, ln_b)):
                sp.dma_start(par_rows[m * DEPTH:(m + 1) * DEPTH, :], s).then_inc(in_par, 16)
            for m in range(2):
                for c, (f0, fn) in enumerate(FCH):
                    k = 2 + m * NF + c
                    sp.dma_start(par_rows[k * DEPTH:(k + 1) * DEPTH, 0:fn],
                                 b1[:, m * DFF + f0:m * DFF + f0 + fn]).then_inc(in_par, 16)
            sp.dma_start(b2_all[:, :, :], b2.rearrange("(o l) d -> o l d", o=1).to_broadcast([T, DEPTH, D])).then_inc(in_par, 16)
            sp.dma_start(bo_b[:, :], x_bo.rearrange("(o d) -> o d", o=1).to_broadcast([T, D])).then_inc(in_par, 16)
            sp.dma_start(wg_n[:, :], m_Wg).then_inc(in_moe, 16)
            sp.dma_start(mw1[:, :, :], m_W1.rearrange("e d h -> d e h")).then_inc(in_moe, 16)
            sp.dma_start(mw2[:, :, :], m_W2.rearrange("(c e) h d -> (e h) c d", e=2)).then_inc(in_moe, 16)
            sp.dma_start(ws1[:, :], m_Ws1).then_inc(in_moe, 16)
            sp.dma_start(ws2[:, :], m_Ws2).then_inc(in_moe, 16)
            pe_v.done(sp, 0)
            for m in range(3):
                sp.dma_start(wqkv[:, 1, m * INNER:(m + 1) * INNER], Wqkv[1, :, m * INNER:(m + 1) * INNER]).then_inc(in_qkv, 16)
            with sp.Fori(0, DEPTH - 2) as l:
                pe_v.done(sp, l * GPL + GPL - 1)
                for m in range(3):
                    sp.dma_start(wqkv[:, l % 2, m * INNER:(m + 1) * INNER], Wqkv[l + 2, :, m * INNER:(m + 1) * INNER]).then_inc(in_qkv, 16)
                pe_Y.done(sp, l * B + B - 1)
                sp.dma_start(wo[:, :, :], Wo[l + 1].rearrange("(c p) d -> p c d", p=128)).then_inc(in_wo, 16)
                pe_f.done(sp, l * 2 + 1)
                load_ffn(l + 1)
            pe_v.done(sp, (DEPTH - 1) * GPL - 1)
            sp.dma_start(wqkv[:, 0, 0:INNER], x_Wq).then_inc(in_qkv, 16)
            sp.dma_start(wqkv[0:DC, 0, INNER:2 * INNER], x_Wk).then_inc(in_qkv, 16)
            sp.dma_start(wqkv[0:DC, 0, 2 * INNER:3 * INNER], x_Wv).then_inc(in_qkv, 16)
            pe_Y.done(sp, (DEPTH - 1) * B - 1)
            sp.dma_start(wo[:, :, :], Wo[DEPTH - 1].rearrange("(c p) d -> p c d", p=128)).then_inc(in_wo, 16)
            pe_f.done(sp, (DEPTH - 1) * 2 - 1)
            load_ffn(DEPTH - 1)
            pe_Y.done(sp, DEPTH * B - 1)
            sp.dma_start(wo[:, :, :], x_Wo.rearrange("(c p) d -> p c d", p=128)).then_inc(in_wo, 16)
            m_out.done(sp, B - 1)
            sp.dma_start(out.rearrange("b t d -> t b d"), xbase[:, :, :]).then_inc(out_done, 16)
            sp.wait_ge(out_done, 16)

        PAR = 16 * (4 + 2 * NF + 2)

        @block.tensor
        def _(pe):
            for s in (pe_v, pe_qk, pe_T, pe_S, pe_PT, pe_PV, pe_Y, m_h, m_T, m_y):
                if s.credit:
                    pe.sem_inc(s.sem, s.credit)

            def tiles_T(src, done):
                for h, bk in enumerate(("f0", "f1")):
                    for j in range(4):
                        i = nc.tensor.transpose(by_head[bk][:, j, :], src[:, 4 * h + j, :], ident)
                    i.then_inc(done.sem, 1)

            pe.wait_ge(in_const, 16)
            pe.wait_ge(in_sim, 16 * 7)
            nc.tensor.transpose(bank["v"][:, 0:HSIM], wv_n[:, :], ident[0:HSIM, 0:HSIM])
            nc.tensor.transpose(bank["v"][0:DC, HSIM:2 * HSIM], wt_n[:, :], ident[0:HSIM, 0:HSIM])
            pe.wait_ge(in_par, PAR)
            nc.tensor.transpose(bank["v"][:, 128:128 + NP * DEPTH], par_rows[:, :], ident[0:NP * DEPTH, 0:NP * DEPTH])
            for h, bk in enumerate(("s", "pt")):
                for j in range(4):
                    i = nc.tensor.transpose(by_head[bk][0:DC, j, :], ctx_sb[:, 4 * h + j, :], ident)
            i.then_inc(sim_pe, 1)
            x_ready.done(pe, 0)
            tiles_T(xn, pe_xt)
            pe.wait_ge(sim_act, 2)
            xf_ready.done(pe, 0)
            for h, bk in enumerate(("qk", "v")):
                nc.tensor.matmul(bank[bk][0:HSIM, :], wvT[:, :], xfT[:, 4 * h:4 * h + 4, :], start=True, stop=True)
            for h, bk in enumerate(("s", "pt")):
                i = nc.tensor.matmul(bank[bk][0:HSIM, :], wtT[:, :], cT[:, 4 * h:4 * h + 4, :], start=True, stop=True)
            i.then_inc(sim_pe, 1)
            pe.wait_ge(sim_act, 6)
            pe.wait_ge(setup, 1)
            for h, bk in enumerate(("f0", "f1")):
                i = nc.tensor.matmul(bank[bk][:, :], ones[0:HSIM, :], tsq[:, 512 * h:512 * h + 512], start=True, stop=True)
            for b in range(B):
                i = nc.tensor.matmul(bank["qkt"][:, b:b + 1], vsq[:, b * T:b * T + T], ones[0:HSIM, 0:1], start=True, stop=True)
            i.then_inc(sim_pe, 1)
            for b in range(B):
                i = nc.tensor.matmul(by_head["ot" if b < 4 else "qk"][:, b % 4, :], vT[:, b * T:b * T + T],
                                     tT[:, b * T:b * T + T], start=True, stop=True)
            i.then_inc(sim_pe, 1)

            def stages(window):
                def run(base, l, b0, s, on, last):
                    seq0, gi, bs = l * B + b0, s % GPB, s // GPB % B
                    x_in = xT[:, bs, :] if window else xcur[:, bs % 2, :]
                    lhs = x_in if window else ccur[:, bs % 2, :]
                    rows = D if window else DC
                    w = wqkv[:, (l + s // GPL) % 2, :]
                    half, f = ffn_step(window, s)
                    unit = l * 2 + half if half is not None else None

                    def gate(c):
                        f0, fn = FCH[c]
                        nc.tensor.matmul(bank["f1" if c == 1 else "f0"][0:fn, :], w1[:, DFF + f0:DFF + f0 + fn],
                                         xfT[:, 0:4, :], start=True, stop=True).then_inc(pe_gate.sem, 1)

                    def value(c):
                        f0, fn = FCH[c]
                        nc.tensor.matmul(bank["f1" if c == 1 else "f0"][0:fn, :], w1[:, f0:f0 + fn],
                                         xfT[:, 0:4, :], start=True, stop=True).then_inc(pe_a.sem, 1)

                    def down(j):
                        for c, (f0, fn) in enumerate(FCH):
                            i = nc.tensor.matmul(by_head["f0"][:, j, :], hT[0:fn, c, j * T:j * T + T], w2[0:fn, c, :],
                                                 start=(c == 0), stop=(c == NF - 1))
                        return i

                    if f == 4:
                        xn_ready.done(pe, unit)
                        if not (last and half):
                            xh_ready.done(pe, unit + 1)
                        for j in range(4):
                            i = nc.tensor.transpose(by_head["f1"][:, j, :], xn[:, j, :], ident)
                        i.then_inc(pe_nt.sem, 1)
                    if f == 5:
                        act_gate.done(pe, unit)
                        gate(0)
                    if on(0):
                        g = base + s
                        if s == 0 and window:
                            pe.wait_ge(in_qkv, 48)
                        if s == GPL - 1 and window and not last:
                            pe.wait_ge(in_qkv, (l + 2) * 48)
                        if s % (GPL // 2) == 0 and window:
                            xh_ready.done(pe, l * 2 + s // (GPL // 2))
                        if gi == 0 and not window:
                            pool_cur.done(pe, b0 + s // GPB)
                        act_qk.free(pe, g, 1)
                        dve_qk.free(pe, g, 1)
                        nc.tensor.matmul(bank["qk"][:, 0:GW], x_in, w[:, gi * GW:(gi + 1) * GW], start=True, stop=True)
                        nc.tensor.matmul(bank["qk"][:, GW:2 * GW], lhs, w[0:rows, INNER + gi * GW:INNER + (gi + 1) * GW],
                                         start=True, stop=True).then_inc(pe_qk.sem, 1)
                    lag = 3 if window else 2
                    if on(lag):
                        g, r = base + s - lag, (s - lag) % 2
                        if window:
                            pool_norm.done(pe, g)
                        else:
                            act_qk.done(pe, g)
                            dve_qk.done(pe, g)
                        act_T.free(pe, g, 1)
                        for p in range(2):
                            nc.tensor.transpose(by_head["qkt"][:, p, :], k_n[:, r, p * 128:p * 128 + 128], ident)
                        for p in range(2):
                            i = nc.tensor.transpose(by_head["qkt"][:, 2 + p, :], q_n[:, r, p * 128:p * 128 + 128], ident)
                        i.then_inc(pe_T.sem, 1)
                    if on(4):
                        g, r = base + s - 4, (s - 4) % 2
                        act_T.done(pe, g)
                        act_exp.free(pe, g, 1)
                        nc.tensor.matmul(by_head["s"], ident_b[:, :],
                                         masks[:, 0 if window else 1, :].unsqueeze(1).to_broadcast([T, HG, T]),
                                         start=True, stop=False, skip_group_check=True)
                        for h in range(HG):
                            i = nc.tensor.matmul(by_head["s"][:, h, :], qT[:, r, h // 2, :], kT[:, r, h, :],
                                                 start=False, stop=(h == HG - 1), skip_group_check=True)
                        i.then_inc(pe_S.sem, 1)
                    if on(7) and (s - 7) % GPB == GPB - 1:
                        ys = (s - 7) // GPB
                        if ys % B == 0 and window:
                            pe.wait_ge(in_wo, (l + ys // B + 1) * 16)
                        act_OT.done(pe, base + s - 7)
                        dve_y.free(pe, seq0 + ys, 1)
                        if f == 4:
                            act_nt.done(pe, unit)
                        if f == 8:
                            dve_h.done(pe, unit * NF + 1)
                        if window and s == GPL + 2 and last:
                            x_half.done(pe, l * 2)
                        for c in range(INNER // 128):
                            i = nc.tensor.matmul(bank["f1" if f in (4, 8) else "f0"][:, 0:D], oT[:, ys % 2, c, :], wo[:, c, :],
                                                 start=(c == 0), stop=(c == INNER // 128 - 1))
                        i.then_inc(pe_Y.sem, 1)
                    if on(6):
                        g, r = base + s - 6, (s - 6) % 2
                        act_PT.done(pe, g)
                        act_OT.free(pe, g, 1)
                        vs = v_n[:, (s - 6) % UNROLL, :]
                        for h in range(HG):
                            i = nc.tensor.matmul(by_head["ot"][64 * (h % 2):64 * (h % 2) + 64, h // 2, :],
                                                 vs[:, h * DH:(h + 1) * DH], pT[:, r, h, :], start=True, stop=True)
                        i.then_inc(pe_PV.sem, 1)
                    if f == 4:
                        pe.wait_ge(in_ffn, (l + 1) * 48)
                        act_nt.done(pe, unit)
                        gate(2)
                    if f == 6:
                        act_gelu.done(pe, unit)
                        value(0)
                    if f == 7:
                        dve_h.done(pe, unit * NF)
                        value(2)
                    if f == 8:
                        dve_h.done(pe, unit * NF + 2)
                        down(0)
                        down(1)
                    if f == 9 and not last:
                        x_half.done(pe, unit)
                        dve_y.done(pe, l * B + (s - 1 - LAG) // GPB)
                        for j in range(4):
                            i = nc.tensor.transpose(by_head["f1"][:, j, :], xres[:, 4 * half + j, :], ident)
                        i.then_inc(pe_xh.sem, 1)
                    if on(0):
                        g = base + s
                        act_v.free(pe, g, 1)
                        nc.tensor.matmul(bank["v"][:, 0:GW], lhs, w[0:rows, 2 * INNER + gi * GW:2 * INNER + (gi + 1) * GW],
                                         start=True, stop=True).then_inc(pe_v.sem, 1)
                    if on(5):
                        g, r = base + s - 5, (s - 5) % 2
                        pool_pn.done(pe, g)
                        act_PT.free(pe, g, 1)
                        for h in range(HG):
                            i = nc.tensor.transpose(by_head["pt"][:, h, :], probs[:, r, h, :], ident)
                        i.then_inc(pe_PT.sem, 1)
                    if f == 0:
                        dve_y.done(pe, l * B + half * 4 + 3)
                        nc.tensor.matmul(bank["f0"][:, 0:4 * D // 2], shift, xres[:, 4 * half:4 * half + 4, D // 2:D],
                                         start=True, stop=True).then_inc(pe_sh.sem, 1)
                    if f == 4:
                        if on(LAG):
                            dve_y.done(pe, l * B + (s - LAG) // GPB)
                        gate(1)
                    if f == 6:
                        value(1)
                    if f == 8:
                        down(2)
                        down(3).then_inc(pe_f.sem, 1)
                return run

            x_ready.done(pe, 1)
            for h, bk in enumerate(("f0", "f1")):
                for j in range(4):
                    i = nc.tensor.transpose(by_head[bk][:, j, :], xres[:, 4 * h + j, :], ident)
                i.then_inc(pe_xh.sem, 1)
            local_layers(stages(True))(pe)

            x_ready.done(pe, 2)
            tiles_T(xn, pe_xt)
            pe.wait_ge(in_qkv, DEPTH * 48 + 48)
            pe.wait_ge(in_wo, DEPTH * 16 + 16)
            cross_layer(stages(False))(pe)

            pe.wait_ge(in_moe, 16 * 5)
            nc.tensor.transpose(bank["v"][:, 0:E], wg_n[:, :], ident[0:E, 0:E]).then_inc(moe_pe, 1)
            x_ready.done(pe, 3)
            tiles_T(xn, pe_xt)
            pe.wait_ge(moe_act, 1)
            xf_ready.done(pe, 2)
            for b in range(B):
                i = nc.tensor.matmul(bank["s"][:, b * E:(b + 1) * E], xfT[:, b, :], wgT[:, :], start=True, stop=True)
            i.then_inc(moe_pe, 1)
            pe.wait_ge(moe_dve, 1)
            h_banks = ("qk", "v", "s", "pt", "ot")

            def hidden(t, r):
                m_cur.done(pe, t)
                m_silu.free(pe, t, 1)
                m_u.free(pe, t, 1)
                for c in range(E // 4):
                    nc.tensor.matmul(bank[h_banks[c]][:, :], xcur[:, r, :], mw1[:, 4 * c:4 * c + 4, :], start=True, stop=True)
                nc.tensor.matmul(bank[h_banks[-1]][:, 0:4 * HE], xcur[:, r, :], ws1[:, :], start=True, stop=True).then_inc(m_h.sem, 1)

            def project(t, r):
                m_w.done(pe, t)
                for c in range(3):
                    n = t * 3 + c
                    bk = ("f0", "f1")[c % 2] if r == 0 else ("f1", "f0")[c % 2]
                    m_ev.free(pe, n, 2)
                    for j in range(4 if c < 2 else 1):
                        k = 4 * c + j
                        i = nc.tensor.transpose(by_head[bk][:, j, :], mh[:, r, k // 2, 128 * (k % 2):128 * (k % 2) + 128], ident)
                    i.then_inc(m_T.sem, 1)
                m_out.free(pe, t, 1)
                for c in range(3):
                    m_ev.done(pe, t * 3 + c)
                    for k in range(4 * c, min(4 * c + 4, 9)):
                        i = nc.tensor.matmul(bank["qkt"][:, 0:D], mhT[:, r, k, :], mw2[:, k, :] if k < 8 else ws2[:, :],
                                             start=(k == 0), stop=(k == 8))
                i.then_inc(m_y.sem, 1)

            hidden(0, 0)
            with pe.Fori(0, B // 2 - 1) as p:
                hidden(p * 2 + 1, 1)
                project(p * 2, 0)
                hidden(p * 2 + 2, 0)
                project(p * 2 + 1, 1)
            hidden(B - 1, 1)
            project(B - 2, 0)
            project(B - 1, 1)

        @block.scalar
        def _(act):
            for s in (act_qk, act_T, act_v, act_exp, act_PT, act_OT, m_silu, m_ev):
                act.sem_inc(s.sem, s.credit)

            def copy(dst, src, **kw):
                return nc.scalar.activation(dst, src, ACT.Copy, **kw)

            def tiles_out(first):
                for h, bk in enumerate(("f0", "f1")):
                    pe_xt.done(act, first + h)
                    i = copy(xfT[:, 4 * h:4 * h + 4, :], by_head[bk])
                i.then_inc(xf_ready.sem, 1)

            def shifted_out(half, n, bk):
                pe_xh.done(act, n)
                dst = xT[:, 4 * half:4 * half + 4, :]
                copy(dst[0:D // 2], by_head[bk][0:D // 2])
                copy(dst[D // 2:D, :, 1:T], by_head[bk][D // 2:D, :, 0:T - 1]).then_inc(xh_ready.sem, 1)

            act.wait_ge(in_sim, 16 * 7)
            nc.scalar.activation(tg[:, :], gates[:, :], ACT.Tanh).then_inc(sim_act, 1)
            act.wait_ge(sim_pe, 1)
            copy(wvT[:, :], bank["v"][:, 0:HSIM])
            copy(wtT[:, :], bank["v"][0:DC, HSIM:2 * HSIM])
            copy(lpar_all[:, :, :], bank["v"][:, 128:128 + NP * DEPTH].rearrange("p (k l) -> p k l", k=NP))
            copy(cT[:, 0:4, :], by_head["s"][0:DC])
            copy(cT[:, 4:8, :], by_head["pt"][0:DC]).then_inc(sim_act, 1)
            tiles_out(0)
            act.wait_ge(sim_pe, 2)
            for h, (vb, tb) in enumerate((("qk", "s"), ("v", "pt"))):
                nc.scalar.activation(vT[:, 512 * h:512 * h + 512], bank[vb][0:HSIM, :], ACT.Identity, bias=bvt[:, 0:1])
                nc.scalar.activation(tT[:, 512 * h:512 * h + 512], bank[tb][0:HSIM, :], ACT.Identity, bias=bvt[:, 1:2])
                nc.scalar.activation(vsq[:, 512 * h:512 * h + 512], bank[vb][0:HSIM, :], ACT.Square, bias=bvt[:, 0:1]).then_inc(sim_act, 1)
                nc.scalar.activation(tsq[:, 512 * h:512 * h + 512], bank[tb][0:HSIM, :], ACT.Square, bias=bvt[:, 1:2]).then_inc(sim_act, 1)
            act.wait_ge(sim_dve, 2)
            nc.scalar.activation(den[:, :, :], den[:, :, :], ACT.Sqrt).then_inc(sim_act, 1)

            def stages(window):
                def run(base, l, b0, s, on, last):
                    seq0, half_f = l * B + b0, ffn_step(window, s)
                    half, f = half_f
                    unit = l * 2 + half if half is not None else None

                    if on(0):
                        g, r = base + s, s % 2
                        pe_qk.done(act, g)
                        if window:
                            dve_n2.free(act, g, 2)
                            nc.scalar.activation(sq[:, r, :], bank["qk"][:, :], ACT.Square).then_inc(act_qk.sem, 1)
                        else:
                            pe_T.free(act, g, 2)
                            copy(q_n[:, r, :], bank["qk"][:, 0:GW], scale=DH ** -0.5).then_inc(act_qk.sem, 1)
                    if f == 4:
                        lpar_ready.done(act, l)
                        pe_nt.done(act, unit)
                        nc.scalar.activation(xfT[:, 0:4, :], by_head["f1"], ACT.Identity,
                                             scale=lpar[:, 0:1], bias=lpar[:, 1:2]).then_inc(act_nt.sem, 1)
                    if on(7):
                        g, gi, bs = base + s - 7, (s - 7) % GPB, (s - 7) // GPB
                        pe_PV.done(act, g)
                        if gi == 0:
                            pe_Y.free(act, seq0 + bs, 2)
                        copy(oT[:, bs % 2, 2 * gi:2 * gi + 2, :], by_head["ot"][:, 0:2, :]).then_inc(act_OT.sem, 1)
                    if on(1):
                        g = base + s - 1
                        pe_v.done(act, g)
                        copy(v_n[:, (s - 1) % UNROLL, :], bank["v"][:, 0:GW]).then_inc(act_v.sem, 1)
                    lag = 3 if window else 2
                    if on(lag):
                        g, r = base + s - lag, (s - lag) % 2
                        pe_T.done(act, g)
                        pe_S.free(act, g, 2)
                        copy(kT[0:DH, r, 0:HG:2, :], by_head["qkt"][0:DH, 0:2, :])
                        copy(kT[DH:2 * DH, r, 1:HG:2, :], by_head["qkt"][DH:2 * DH, 0:2, :])
                        copy(qT[:, r], by_head["qkt"][:, 2:4, :]).then_inc(act_T.sem, 1)
                    if f == 9 and not last:
                        shifted_out(half, unit + 2, "f1")
                    if on(4):
                        g, r = base + s - 4, (s - 4) % 2
                        dve_max.done(act, g)
                        pe_PT.free(act, g, 2)
                        for h in range(HG):
                            i = nc.scalar.activation(probs[:, r, h, :], by_head["s"][:, h, :], ACT.Exp, bias=negm[:, r, h:h + 1],
                                                     accum_out=sums[:, r, h:h + 1])
                        i.then_inc(act_exp.sem, 1)
                    if f == 4:
                        pe_gate.done(act, unit * NF)
                        nc.scalar.activation(gact[0:FCH[-1][1], NF - 1, :], bank["f0"][0:FCH[-1][1], :], ACT.Identity,
                                             bias=lpar[0:FCH[-1][1], 1 + 2 * NF:2 + 2 * NF]).then_inc(act_gate.sem, 1)
                    if on(5):
                        g, r = base + s - 5, (s - 5) % 2
                        pe_PT.done(act, g)
                        pe_PV.free(act, g, 2)
                        copy(pT[:, r], by_head["pt"]).then_inc(act_PT.sem, 1)
                    if f == 5:
                        act_gate.done(act, unit)
                        nc.scalar.activation(gact[0:FCH[-1][1], NF - 1, :], gact[0:FCH[-1][1], NF - 1, :], ACT.Gelu)
                        pe_gate.done(act, unit * NF + 2)
                        for c, bk in ((1, "f1"), (0, "f0")):
                            i = nc.scalar.activation(gact[:, c, :], bank[bk][:, :], ACT.Gelu,
                                                     bias=lpar[:, 2 + NF + c:3 + NF + c])
                        i.then_inc(act_gelu.sem, 1)
                return run

            shifted_out(0, 0, "f0")
            shifted_out(1, 1, "f1")
            local_layers(stages(True))(act)

            tiles_out(2)
            cross_layer(stages(False))(act)

            act.wait_ge(moe_pe, 1)
            copy(wgT[:, :], bank["v"][:, 0:E]).then_inc(moe_act, 1)
            tiles_out(4)
            act.wait_ge(moe_dve, 2)
            nc.scalar.activation(sc[:, :, :], sc[:, :, :], ACT.Exp).then_inc(moe_act, 1)

            def silu(t, r):
                m_h.done(act, t)
                m_u.free(act, t, 2)
                for c in range(E // 4):
                    bk = ("qk", "v", "s", "pt")[c]
                    nc.scalar.activation(sg[:, r, c, :].rearrange("p (e h) -> p e h", h=HE),
                                         bank[bk][:, :].rearrange("p (e u h) -> p e u h", u=2, h=HE)[:, :, 1, :], ACT.Silu)
                nc.scalar.activation(sg[:, r, NCH - 1, 0:2 * HE], bank["ot"][:, 2 * HE:4 * HE], ACT.Silu).then_inc(m_silu.sem, 1)

            def evict(t, r):
                for c in range(3):
                    n = t * 3 + c
                    bk = ("f0", "f1")[c % 2] if r == 0 else ("f1", "f0")[c % 2]
                    k = 4 if c < 2 else 1
                    m_T.done(act, n)
                    if c == 0:
                        m_y.free(act, t, 2)
                    copy(mhT[:, r, 4 * c:4 * c + k, :], by_head[bk][:, 0:k, :]).then_inc(m_ev.sem, 1)

            silu(0, 0)
            with act.Fori(0, B // 2 - 1) as p:
                silu(p * 2 + 1, 1)
                evict(p * 2, 0)
                silu(p * 2 + 2, 0)
                evict(p * 2 + 1, 1)
            silu(B - 1, 1)
            evict(B - 2, 0)
            evict(B - 1, 1)

        @block.vector
        def _(dve):
            for s in (dve_qk, dve_y, dve_n2, m_u, m_out):
                dve.sem_inc(s.sem, s.credit)
            nc.vector.memset(par_rows[:, :], 0.0).then_inc(par_clear, 1)
            nc.vector.memset(ones[:, :], 1.0).then_inc(setup, 1)
            nc.vector.memset(masks[:, 1, :], 0.0)
            nc.vector.memset(xT[D // 2:D, :, 0:1], 0.0)
            dve.wait_ge(in_const, 16)
            nc.vector.tensor_copy(ident_b[:, :], ident)
            nc.vector.tensor_copy(masks[:, 0, :], cst[:, C_MASK:C_MASK + T])
            dve.wait_ge(in_x, 16)
            dve.wait_ge(in_par, PAR)
            layernorm(dve, xn, xbase, 0, x_ready)
            dve.wait_ge(sim_pe, 3)
            nc.vector.tensor_copy(vn2[:, :], bank["qkt"][:, 0:B]).then_inc(sim_dve, 1)
            dve.wait_ge(sim_dve, 1)
            for b in range(B):
                i = nc.vector.tensor_scalar(den[:, b, :], by_head["f0" if b < 4 else "f1"][:, b % 4, :], vn2[:, b:b + 1], 1e-16,
                                            ALU.mult, ALU.max)
            i.then_inc(sim_dve, 1)
            dve.wait_ge(sim_act, 7)
            nc.vector.reciprocal(den[:, :, :], den[:, :, :]).then_inc(sim_dve, 1)
            dve.wait_ge(sim_dve, 3)
            dve.wait_ge(sim_pe, 4)
            for h, bk in enumerate(("ot", "qk")):
                i = nc.vector.tensor_tensor(den[:, 4 * h:4 * h + 4, :], by_head[bk], den[:, 4 * h:4 * h + 4, :], ALU.mult)
            i.then_inc(sim_dve, 1)
            dve.wait_ge(sim_dve, 4)
            nc.vector.scalar_tensor_tensor(out=xbase[:, :, :], in0=den[:, :, :], scalar=tg[:, 0:1], in1=xbase[:, :, :],
                                           op0=ALU.mult, op1=ALU.add).then_inc(sim_dve, 1)
            dve.wait_ge(sim_dve, 5)
            layernorm(dve, xres, xbase, 1, x_ready)

            def stages(window):
                def run(base, l, b0, s, on, last):
                    seq0 = l * B + b0
                    half, f = ffn_step(window, s)
                    unit = l * 2 + half if half is not None else None

                    def norms(lag, *ks):
                        if not (window and on(lag)):
                            return
                        g, r = base + s - lag, (s - lag) % 2
                        at = g * (RS_OPS + 1)
                        for k in ks:
                            if k < 0:
                                dve_n2.done(dve, g)
                                pool_norm.free(dve, g, 2)
                                nc.vector.tensor_scalar(n2[:, r, :], n2[:, r, :], 1e-24, None, ALU.max).then_inc(dve_rn, 1)
                            else:
                                if k == 0:
                                    dve.wait_ge(dve_rn, at + 1)
                                rsqrt_step(dve, k, rn[:, r, :], n2[:, r, :], nt[:, :], dve_rn, at + 1)

                    def norm_ffn(*ks):
                        for k in ks:
                            layernorm_step(dve, k, xn, xsh, 4, unit + 2, xn_ready)

                    def ffn(p):
                        if f is None:
                            return
                        if (f, p) == (0, 6):
                            dve_y.done(dve, l * B + half * 4 + 3)
                            nc.vector.tensor_copy(xsh[:, :, 0:D // 2], xres[:, 4 * half:4 * half + 4, 0:D // 2])
                            pe_sh.done(dve, unit)
                            nc.vector.tensor_copy(xsh[:, :, D // 2:D], bank["f0"][:, 0:4 * D // 2].rearrange(
                                "p (b d) -> p b d", b=4)).then_inc(dve_sh.sem, 1)
                        for k, place in enumerate(((0, 6), (1, 0), (1, 1), (1, 2), (1, 3), (1, 4), (1, 5), (1, 6), (2, 0), (2, 1), (2, 2), (2, 3), (2, 4), (2, 5), (2, 6), (3, 0))):
                            if (f, p) == place:
                                if k == 0:
                                    dve_sh.done(dve, unit)
                                norm_ffn(k)
                        for c, place in enumerate(((6, 6), (7, 0), (7, 6))):
                            if (f, p) == place:
                                fn = FCH[c][1]
                                act_gelu.done(dve, unit)
                                pe_a.done(dve, unit * NF + c)
                                nc.vector.scalar_tensor_tensor(out=hT[0:fn, c, :], in0=bank["f1" if c == 1 else "f0"][0:fn, :],
                                                               scalar=lpar[0:fn, 2 + c:3 + c], in1=gact[0:fn, c, :],
                                                               op0=ALU.add, op1=ALU.mult).then_inc(dve_h.sem, 1)
                        if f == 8 and p == 6:
                            pool_b2.done(dve, unit)
                            pe_f.done(dve, unit)
                            xb = xres[:, 4 * half:4 * half + 4, :]
                            nc.vector.tensor_tensor(xb, by_head["f0"], xb, ALU.add).then_inc(x_half.sem, 1)

                    def maxima():
                        if on(4):
                            g, r = base + s - 4, (s - 4) % 2
                            pe_S.done(dve, g)
                            act_exp.free(dve, g, 2)
                            nc.vector.tensor_reduce(negm[:, r, :], by_head["s"], AX.X, ALU.max, negate=True).then_inc(dve_max.sem, 1)

                    ffn(0)
                    if on(0):
                        g, r = base + s, s % 2
                        pe_qk.done(dve, g)
                        act_qk.done(dve, g)
                        if window:
                            if s % GPL == 0:
                                tab_ready.done(dve, l + s // GPL)
                            pool_add.free(dve, g, 2)
                            qk = bank["qk"][:, :].rearrange("p (m h d) -> p m h d", m=2, d=DH)
                            ra = rot_a[:, r, :].rearrange("p (m h d) -> p m h d", m=2, d=DH)
                            rb = rot_b[:, r, :].rearrange("p (m h d) -> p m h d", m=2, d=DH)
                            H = DH // 2

                            def table(t, a, b):
                                return t[:, :, a:b].unsqueeze(2).to_broadcast([T, 2, HG, b - a])

                            nc.vector.tensor_tensor(ra, qk, table(tab_cos, 0, DH), ALU.mult)
                            norms(1, 7)
                            ffn(1)
                            maxima()
                            norms(1, 8)
                            nc.vector.tensor_tensor(rb[:, :, :, 0:H], qk[:, :, :, H:DH], table(tab_sin, 0, H), ALU.mult)
                            norms(1, 9)
                            ffn(2)
                            nc.vector.tensor_tensor(rb[:, :, :, H:DH], qk[:, :, :, 0:H], table(tab_sin, H, DH),
                                                    ALU.mult).then_inc(dve_qk.sem, 1)
                        else:
                            pe_T.free(dve, g, 2)
                            nc.vector.tensor_copy(k_n[:, r, :], bank["qk"][:, GW:2 * GW]).then_inc(dve_qk.sem, 1)
                            maxima()
                    else:
                        norms(1, 7, 8, 9)
                        ffn(1)
                        maxima()
                        ffn(2)
                    ffn(3)
                    if on(7) and (s - 7) % GPB == GPB - 1:
                        bs = (s - 7) // GPB
                        pe_Y.done(dve, seq0 + bs)
                        xb = (xres if window else xbase)[:, b0 + bs % B, :]
                        y = bank["f1" if f in (4, 8) else "f0"][:, 0:D]
                        if window:
                            i = nc.vector.tensor_tensor(xb, y, xb, ALU.add)
                        else:
                            i = nc.vector.scalar_tensor_tensor(out=xb, in0=y, scalar=tg[:, 1:2], in1=xb,
                                                               op0=ALU.mult, op1=ALU.add)
                        i.then_inc(dve_y.sem, 1)
                    if on(0) and window:
                        r = s % 2
                        nc.vector.tensor_reduce(n2[:, r, :], sq[:, r, :].rearrange("p (h d) -> p h d", d=DH), AX.X,
                                                ALU.add).then_inc(dve_n2.sem, 1)
                    ffn(4)
                    norms(0, -1, 0)
                    ffn(7)
                    norms(0, 1)
                    ffn(8)
                    ffn(5)
                    if on(4):
                        g, r = base + s - 4, (s - 4) % 2
                        act_exp.done(dve, g)
                        nc.vector.reciprocal(rsum[:, r, :], sums[:, r, :]).then_inc(dve_rs.sem, 1)
                    for k in range(2, 7):
                        norms(0, k)
                        ffn(k + 7)
                    ffn(6)
                return run

            local_layers(stages(True))(dve)
            for h in range(2):
                x_half.done(dve, (DEPTH - 1) * 2 + h)
            nc.vector.scalar_tensor_tensor(out=xbase[:, :, :], in0=xres[:, :, :], scalar=tg[:, 2:3], in1=xbase[:, :, :],
                                           op0=ALU.mult, op1=ALU.add).then_inc(sim_dve, 1)
            dve.wait_ge(sim_dve, 6)
            layernorm(dve, xn, xbase, DEPTH * 2 + 2, x_ready)
            for b in range(B):
                i = nc.vector.scalar_tensor_tensor(out=xbase[:, b, :], in0=bo_b[:, :], scalar=tg[:, 1:2], in1=xbase[:, b, :],
                                                   op0=ALU.mult, op1=ALU.add)
            i.then_inc(sim_dve, 1)
            dve.wait_ge(sim_dve, 7)
            cross_layer(stages(False))(dve)
            dve_y.done(dve, (DEPTH + 1) * B - 1)
            layernorm(dve, xn, xbase, DEPTH * 2 + 3, x_ready)

            dve.wait_ge(moe_pe, 2)
            nc.vector.tensor_copy(sc[:, :, :], bank["s"][:, 0:B * E].rearrange("p (b e) -> p b e", e=E)).then_inc(moe_dve, 1)
            n = 1
            dve.wait_ge(moe_dve, n)
            nc.vector.tensor_reduce(scm[:, :], sc[:, :, :], AX.X, ALU.max).then_inc(moe_self, 1)
            dve.wait_ge(moe_self, 1)
            nc.vector.tensor_tensor(sc[:, :, :], sc[:, :, :], scm[:, :].unsqueeze(2).to_broadcast([T, B, E]),
                                    ALU.subtract).then_inc(moe_dve, 1)
            dve.wait_ge(moe_act, 2)
            nc.vector.tensor_reduce(scs[:, :], sc[:, :, :], AX.X, ALU.add).then_inc(moe_self, 1)
            dve.wait_ge(moe_self, 2)
            nc.vector.reciprocal(scm[:, :], scs[:, :]).then_inc(moe_self, 1)
            dve.wait_ge(moe_self, 3)
            nc.vector.tensor_tensor(sc[:, :, :], sc[:, :, :], scm[:, :].unsqueeze(2).to_broadcast([T, B, E]),
                                    ALU.mult).then_inc(moe_self, 1)
            dve.wait_ge(moe_self, 4)
            for b in range(B):
                i = nc.vector.max(top[:, b, :], sc[:, b, :])
            i.then_inc(moe_self, 1)
            dve.wait_ge(moe_self, 5)
            for b in range(B):
                i = nc.vector.max_index(tidx[:, b, :], top[:, b, :], sc[:, b, :])
            i.then_inc(moe_self, 1)
            dve.wait_ge(moe_self, 6)
            nc.vector.tensor_copy(tidf[:, :, :], tidx[:, :, 0:2]).then_inc(moe_self, 1)
            dve.wait_ge(moe_self, 7)
            experts = cst[:, C_IOTA:C_IOTA + E].unsqueeze(1).to_broadcast([T, B, E])
            for k, hot in enumerate((cw, sc2)):
                i = nc.vector.tensor_tensor(hot[:, :, :], experts, tidf[:, :, k:k + 1].to_broadcast([T, B, E]), ALU.is_equal)
            i.then_inc(moe_self, 1)
            dve.wait_ge(moe_self, 8)
            nc.vector.tensor_tensor(cw[:, :, :], cw[:, :, :], sc2[:, :, :], ALU.add).then_inc(moe_self, 1)
            dve.wait_ge(moe_self, 9)
            nc.vector.tensor_tensor(cw[:, :, :], cw[:, :, :], sc[:, :, :], ALU.mult).then_inc(moe_dve, 1)

            def gated(t, r):
                m_silu.done(dve, t)
                m_T.free(dve, t * 3 + 2, 6)
                for c in range(E // 4):
                    bk = ("qk", "v", "s", "pt")[c]
                    nc.vector.tensor_tensor(mh[:, r, c, :].rearrange("p (e h) -> p e h", h=HE),
                                            bank[bk][:, :].rearrange("p (e u h) -> p e u h", u=2, h=HE)[:, :, 0, :],
                                            sg[:, r, c, :].rearrange("p (e h) -> p e h", h=HE), ALU.mult)
                nc.vector.tensor_tensor(mh[:, r, NCH - 1, 0:2 * HE], bank["ot"][:, 0:2 * HE], sg[:, r, NCH - 1, 0:2 * HE],
                                        ALU.mult).then_inc(m_u.sem, 1)

            def add_out(t):
                m_y.done(dve, t)
                xb = xbase[:, t, :]
                nc.vector.scalar_tensor_tensor(out=xb, in0=bank["qkt"][:, 0:D], scalar=tg[:, 3:4], in1=xb,
                                               op0=ALU.mult, op1=ALU.add).then_inc(m_out.sem, 1)

            gated(0, 0)
            with dve.Fori(0, B // 2 - 1) as p:
                gated(p * 2 + 1, 1)
                add_out(p * 2)
                gated(p * 2 + 2, 0)
                add_out(p * 2 + 1)
            gated(B - 1, 1)
            add_out(B - 2)
            add_out(B - 1)

        @block.gpsimd
        def _(pool):
            for s in (pool_add, pool_norm):
                pool.sem_inc(s.sem, s.credit)
            nc.gpsimd.memset(kT[:, :, :, :], 0.0)
            pool.wait_ge(in_const, 16)
            pool.wait_ge(in_par, PAR)

            def stage(b, r):
                nc.gpsimd.tensor_copy(xcur[:, r, :], xfT[:, b, :])
                nc.gpsimd.tensor_copy(ccur[:, r, :], cT[:, b, :]).then_inc(pool_cur.sem, 1)

            def tables(l):
                H = DH // 2
                nc.gpsimd.tensor_tensor(tab_cos[:, :, :], cst[:, C_COS:C_COS + 2 * DH].rearrange("p (m d) -> p m d", m=2),
                                        scales[:, l, :, :], ALU.mult)
                sin = cst[:, C_SIN:C_SIN + 2 * DH].rearrange("p (m d) -> p m d", m=2)
                nc.gpsimd.tensor_tensor(tab_sin[:, :, 0:H], sin[:, :, 0:H], scales[:, l, :, H:DH], ALU.mult)
                nc.gpsimd.tensor_tensor(tab_sin[:, :, H:DH], sin[:, :, H:DH], scales[:, l, :, 0:H], ALU.mult).then_inc(tab_ready.sem, 1)

            def stages(window):
                def run(base, l, b0, s, on, last):
                    half, f = ffn_step(window, s)
                    unit = l * 2 + half if half is not None else None
                    if on(1) and window:
                        g, r = base + s - 1, (s - 1) % 2
                        pool.wait_ge(dve_rn, (g + 1) * (RS_OPS + 1))
                        pool_add.done(pool, g)
                        pe_T.free(pool, g, 2)
                        u = rot[:, :].rearrange("p (m h d) -> p m h d", m=2, d=DH)
                        n = rn[:, r, :].rearrange("p (m h) -> p m h", m=2).unsqueeze(3).to_broadcast([T, 2, HG, DH])
                        nc.gpsimd.tensor_tensor(q_n[:, r, :].rearrange("p (h d) -> p h d", d=DH), u[:, 0], n[:, 0], ALU.mult)
                        nc.gpsimd.tensor_tensor(k_n[:, r, :].rearrange("p (h d) -> p h d", d=DH), u[:, 1], n[:, 1],
                                                ALU.mult).then_inc(pool_norm.sem, 1)
                    if f == 3:
                        if last:
                            dve_sh.done(pool, unit)
                        xb = xres[:, 4 * half:4 * half + 4, :]
                        nc.gpsimd.tensor_tensor(xb, xb, b2_all[:, l, :].unsqueeze(1).to_broadcast([T, 4, D]),
                                                ALU.add).then_inc(pool_b2.sem, 1)
                    if on(0) and window:
                        g, r = base + s, s % 2
                        dve_qk.done(pool, g)
                        pool_norm.free(pool, g, 1)
                        nc.gpsimd.tensor_tensor(rot[:, :], rot_a[:, r, :], rot_b[:, r, :], ALU.add).then_inc(pool_add.sem, 1)
                        if s == 20:
                            nc.gpsimd.tensor_copy(lpar[:, :], lpar_all[:, :, l]).then_inc(lpar_ready.sem, 1)
                        if s == GPL - 1 and not last:
                            tables(l + 1)
                    if on(4):
                        g, r = base + s - 4, (s - 4) % 2
                        dve_rs.done(pool, g)
                        nc.gpsimd.tensor_tensor(probs[:, r], probs[:, r], rsum[:, r, :].unsqueeze(2).to_broadcast([T, HG, T]),
                                                ALU.mult).then_inc(pool_pn.sem, 1)
                    if not window and (s + 2) % GPB == 0 and s + 2 < GPL:
                        stage(b0 + (s + 2) // GPB, (s + 2) // GPB % 2)
                return run

            tables(0)
            local_layers(stages(True))(pool)
            xf_ready.done(pool, 1)
            stage(0, 0)
            cross_layer(stages(False), first=LAG - 1)(pool)

            def weigh(t, r):
                m_u.done(pool, t)
                nc.gpsimd.tensor_tensor(mh[:, r, 0:E // 4, :].rearrange("p c (e h) -> p (c e) h", h=HE),
                                        mh[:, r, 0:E // 4, :].rearrange("p c (e h) -> p (c e) h", h=HE),
                                        cw[:, t, :].unsqueeze(2).to_broadcast([T, E, HE]), ALU.mult).then_inc(m_w.sem, 1)

            def stage_tile(t, r):
                nc.gpsimd.tensor_copy(xcur[:, r, :], xfT[:, t, :]).then_inc(m_cur.sem, 1)

            xf_ready.done(pool, 2)
            stage_tile(0, 0)
            stage_tile(1, 1)
            pool.wait_ge(moe_dve, 3)
            weigh(0, 0)
            with pool.Fori(0, B // 2 - 1) as p:
                stage_tile(p * 2 + 2, 0)
                weigh(p * 2 + 1, 1)
                stage_tile(p * 2 + 3, 1)
                weigh(p * 2 + 2, 0)
            weigh(B - 1, 1)


_IN = ['x', 'ctx_768', 'g_xattn', 'g_ffn', 'L0_xattn_Wv', 'L0_xattn_bv', 'L0_xattn_Wt', 'L0_xattn_bt', 'L0_ffn_Wqkv',
       'L0_ffn_q_scale', 'L0_ffn_k_scale', 'L0_ffn_Wo', 'L0_ffn_ln_g', 'L0_ffn_ln_b', 'L0_ffn_W1', 'L0_ffn_b1', 'L0_ffn_W2',
       'L0_ffn_b2', 'L1_xattn_Wq', 'L1_xattn_Wk', 'L1_xattn_Wv', 'L1_xattn_Wo', 'L1_xattn_bo', 'L1_ffn_Wg', 'L1_ffn_W1',
       'L1_ffn_W2', 'L1_ffn_Ws1', 'L1_ffn_Ws2']


def kernel(**inputs):
    import concourse.bacc as bacc
    from concourse.bass_utils import run_bass_kernel_spmd

    nc = bacc.Bacc("TRN2", target_bir_lowering=False, num_devices=1)
    arrays = {f"in_{n}": np.ascontiguousarray(inputs[n]) for n in _IN}
    arrays["in_consts"] = shape_constants()
    args = [nc.dram_tensor(n, a.shape, mybir.dt.from_np(a.dtype), kind="ExternalInput").ap() for n, a in arrays.items()]
    res = nc.dram_tensor("out", (B, T, D), F32, kind="ExternalOutput").ap()
    build(nc, *args, res)
    r = run_bass_kernel_spmd(nc, [arrays], core_ids=[0])
    return r.results[0]["out"]
```

```python
from contextlib import ExitStack

import numpy as np

import concourse.bass as bass
from concourse import mybir

ALU = mybir.AluOpType
ACT = mybir.ActivationFunctionType
AX = mybir.AxisListType
F32 = mybir.dt.float32
BF16 = mybir.dt.bfloat16
I32 = mybir.dt.int32

B = 8
T = 128
D = 128
DC = 96
HEADS = 16
DH = 64
INNER = HEADS * DH
WINDOW = 32
DEPTH = 6
DFF = int(D * 4 * 2 / 3)
HSIM = 64
E = 16
HE = 64
HG = 4
GPB = HEADS // HG
GPL = B * GPB
LAG = 7
GAP = 4
UNROLL = 8
GW = HG * DH
FCH = [(c, min(128, DFF - c)) for c in range(0, DFF, 128)]
NF = len(FCH)
NP = 2 + 2 * NF
RSQRT_SEED = float(0x5F3759DF)
RS_OPS = 8
HALLEY = 0.375 ** 0.5
LN_OPS = 5 + RS_OPS
LN_ALONE = {k: (p // 7, p % 7) for k, p in enumerate(range(6, 6 + LN_OPS + 1))}
LN_JOINT = {0: (0, 6), 1: (1, 0), 2: (1, 1), 3: (1, 2), 4: (1, 3), LN_OPS: (2, 4)}
C_ID, C_SH, C_MASK, C_COS, C_SIN, C_IOTA, C_END = 0, 128, 256, 384, 512, 640, 656


def shape_constants():
    c = np.zeros((T, C_END), np.float32)
    c[:, C_ID:C_ID + T] = np.eye(T)
    c[:, C_SH:C_SH + T] = np.eye(T, k=1)
    i, j = np.arange(T)[:, None], np.arange(T)[None, :]
    seen = (j // WINDOW >= i // WINDOW - 1) & (j <= i) & (i <= j + WINDOW)
    c[:, C_MASK:C_MASK + T] = np.where(seen, 0.0, -1e30)
    half = np.arange(0, DH, 2, dtype=np.float32)
    inv = (1.0 / 10000.0 ** (half / DH)).astype(np.float32)
    t = np.arange(T, dtype=np.float32)
    freqs = (t[:, None] * inv[None, :]).astype(np.float32)
    base = ((half + 0.4 * DH) / (1.4 * DH)).astype(np.float32)
    power = ((t - T // 2) / (WINDOW // 2)).astype(np.float32)
    scale = (base[None, :] ** power[:, None]).astype(np.float32)
    cos, sin = np.cos(freqs), np.sin(freqs)
    for n, s in enumerate((8.0 * scale, 1.0 / scale)):
        c[:, C_COS + n * DH:C_COS + (n + 1) * DH] = np.concatenate([cos * s, cos * s], 1)
        c[:, C_SIN + n * DH:C_SIN + (n + 1) * DH] = np.concatenate([-sin * s, sin * s], 1)
    c[:, C_IOTA:C_IOTA + E] = np.arange(E)
    return c


class Steps:

    def __init__(self, sem, credit=0):
        self.sem, self.credit = sem, credit

    def done(self, eng, step):
        eng.wait_ge(self.sem, step + 1 + self.credit)

    def free(self, eng, step, ring):
        assert self.credit >= ring
        eng.wait_ge(self.sem, step + 1 - ring + self.credit)


def build(nc, x, ctx, g_xattn, g_ffn, s_Wv, s_bv, s_Wt, s_bt, Wqkv, q_scale, k_scale, Wo, ln_g, ln_b, W1, b1,
          W2, b2, x_Wq, x_Wk, x_Wv, x_Wo, x_bo, m_Wg, m_W1, m_W2, m_Ws1, m_Ws2, consts, out):
    with ExitStack() as stack:
        def sb(name, shape, dt=F32):
            return stack.enter_context(nc.sbuf_tensor(name, shape, dt))

        def sem(name):
            return stack.enter_context(nc.semaphore(name))

        def steps(name, credit=0):
            return Steps(sem(name), credit)

        cst = sb("cst", [T, C_END])
        ident = cst[:, C_ID:C_ID + T]
        shift = cst[:, C_SH:C_SH + T]
        ident_b = sb("ident_b", [T, T], BF16)
        masks = sb("masks", [T, 2, T], BF16)
        ones = sb("ones", [T, T])
        xbase = sb("xbase", [T, B, D])
        xres = sb("xres", [T, B, D])
        xsh = sb("xsh", [T, B // 2, D])
        xn = sb("xn", [T, B, D])
        xT = sb("xT", [D, B, T])
        xfT = sb("xfT", [D, B, T])
        xcur = sb("xcur", [D, 2, T])
        ctx_sb = sb("ctx_sb", [T, B, DC])
        cT = sb("cT", [DC, B, T])
        gates = sb("gates", [T, 4])
        tg = sb("tg", [T, 4])
        wv_n = sb("wv_n", [HSIM, D])
        wt_n = sb("wt_n", [HSIM, DC])
        wvT = sb("wvT", [D, HSIM])
        wtT = sb("wtT", [DC, HSIM])
        bvt = sb("bvt", [HSIM, 2])
        vT = sb("vT", [HSIM, B * T])
        tT = sb("tT", [HSIM, B * T])
        vsq = sb("vsq", [HSIM, B * T])
        tsq = sb("tsq", [HSIM, B * T])
        vn2 = sb("vn2", [T, B])
        wqkv = sb("wqkv", [D, 2, 3 * INNER])
        wo = sb("wo", [D, INNER // 128, D])
        scales = sb("scales", [T, DEPTH, 2, DH])
        tab_cos = sb("tab_cos", [T, 2, DH])
        tab_sin = sb("tab_sin", [T, 2, DH])
        sq = sb("sq", [T, 2, 512])
        rot_a = sb("rot_a", [T, 2, 512])
        rot_b = sb("rot_b", [T, 2, 512])
        rot = sb("rot", [T, 512])
        n2 = sb("n2", [T, 2, 12])
        nt = sb("nt", [T, 12])
        rn = sb("rn", [T, 2, 12])
        q_n = sb("q_n", [T, 4, GW])
        k_n = sb("k_n", [T, 4, GW])
        qT = sb("qT", [T, 2, 2, T])
        kT = sb("kT", [T, 2, HG, T])
        v_n = sb("v_n", [T, UNROLL, GW])
        negm = sb("negm", [T, 2, HG])
        probs = sb("probs", [T, 2, HG, T])
        sums = sb("sums", [T, 2, HG])
        rsum = sb("rsum", [T, 2, HG])
        pT = sb("pT", [T, 2, HG, T])
        oT = sb("oT", [T, 2, INNER // 128, T])
        w1 = sb("w1", [D, 2 * DFF])
        w2 = sb("w2", [128, NF, D])
        par_rows = sb("par_rows", [NP * DEPTH, 128])
        lpar_all = sb("lpar_all", [D, NP, DEPTH])
        lpar = sb("lpar", [D, NP])
        b2_all = sb("b2_all", [T, DEPTH, D])
        bo_b = sb("bo_b", [T, D])
        stats = sb("stats", [T, B, 6])
        mean = sb("mean", [T, B])
        lvar = sb("lvar", [T, B])
        lt = sb("lt", [T, B])
        lr = sb("lr", [T, B])
        gact = sb("gact", [128, NF, 512])
        hT = sb("hT", [128, NF, 512])
        den = hT[:, 0:2, :].rearrange("p a (b t) -> p (a b) t", t=T)
        wg_n = sb("wg_n", [E, D])
        wgT = sb("wgT", [D, E])
        mw1 = sb("mw1", [D, E, 2 * HE])
        mw2 = sb("mw2", [128, E * HE // 128, D])
        ws1 = sb("ws1", [D, 4 * HE])
        ws2 = sb("ws2", [2 * HE, D])
        sc = sb("sc", [T, B, E])
        scm = sb("scm", [T, B])
        scs = sb("scs", [T, B])
        sc2 = sb("sc2", [T, B, E])
        top = sb("top", [T, B, 8])
        tidx = sb("tidx", [T, B, 8], mybir.dt.uint32)
        tidf = sb("tidf", [T, B, 2])
        cw = sb("cw", [T, B, E])
        NCH = E // 4 + 1
        sg = sb("sg", [T, 2, NCH, 256])
        mh = sb("mh", [T, 2, NCH, 256])
        mhT = sb("mhT", [128, 2, 12, T])

        bank = {n: stack.enter_context(nc.psum_tensor("ps_" + n, [128, 512], F32))
                for n in ("qk", "v", "qkt", "s", "pt", "ot", "f0", "f1")}
        by_head = {n: b[:, :].rearrange("p (h t) -> p h t", t=128) for n, b in bank.items()}

        in_const, in_x, in_sim, in_par, in_moe = (sem("in_" + n) for n in ("const", "x", "sim", "par", "moe"))
        in_qkv, in_wo, in_ffn = sem("in_qkv"), sem("in_wo"), sem("in_ffn")
        out_done = sem("out_done")
        setup, par_clear = sem("setup"), sem("par_clear")
        pe_v, pe_qk, pe_T, pe_S, pe_PT, pe_PV, pe_Y = (
            steps(n, c) for n, c in (("pe_v", 0), ("pe_qk", 2), ("pe_T", 4), ("pe_S", 2), 
                                     ("pe_PT", 2), ("pe_PV", 2), ("pe_Y", 2)))
        act_qk, act_T, act_v, act_exp, act_PT, act_OT = (
            steps(n, c) for n, c in (("act_qk", 1), ("act_T", 1), ("act_v", 1), ("act_exp", 2), ("act_PT", 1), ("act_OT", 1)))
        dve_qk, dve_y, dve_n2 = steps("dve_qk", 1), steps("dve_y", 1), steps("dve_n2", 2)
        dve_max, dve_rs, dve_rn = steps("dve_max"), steps("dve_rs"), sem("dve_rn")
        pool_add, pool_norm, pool_pn = steps("pool_add", 2), steps("pool_norm", 2), steps("pool_pn")
        x_ready, pe_xt, xf_ready = steps("x_ready"), steps("pe_xt"), steps("xf_ready")
        tab_ready, lpar_ready = steps("tab_ready"), steps("lpar_ready")
        ln = sem("ln")
        pe_sh, dve_sh, xn_ready, pe_nt, act_nt = (steps(n) for n in ("pe_sh", "dve_sh", "xn_ready", "pe_nt", "act_nt"))
        pe_gate, act_gate, act_gelu, pe_a, dve_h, pe_f, pool_b2, x_half = (steps(n) for n in (
            "pe_gate", "act_gate", "act_gelu", "pe_a", "dve_h", "pe_f", "pool_b2", "x_half"))
        pe_xh, xh_ready = steps("pe_xh"), steps("xh_ready")
        xc_norm, pe_xc, xc_ready, dve_x1 = (steps(n) for n in ("xc_norm", "pe_xc", "xc_ready", "dve_x1"))
        sim_pe, sim_act, sim_dve = sem("sim_pe"), sem("sim_act"), sem("sim_dve")
        moe_pe, moe_act, moe_dve, moe_self = sem("moe_pe"), sem("moe_act"), sem("moe_dve"), sem("moe_self")
        m_cur, m_h, m_silu, m_u, m_w, m_T, m_ev, m_y, m_out = (steps(n, c) for n, c in (
            ("m_cur", 0), ("m_h", 0), ("m_silu", 0), ("m_u", 2 * NCH), ("m_w", 0), ("m_T", 6), ("m_ev", 2), ("m_y", 2),
            ("m_out", 1)))

        block = stack.enter_context(nc.Block())


        def all_layers(run):
            def layers(eng):
                for s in range(GPL // 2):
                    run(0, s, lambda lag, s=s: s - lag if s >= lag else None, False)
                with eng.Fori(0, DEPTH - 1) as l:
                    for s in range(GPL // 2, GPL // 2 + GPL):
                        run(l, s, lambda lag, s=s: s - lag, False)
                for s in range(GPL // 2, 2 * GPL + GAP + LAG):
                    def at(lag, s=s):
                        n = s - lag if s - lag < GPL else s - lag - GAP
                        return None if s - lag >= GPL and not GPL <= n < 2 * GPL else n
                    run(DEPTH - 1, s, at, True)
            return layers

        def ffn_step(s):
            for h in range(2):
                f = s - (GPL // 2 * (h + 1) + LAG - 1)
                if 0 <= f <= GPL // 2 - LAG:
                    return h, f
            return None, None

        def cross_step(s, last):
            for h in range(2):
                c = s - (GPL // 2 * (h + 2) - 1)
                if last and 0 <= c <= GAP:
                    return h, c
            return None, None

        def moe_step(s, last):
            e = s - (2 * GPL - 4)
            return e if last and 0 <= e <= 4 else None

        H_BANKS = ("qk", "v", "s", "pt", "ot")

        def rsqrt_step(dve, k, r, v, t, sig, at):
            def stt(out, in0, scalar, in1, op0):
                return nc.vector.scalar_tensor_tensor(out=out, in0=in0, scalar=scalar, in1=in1, op0=op0, op1=ALU.mult)

            if k:
                dve.wait_ge(sig, at + k)
            if k == 0:
                i = nc.vector.tensor_scalar(r.bitcast(I32), v.bitcast(I32), -0.5, RSQRT_SEED, ALU.mult, ALU.add)
            elif k in (1, 4):
                i = nc.vector.tensor_tensor(t, r, r, ALU.mult)
            elif k == 2:
                i = stt(t, t, -0.5, v, ALU.mult)
            elif k == 3:
                i = stt(r, t, 1.5, r, ALU.add)
            elif k == 5:
                i = stt(t, t, HALLEY, v, ALU.mult)
            elif k == 6:
                i = stt(t, t, -1.25 / HALLEY, t, ALU.add)
            else:
                i = stt(r, t, 1.875, r, ALU.add)
            i.then_inc(sig, 1)

        def layernorm_step(dve, k, dst, src, tiles, at, done, joint=None):
            if k and not (joint is not None and k == LN_OPS):
                dve.wait_ge(ln, at + k)
            if k == 0:
                for b in range(tiles):
                    i = nc.vector.bn_stats(stats[:, b, :], src[:, b, :])
                i.then_inc(ln, 1)
                return
            me, ve, mo, vo = (stats[:, 0:tiles, j] for j in (1, 2, 4, 5))
            m, v, t, r = (z[:, 0:tiles] for z in (mean, lvar, lt, lr))
            v4 = v if joint is None else joint[0]
            r = r if joint is None else joint[1]
            if k == 1:
                nc.vector.tensor_tensor(m, me, mo, ALU.add)
                nc.vector.tensor_tensor(t, me, mo, ALU.subtract)
                nc.vector.tensor_tensor(v, ve, vo, ALU.add).then_inc(ln, 1)
            elif k == 2:
                nc.vector.tensor_scalar(m, m, 0.5, None, ALU.mult)
                nc.vector.tensor_tensor(t, t, t, ALU.mult).then_inc(ln, 1)
            elif k == 3:
                nc.vector.tensor_scalar(t, t, 0.25, 1e-5, ALU.mult, ALU.add).then_inc(ln, 1)
            elif k == 4:
                nc.vector.scalar_tensor_tensor(out=v4, in0=v, scalar=1.0 / D, in1=t, op0=ALU.mult, op1=ALU.add).then_inc(ln, 1)
            elif k < LN_OPS:
                rsqrt_step(dve, k - 5, r, v, t, ln, at + 5)
            else:
                for b in range(tiles):
                    i = nc.vector.tensor_scalar(dst[:, b, :], src[:, b, :], m[:, b:b + 1], r[:, b:b + 1],
                                                ALU.subtract, ALU.mult)
                i.then_inc(done.sem, 1)

        def layernorm(dve, dst, src, at, done):
            for k in range(LN_OPS + 1):
                layernorm_step(dve, k, dst, src, B, at, done)

        LN_FFN = 2 * LN_OPS
        LN_CROSS = (LN_FFN + 5 * (2 * DEPTH - 1), LN_FFN + 5 * (2 * DEPTH - 1) + 2 * LN_OPS)
        LN_LAST = LN_CROSS[0] + LN_OPS
        LN_MOE = LN_CROSS[1] + LN_OPS

        @block.sync
        def _(sp):
            sp.dma_start(cst[:, :], consts).then_inc(in_const, 16)
            sp.dma_start(xbase[:, :, :], x.rearrange("b t d -> t b d")).then_inc(in_x, 16)
            sp.dma_start(ctx_sb[:, :, :], ctx.rearrange("b t d -> t b d")).then_inc(in_sim, 16)
            sp.dma_start(wv_n[:, :], s_Wv).then_inc(in_sim, 16)
            sp.dma_start(wt_n[:, :], s_Wt).then_inc(in_sim, 16)
            sp.dma_start(bvt[:, 0:1], s_bv.rearrange("(h o) -> h o", o=1)).then_inc(in_sim, 16)
            sp.dma_start(bvt[:, 1:2], s_bt.rearrange("(h o) -> h o", o=1)).then_inc(in_sim, 16)
            sp.dma_start(gates[:, 0:2], g_xattn.rearrange("(o n) -> o n", o=1).to_broadcast([T, 2])).then_inc(in_sim, 16)
            sp.dma_start(gates[:, 2:4], g_ffn.rearrange("(o n) -> o n", o=1).to_broadcast([T, 2])).then_inc(in_sim, 16)
            for m in range(3):
                sp.dma_start(wqkv[:, 0, m * INNER:(m + 1) * INNER], Wqkv[0, :, m * INNER:(m + 1) * INNER]).then_inc(in_qkv, 16)
            for m, s in enumerate((q_scale, k_scale)):
                sp.dma_start(scales[:, :, m, :], s.rearrange("(o l) d -> o l d", o=1).to_broadcast([T, DEPTH, DH])).then_inc(in_par, 16)
            sp.dma_start(wo[:, :, :], Wo[0].rearrange("(c p) d -> p c d", p=128)).then_inc(in_wo, 16)

            def load_ffn(l):
                sp.dma_start(w1[:, :], W1[l]).then_inc(in_ffn, 16)
                sp.dma_start(w2[:, 0:NF - 1, :], W2[l, 0:128 * (NF - 1), :].rearrange("(c p) d -> p c d", p=128)).then_inc(in_ffn, 16)
                sp.dma_start(w2[0:FCH[-1][1], NF - 1, :], W2[l, FCH[-1][0]:DFF, :]).then_inc(in_ffn, 16)

            load_ffn(0)
            sp.wait_ge(par_clear, 1)
            for m, s in enumerate((ln_g, ln_b)):
                sp.dma_start(par_rows[m * DEPTH:(m + 1) * DEPTH, :], s).then_inc(in_par, 16)
            for m in range(2):
                for c, (f0, fn) in enumerate(FCH):
                    k = 2 + m * NF + c
                    sp.dma_start(par_rows[k * DEPTH:(k + 1) * DEPTH, 0:fn],
                                 b1[:, m * DFF + f0:m * DFF + f0 + fn]).then_inc(in_par, 16)
            sp.dma_start(b2_all[:, :, :], b2.rearrange("(o l) d -> o l d", o=1).to_broadcast([T, DEPTH, D])).then_inc(in_par, 16)
            sp.dma_start(bo_b[:, :], x_bo.rearrange("(o d) -> o d", o=1).to_broadcast([T, D])).then_inc(in_par, 16)
            sp.dma_start(wg_n[:, :], m_Wg).then_inc(in_moe, 16)
            sp.dma_start(mw1[:, :, :], m_W1.rearrange("e d h -> d e h")).then_inc(in_moe, 16)
            sp.dma_start(mw2[:, :, :], m_W2.rearrange("(c e) h d -> (e h) c d", e=2)).then_inc(in_moe, 16)
            sp.dma_start(ws1[:, :], m_Ws1).then_inc(in_moe, 16)
            sp.dma_start(ws2[:, :], m_Ws2).then_inc(in_moe, 16)
            pe_v.done(sp, 0)
            for m in range(3):
                sp.dma_start(wqkv[:, 1, m * INNER:(m + 1) * INNER], Wqkv[1, :, m * INNER:(m + 1) * INNER]).then_inc(in_qkv, 16)
            with sp.Fori(0, DEPTH - 2) as l:
                pe_v.done(sp, l * GPL + GPL - 1)
                for m in range(3):
                    sp.dma_start(wqkv[:, l % 2, m * INNER:(m + 1) * INNER], Wqkv[l + 2, :, m * INNER:(m + 1) * INNER]).then_inc(in_qkv, 16)
                pe_Y.done(sp, l * B + B - 1)
                sp.dma_start(wo[:, :, :], Wo[l + 1].rearrange("(c p) d -> p c d", p=128)).then_inc(in_wo, 16)
                pe_f.done(sp, l * 2 + 1)
                load_ffn(l + 1)
            pe_v.done(sp, (DEPTH - 1) * GPL - 1)
            sp.dma_start(wqkv[:, 0, 0:INNER], x_Wq).then_inc(in_qkv, 16)
            sp.dma_start(wqkv[0:DC, 0, INNER:2 * INNER], x_Wk).then_inc(in_qkv, 16)
            sp.dma_start(wqkv[0:DC, 0, 2 * INNER:3 * INNER], x_Wv).then_inc(in_qkv, 16)
            pe_Y.done(sp, (DEPTH - 1) * B - 1)
            sp.dma_start(wo[:, :, :], Wo[DEPTH - 1].rearrange("(c p) d -> p c d", p=128)).then_inc(in_wo, 16)
            pe_f.done(sp, (DEPTH - 1) * 2 - 1)
            load_ffn(DEPTH - 1)
            pe_Y.done(sp, DEPTH * B - 1)
            sp.dma_start(wo[:, :, :], x_Wo.rearrange("(c p) d -> p c d", p=128)).then_inc(in_wo, 16)
            m_out.done(sp, B - 1)
            sp.dma_start(out.rearrange("b t d -> t b d"), xbase[:, :, :]).then_inc(out_done, 16)
            sp.wait_ge(out_done, 16)

        PAR = 16 * (4 + 2 * NF + 2)

        @block.tensor
        def _(pe):
            for s in (pe_v, pe_qk, pe_T, pe_S, pe_PT, pe_PV, pe_Y, m_T, m_y):
                if s.credit:
                    pe.sem_inc(s.sem, s.credit)

            def tiles_T(src, done):
                for h, bk in enumerate(("f0", "f1")):
                    for j in range(4):
                        i = nc.tensor.transpose(by_head[bk][:, j, :], src[:, 4 * h + j, :], ident)
                    i.then_inc(done.sem, 1)

            pe.wait_ge(in_const, 16)
            pe.wait_ge(in_sim, 16 * 7)
            nc.tensor.transpose(bank["v"][:, 0:HSIM], wv_n[:, :], ident[0:HSIM, 0:HSIM])
            nc.tensor.transpose(bank["v"][0:DC, HSIM:2 * HSIM], wt_n[:, :], ident[0:HSIM, 0:HSIM])
            for h, bk in enumerate(("s", "pt")):
                for j in range(4):
                    i = nc.tensor.transpose(by_head[bk][0:DC, j, :], ctx_sb[:, 4 * h + j, :], ident)
            i.then_inc(sim_pe, 1)
            pe.wait_ge(sim_act, 2)
            for h, bk in enumerate(("s", "pt")):
                i = nc.tensor.matmul(bank[bk][0:HSIM, :], wtT[:, :], cT[:, 4 * h:4 * h + 4, :], start=True, stop=True)
            i.then_inc(sim_pe, 1)
            x_ready.done(pe, 0)
            tiles_T(xn, pe_xt)
            xf_ready.done(pe, 0)
            for h, bk in enumerate(("qk", "v")):
                i = nc.tensor.matmul(bank[bk][0:HSIM, :], wvT[:, :], xfT[:, 4 * h:4 * h + 4, :], start=True, stop=True)
            i.then_inc(sim_pe, 1)
            pe.wait_ge(sim_act, 4)
            pe.wait_ge(setup, 1)
            for h, bk in enumerate(("f0", "f1")):
                nc.tensor.matmul(bank[bk][:, :], ones[0:HSIM, :], tsq[:, 512 * h:512 * h + 512], start=True, stop=True)
            pe.wait_ge(sim_act, 6)
            for b in range(B):
                i = nc.tensor.matmul(bank["qkt"][:, b:b + 1], vsq[:, b * T:b * T + T], ones[0:HSIM, 0:1], start=True, stop=True)
            i.then_inc(sim_pe, 1)
            for b in range(B):
                i = nc.tensor.matmul(by_head["ot" if b < 4 else "qk"][:, b % 4, :], vT[:, b * T:b * T + T],
                                     tT[:, b * T:b * T + T], start=True, stop=True)
            i.then_inc(sim_pe, 1)

            def stage_step(l, s, at, last):
                base = l * GPL
                n = at(0)
                if n is not None:
                    gi, bs = n % GPB, n // GPB % B
                    crossing = last and n >= GPL
                    x_in = xT[:, bs, :]
                    lhs, rows = (cT[:, bs, :], DC) if crossing else (x_in, D)
                    w = wqkv[:, (l + n // GPL) % 2, :]
                half, f = ffn_step(s)
                unit = l * 2 + half if half is not None else None
                ch, cs = cross_step(s, last)
                ms = moe_step(s, last)

                def gate(c):
                    f0, fn = FCH[c]
                    nc.tensor.matmul(bank["f1" if c == 1 else "f0"][0:fn, :], w1[:, DFF + f0:DFF + f0 + fn],
                                     xfT[:, 0:4, :], start=True, stop=True).then_inc(pe_gate.sem, 1)

                def value(c):
                    f0, fn = FCH[c]
                    nc.tensor.matmul(bank["f1" if c == 1 else "f0"][0:fn, :], w1[:, f0:f0 + fn],
                                     xfT[:, 0:4, :], start=True, stop=True).then_inc(pe_a.sem, 1)

                def down(j):
                    for c, (f0, fn) in enumerate(FCH):
                        i = nc.tensor.matmul(by_head["f0"][:, j, :], hT[0:fn, c, j * T:j * T + T], w2[0:fn, c, :],
                                             start=(c == 0), stop=(c == NF - 1))
                    return i

                if f == 4:
                    xn_ready.done(pe, unit)
                    if last and half:
                        xc_ready.done(pe, 0)
                    else:
                        xh_ready.done(pe, unit + 1)
                    for j in range(4):
                        i = nc.tensor.transpose(by_head["f1"][:, j, :], xn[:, j, :], ident)
                    i.then_inc(pe_nt.sem, 1)
                if f == 5:
                    act_gate.done(pe, unit)
                    gate(0)
                n = at(0)
                if n is not None:
                    g = base + n
                    if n == 0 and not last:
                        pe.wait_ge(in_qkv, 48)
                    if n == GPL - 1:
                        pe.wait_ge(in_qkv, (l + 2) * 48)
                    if n % (GPL // 2) == 0 and not crossing:
                        xh_ready.done(pe, l * 2 + n // (GPL // 2))
                    if n % (GPL // 2) == 0 and crossing:
                        xc_ready.done(pe, n // (GPL // 2) - 2)
                    act_qk.free(pe, g, 1)
                    dve_qk.free(pe, g, 1)
                    nc.tensor.matmul(bank["qk"][:, 0:GW], x_in, w[:, gi * GW:(gi + 1) * GW], start=True, stop=True)
                    nc.tensor.matmul(bank["qk"][:, GW:2 * GW], lhs, w[0:rows, INNER + gi * GW:INNER + (gi + 1) * GW],
                                     start=True, stop=True).then_inc(pe_qk.sem, 1)
                n = at(4)
                if n is not None:
                    g, r = base + n, n % 2
                    act_T.done(pe, g)
                    act_exp.free(pe, g, 1)
                    nc.tensor.matmul(by_head["s"], ident_b[:, :],
                                     masks[:, 1 if last and n >= GPL else 0, :].unsqueeze(1).to_broadcast([T, HG, T]),
                                     start=True, stop=False, skip_group_check=True)
                    for h in range(HG):
                        i = nc.tensor.matmul(by_head["s"][:, h, :], qT[:, r, h // 2, :], kT[:, r, h, :],
                                             start=False, stop=(h == HG - 1), skip_group_check=True)
                    i.then_inc(pe_S.sem, 1)
                n = at(3)
                if n is not None:
                    g, r, r4 = base + n, n % 2, n % 4
                    if not (last and n >= GPL):
                        pool_norm.done(pe, g)
                    else:
                        act_qk.done(pe, g)
                        dve_qk.done(pe, g)
                    act_T.free(pe, g, 1)
                    for p in range(2):
                        nc.tensor.transpose(by_head["qkt"][:, p, :], k_n[:, r4, p * 128:p * 128 + 128], ident)
                    for p in range(2):
                        i = nc.tensor.transpose(by_head["qkt"][:, 2 + p, :], q_n[:, r4, p * 128:p * 128 + 128], ident)
                    i.then_inc(pe_T.sem, 1)
                n = at(7)
                if n is not None and n % GPB == GPB - 1:
                    ys = n // GPB
                    if ys % B == 0:
                        pe.wait_ge(in_wo, (l + ys // B + 1) * 16)
                    act_OT.done(pe, base + n)
                    dve_y.free(pe, l * B + ys, 1)
                    if f == 4:
                        act_nt.done(pe, unit)
                    if f == 8:
                        dve_h.done(pe, unit * NF + 1)
                    if last and s in (GPL + 2, GPL + 2 + GPL // 2):
                        x_half.done(pe, l * 2 + (s - GPL) // (GPL // 2))
                    for c in range(INNER // 128):
                        i = nc.tensor.matmul(bank["f1" if f in (4, 8) else "f0"][:, 0:D], oT[:, ys % 2, c, :], wo[:, c, :],
                                             start=(c == 0), stop=(c == INNER // 128 - 1))
                    i.then_inc(pe_Y.sem, 1)
                n = at(6)
                if n is not None:
                    g, r = base + n, n % 2
                    act_PT.done(pe, g)
                    act_OT.free(pe, g, 1)
                    vs = v_n[:, n % UNROLL, :]
                    for h in range(HG):
                        i = nc.tensor.matmul(by_head["ot"][64 * (h % 2):64 * (h % 2) + 64, h // 2, :],
                                             vs[:, h * DH:(h + 1) * DH], pT[:, r, h, :], start=True, stop=True)
                    i.then_inc(pe_PV.sem, 1)
                if f == 4:
                    pe.wait_ge(in_ffn, (l + 1) * 48)
                    act_nt.done(pe, unit)
                    gate(2)
                if f == 6:
                    act_gelu.done(pe, unit)
                    value(0)
                if f == 7:
                    dve_h.done(pe, unit * NF)
                    value(2)
                if f == 8:
                    dve_h.done(pe, unit * NF + 2)
                    down(0)
                    down(1)
                if f == 9 and not last:
                    x_half.done(pe, unit)
                    dve_y.done(pe, l * B + (s - 1 - LAG) // GPB)
                    for j in range(4):
                        i = nc.tensor.transpose(by_head["f1"][:, j, :], xres[:, 4 * half + j, :], ident)
                    i.then_inc(pe_xh.sem, 1)
                n = at(0)
                if n is not None:
                    g = base + n
                    act_v.free(pe, g, 1)
                    nc.tensor.matmul(bank["v"][:, 0:GW], lhs, w[0:rows, 2 * INNER + gi * GW:2 * INNER + (gi + 1) * GW],
                                     start=True, stop=True).then_inc(pe_v.sem, 1)
                n = at(5)
                if n is not None:
                    g, r = base + n, n % 2
                    pool_pn.done(pe, g)
                    act_PT.free(pe, g, 1)
                    for h in range(HG):
                        i = nc.tensor.transpose(by_head["pt"][:, h, :], probs[:, r, h, :], ident)
                    i.then_inc(pe_PT.sem, 1)
                if f == 0:
                    dve_y.done(pe, l * B + half * 4 + 3)
                    nc.tensor.matmul(bank["f0"][:, 0:4 * D // 2], shift, xres[:, 4 * half:4 * half + 4, D // 2:D],
                                     start=True, stop=True).then_inc(pe_sh.sem, 1)
                if f == 4:
                    if at(LAG) is not None:
                        dve_y.done(pe, l * B + at(LAG) // GPB)
                    gate(1)
                if f == 6:
                    value(1)
                if ms == 3:
                    x_ready.done(pe, 2)
                    for j in range(4):
                        i = nc.tensor.transpose(by_head["f1"][:, j, :], xn[:, j, :], ident)
                    i.then_inc(pe_xt.sem, 1)
                if cs == 3:
                    xc_norm.done(pe, ch)
                    for j in range(4):
                        i = nc.tensor.transpose(by_head["f1"][:, j, :], xn[:, 4 + j, :], ident)
                    i.then_inc(pe_xc.sem, 1)
                if f == 8:
                    down(2)
                    down(3).then_inc(pe_f.sem, 1)

            pe.wait_ge(in_par, PAR)
            nc.tensor.transpose(bank["s"][:, 0:NP * DEPTH], par_rows[:, :], ident[0:NP * DEPTH, 0:NP * DEPTH]).then_inc(sim_pe, 1)
            x_ready.done(pe, 1)
            for h, bk in enumerate(("f0", "f1")):
                for j in range(4):
                    i = nc.tensor.transpose(by_head[bk][:, j, :], xres[:, 4 * h + j, :], ident)
                i.then_inc(pe_xh.sem, 1)
            all_layers(stage_step)(pe)

            pe.wait_ge(in_moe, 16 * 5)
            nc.tensor.transpose(bank["v"][:, 0:E], wg_n[:, :], ident[0:E, 0:E]).then_inc(moe_pe, 1)
            pe.wait_ge(moe_act, 1)

            def scores(h):
                xf_ready.done(pe, 1 + h)
                for b in range(4 * h, 4 * h + 4):
                    i = nc.tensor.matmul(bank["s"][:, b * E:(b + 1) * E], xfT[:, b, :], wgT[:, :], start=True, stop=True)
                return i

            scores(0)
            x_ready.done(pe, 3)
            for j in range(4):
                i = nc.tensor.transpose(by_head["f1"][:, j, :], xn[:, 4 + j, :], ident)
            i.then_inc(pe_xt.sem, 1)
            i = scores(1)
            i.then_inc(moe_pe, 1)
            pe.wait_ge(moe_dve, 1)

            def hidden(t, r, chunks):
                for c in chunks:
                    if c == 0:
                        m_cur.done(pe, t)
                    m_u.free(pe, t * NCH + c, NCH)
                    if c < NCH - 1:
                        i = nc.tensor.matmul(bank[H_BANKS[c]][:, :], xcur[:, r, :], mw1[:, 4 * c:4 * c + 4, :], start=True, stop=True)
                    else:
                        i = nc.tensor.matmul(bank[H_BANKS[c]][:, 0:4 * HE], xcur[:, r, :], ws1[:, :], start=True, stop=True)
                    i.then_inc(m_h.sem, 1)

            def weighted_T(t, r, c):
                if c == 0:
                    m_w.done(pe, t)
                if c == 2:
                    m_u.done(pe, t * NCH + NCH - 1)
                n = t * 3 + c
                bk = ("f0", "f1")[(c + r) % 2]
                m_ev.free(pe, n, 2)
                for j in range(4 if c < 2 else 1):
                    k = 4 * c + j
                    i = nc.tensor.transpose(by_head[bk][:, j, :], mh[:, r, k // 2, 128 * (k % 2):128 * (k % 2) + 128], ident)
                i.then_inc(m_T.sem, 1)

            def output(t, r):
                m_out.free(pe, t, 1)
                for c in range(3):
                    m_ev.done(pe, t * 3 + c)
                    for k in range(4 * c, min(4 * c + 4, 9)):
                        i = nc.tensor.matmul(bank["qkt"][:, 0:D], mhT[:, r, k, :], mw2[:, k, :] if k < 8 else ws2[:, :],
                                             start=(k == 0), stop=(k == 8))
                i.then_inc(m_y.sem, 1)

            def tile_after(t, r):
                hidden(t, r, (0, 1))
                weighted_T(t - 1, 1 - r, 0)
                weighted_T(t - 1, 1 - r, 1)
                hidden(t, r, (2, 3))
                weighted_T(t - 1, 1 - r, 2)
                hidden(t, r, (4,))
                output(t - 1, 1 - r)

            hidden(0, 0, range(NCH))
            with pe.Fori(0, B // 2 - 1) as p:
                tile_after(p * 2 + 1, 1)
                tile_after(p * 2 + 2, 0)
            tile_after(B - 1, 1)
            for c in range(3):
                weighted_T(B - 1, 1, c)
            output(B - 1, 1)

        @block.scalar
        def _(act):
            for s in (act_qk, act_T, act_v, act_exp, act_PT, act_OT, m_ev):
                act.sem_inc(s.sem, s.credit)

            def copy(dst, src, **kw):
                return nc.scalar.activation(dst, src, ACT.Copy, **kw)

            def experts_in(h):
                pe_xt.done(act, 2 + h)
                copy(xfT[:, 4 * h:4 * h + 4, :], by_head["f1"]).then_inc(xf_ready.sem, 1)

            def tiles_out(first):
                for h, bk in enumerate(("f0", "f1")):
                    pe_xt.done(act, first + h)
                    i = copy(xfT[:, 4 * h:4 * h + 4, :], by_head[bk])
                i.then_inc(xf_ready.sem, 1)

            def shifted_out(half, n, bk):
                pe_xh.done(act, n)
                dst = xT[:, 4 * half:4 * half + 4, :]
                copy(dst[0:D // 2], by_head[bk][0:D // 2])
                copy(dst[D // 2:D, :, 1:T], by_head[bk][D // 2:D, :, 0:T - 1]).then_inc(xh_ready.sem, 1)

            act.wait_ge(in_sim, 16 * 7)
            nc.scalar.activation(tg[:, :], gates[:, :], ACT.Tanh).then_inc(sim_act, 1)
            act.wait_ge(sim_pe, 1)
            copy(wvT[:, :], bank["v"][:, 0:HSIM])
            copy(wtT[:, :], bank["v"][0:DC, HSIM:2 * HSIM])
            copy(cT[:, 0:4, :], by_head["s"][0:DC])
            copy(cT[:, 4:8, :], by_head["pt"][0:DC]).then_inc(sim_act, 1)
            act.wait_ge(sim_pe, 2)
            for h, tb in enumerate(("s", "pt")):
                nc.scalar.activation(tT[:, 512 * h:512 * h + 512], bank[tb][0:HSIM, :], ACT.Identity, bias=bvt[:, 1:2])
                nc.scalar.activation(tsq[:, 512 * h:512 * h + 512], bank[tb][0:HSIM, :], ACT.Square, bias=bvt[:, 1:2]).then_inc(sim_act, 1)
            tiles_out(0)
            act.wait_ge(sim_pe, 3)
            for h, vb in enumerate(("qk", "v")):
                nc.scalar.activation(vT[:, 512 * h:512 * h + 512], bank[vb][0:HSIM, :], ACT.Identity, bias=bvt[:, 0:1])
                nc.scalar.activation(vsq[:, 512 * h:512 * h + 512], bank[vb][0:HSIM, :], ACT.Square, bias=bvt[:, 0:1]).then_inc(sim_act, 1)
            act.wait_ge(sim_dve, 2)
            nc.scalar.activation(den[:, :, :], den[:, :, :], ACT.Sqrt).then_inc(sim_act, 1)
            act.wait_ge(sim_pe, 6)
            copy(lpar_all[:, :, :], bank["s"][:, 0:NP * DEPTH].rearrange("p (k l) -> p k l", k=NP)).then_inc(sim_act, 1)

            def stage_step(l, s, at, last):
                base = l * GPL
                half, f = ffn_step(s)
                unit = l * 2 + half if half is not None else None
                ch, cs = cross_step(s, last)
                ms = moe_step(s, last)

                if ms == 4:
                    experts_in(0)
                if cs == 4:
                    pe_xc.done(act, ch)
                    copy(xT[:, 4 * ch:4 * ch + 4, :], by_head["f1"]).then_inc(xc_ready.sem, 1)
                n = at(0)
                if n is not None:
                    g, r = base + n, n % 2
                    pe_qk.done(act, g)
                    if not (last and n >= GPL):
                        dve_n2.free(act, g, 2)
                        nc.scalar.activation(sq[:, r, :], bank["qk"][:, :], ACT.Square).then_inc(act_qk.sem, 1)
                    else:
                        pe_T.free(act, g, 4)
                        copy(q_n[:, n % 4, :], bank["qk"][:, 0:GW], scale=DH ** -0.5).then_inc(act_qk.sem, 1)
                if f == 4:
                    lpar_ready.done(act, l)
                    pe_nt.done(act, unit)
                    nc.scalar.activation(xfT[:, 0:4, :], by_head["f1"], ACT.Identity,
                                         scale=lpar[:, 0:1], bias=lpar[:, 1:2]).then_inc(act_nt.sem, 1)
                n = at(7)
                if n is not None:
                    g, gi, bs = base + n, n % GPB, n // GPB
                    pe_PV.done(act, g)
                    if gi == 0:
                        pe_Y.free(act, l * B + bs, 2)
                    copy(oT[:, bs % 2, 2 * gi:2 * gi + 2, :], by_head["ot"][:, 0:2, :]).then_inc(act_OT.sem, 1)
                n = at(1)
                if n is not None:
                    g = base + n
                    pe_v.done(act, g)
                    copy(v_n[:, n % UNROLL, :], bank["v"][:, 0:GW]).then_inc(act_v.sem, 1)
                n = at(3)
                if n is not None:
                    g, r, r4 = base + n, n % 2, n % 4
                    pe_T.done(act, g)
                    pe_S.free(act, g, 2)
                    copy(kT[0:DH, r, 0:HG:2, :], by_head["qkt"][0:DH, 0:2, :])
                    copy(kT[DH:2 * DH, r, 1:HG:2, :], by_head["qkt"][DH:2 * DH, 0:2, :])
                    copy(qT[:, r], by_head["qkt"][:, 2:4, :]).then_inc(act_T.sem, 1)
                if f == 9 and not last:
                    shifted_out(half, unit + 2, "f1")
                n = at(4)
                if n is not None:
                    g, r = base + n, n % 2
                    dve_max.done(act, g)
                    pe_PT.free(act, g, 2)
                    for h in range(HG):
                        i = nc.scalar.activation(probs[:, r, h, :], by_head["s"][:, h, :], ACT.Exp, bias=negm[:, r, h:h + 1],
                                                 accum_out=sums[:, r, h:h + 1])
                    i.then_inc(act_exp.sem, 1)
                if f == 4:
                    pe_gate.done(act, unit * NF)
                    nc.scalar.activation(gact[0:FCH[-1][1], NF - 1, :], bank["f0"][0:FCH[-1][1], :], ACT.Identity,
                                         bias=lpar[0:FCH[-1][1], 1 + 2 * NF:2 + 2 * NF]).then_inc(act_gate.sem, 1)
                n = at(5)
                if n is not None:
                    g, r = base + n, n % 2
                    pe_PT.done(act, g)
                    pe_PV.free(act, g, 2)
                    copy(pT[:, r], by_head["pt"]).then_inc(act_PT.sem, 1)
                if f == 5:
                    act_gate.done(act, unit)
                    nc.scalar.activation(gact[0:FCH[-1][1], NF - 1, :], gact[0:FCH[-1][1], NF - 1, :], ACT.Gelu)
                    pe_gate.done(act, unit * NF + 2)
                    for c, bk in ((1, "f1"), (0, "f0")):
                        i = nc.scalar.activation(gact[:, c, :], bank[bk][:, :], ACT.Gelu,
                                                 bias=lpar[:, 2 + NF + c:3 + NF + c])
                    i.then_inc(act_gelu.sem, 1)

            shifted_out(0, 0, "f0")
            shifted_out(1, 1, "f1")
            all_layers(stage_step)(act)

            act.wait_ge(moe_pe, 1)
            copy(wgT[:, :], bank["v"][:, 0:E]).then_inc(moe_act, 1)
            experts_in(1)
            act.wait_ge(moe_dve, 2)
            nc.scalar.activation(sc[:, :, :], sc[:, :, :], ACT.Exp).then_inc(moe_act, 1)

            def silu(t, r, chunks):
                for c in chunks:
                    m_h.done(act, t * NCH + c)
                    m_u.free(act, t * NCH + c, 2 * NCH)
                    if c < NCH - 1:
                        i = nc.scalar.activation(sg[:, r, c, :].rearrange("p (e h) -> p e h", h=HE),
                                                 bank[H_BANKS[c]][:, :].rearrange("p (e u h) -> p e u h", u=2, h=HE)[:, :, 1, :],
                                                 ACT.Silu)
                    else:
                        i = nc.scalar.activation(sg[:, r, c, 0:2 * HE], bank[H_BANKS[c]][:, 2 * HE:4 * HE], ACT.Silu)
                    i.then_inc(m_silu.sem, 1)

            def evict(t, r, c):
                bk = ("f0", "f1")[(c + r) % 2]
                k = 4 if c < 2 else 1
                m_T.done(act, t * 3 + c)
                if c == 0:
                    m_y.free(act, t, 2)
                copy(mhT[:, r, 4 * c:4 * c + k, :], by_head[bk][:, 0:k, :]).then_inc(m_ev.sem, 1)

            def tile_after(t, r):
                silu(t, r, (0, 1))
                evict(t - 1, 1 - r, 0)
                evict(t - 1, 1 - r, 1)
                silu(t, r, (2, 3))
                evict(t - 1, 1 - r, 2)
                silu(t, r, (4,))

            silu(0, 0, range(NCH))
            with act.Fori(0, B // 2 - 1) as p:
                tile_after(p * 2 + 1, 1)
                tile_after(p * 2 + 2, 0)
            tile_after(B - 1, 1)
            for c in range(3):
                evict(B - 1, 1, c)

        @block.vector
        def _(dve):
            for s in (dve_qk, dve_y, dve_n2, m_u, m_out):
                dve.sem_inc(s.sem, s.credit)
            nc.vector.memset(par_rows[:, :], 0.0).then_inc(par_clear, 1)
            nc.vector.memset(ones[:, :], 1.0).then_inc(setup, 1)
            nc.vector.memset(masks[:, 1, :], 0.0)
            nc.vector.memset(n2[:, :, :], 1.0)
            nc.vector.memset(xT[D // 2:D, :, 0:1], 0.0)
            dve.wait_ge(in_const, 16)
            nc.vector.tensor_copy(ident_b[:, :], ident)
            nc.vector.tensor_copy(masks[:, 0, :], cst[:, C_MASK:C_MASK + T])
            dve.wait_ge(in_x, 16)
            layernorm(dve, xn, xbase, 0, x_ready)
            dve.wait_ge(sim_pe, 4)
            nc.vector.tensor_copy(vn2[:, :], bank["qkt"][:, 0:B]).then_inc(sim_dve, 1)
            dve.wait_ge(sim_dve, 1)
            for b in range(B):
                i = nc.vector.tensor_scalar(den[:, b, :], by_head["f0" if b < 4 else "f1"][:, b % 4, :], vn2[:, b:b + 1], 1e-16,
                                            ALU.mult, ALU.max)
            i.then_inc(sim_dve, 1)
            dve.wait_ge(sim_act, 7)
            nc.vector.reciprocal(den[:, :, :], den[:, :, :]).then_inc(sim_dve, 1)
            dve.wait_ge(sim_dve, 3)
            dve.wait_ge(sim_pe, 5)
            for h, bk in enumerate(("ot", "qk")):
                i = nc.vector.tensor_tensor(den[:, 4 * h:4 * h + 4, :], by_head[bk], den[:, 4 * h:4 * h + 4, :], ALU.mult)
            i.then_inc(sim_dve, 1)
            dve.wait_ge(sim_dve, 4)
            nc.vector.scalar_tensor_tensor(out=xbase[:, :, :], in0=den[:, :, :], scalar=tg[:, 0:1], in1=xbase[:, :, :],
                                           op0=ALU.mult, op1=ALU.add).then_inc(sim_dve, 1)
            dve.wait_ge(sim_dve, 5)
            layernorm(dve, xres, xbase, LN_OPS, x_ready)
            dve.wait_ge(in_par, PAR)

            def stage_step(l, s, at, last):
                base = l * GPL
                half, f = ffn_step(s)
                unit = l * 2 + half if half is not None else None
                ch, cs = cross_step(s, last)
                ms = moe_step(s, last)

                def norms(lag, *ks):
                    n = at(lag)
                    if n is None or last and n >= GPL:
                        return
                    g, r = base + n, n % 2
                    done = g * (RS_OPS + 1)
                    for k in ks:
                        if k < 0:
                            dve_n2.done(dve, g)
                            pool_norm.free(dve, g, 2)
                            nc.vector.tensor_scalar(n2[:, r, :], n2[:, r, :], 1e-24, None, ALU.max).then_inc(dve_rn, 1)
                        else:
                            if k == 0:
                                dve.wait_ge(dve_rn, done + 1)
                            rsqrt_step(dve, k, rn[:, r, :], n2[:, r, :], nt[:, :], dve_rn, done + 1)

                def norm_ffn(k):
                    if last and half:
                        layernorm_step(dve, k, xn, xsh, 4, LN_LAST, xn_ready)
                        return
                    n = at(f - 1)
                    joint = n2[:, n % 2, 8:12], rn[:, n % 2, 8:12]
                    if k == LN_OPS:
                        dve.wait_ge(dve_rn, (base + n + 1) * (RS_OPS + 1))
                    layernorm_step(dve, k, xn, xsh, 4, LN_FFN + unit * 5, xn_ready, joint)

                def cross_input(p):
                    xb = xbase[:, 4 * ch:4 * ch + 4, :]
                    if (cs, p) == (0, 0):
                        x_half.done(dve, l * 2 + ch)
                        nc.vector.scalar_tensor_tensor(out=xb, in0=xres[:, 4 * ch:4 * ch + 4, :], scalar=tg[:, 2:3],
                                                       in1=xb, op0=ALU.mult, op1=ALU.add).then_inc(dve_x1.sem, 1)
                    k = None
                    if (cs, p) == (0, 4):
                        dve_x1.done(dve, 2 * ch)
                        k = 0
                    elif cs in (1, 2) and p < 7 and 7 * cs - 6 + p < LN_OPS:
                        k = 7 * cs - 6 + p
                    elif (cs, p) == (3, 0):
                        k = LN_OPS
                    if k is not None:
                        layernorm_step(dve, k, xn[:, 4:8, :], xb, 4, LN_CROSS[ch], xc_norm)
                    if (cs, p) == (3, 3):
                        for j in range(4):
                            i = nc.vector.scalar_tensor_tensor(out=xb[:, j, :], in0=bo_b[:, :], scalar=tg[:, 1:2],
                                                               in1=xb[:, j, :], op0=ALU.mult, op1=ALU.add)
                        i.then_inc(dve_x1.sem, 1)

                def ffn(p):
                    if cs is not None:
                        cross_input(p)
                    if ms is not None:
                        k = 0 if (ms, p) == (0, 4) else LN_OPS if (ms, p) == (3, 0) else None
                        if ms in (1, 2) and p < 6:
                            k = 6 * ms - 5 + p
                        if k == 0:
                            dve_y.done(dve, l * B + B + 3)
                        if k is not None:
                            layernorm_step(dve, k, xn, xbase, 4, LN_MOE, x_ready)
                    if f is None:
                        return
                    if (f, p) == (0, 6):
                        dve_y.done(dve, l * B + half * 4 + 3)
                        nc.vector.tensor_copy(xsh[:, :, 0:D // 2], xres[:, 4 * half:4 * half + 4, 0:D // 2])
                        pe_sh.done(dve, unit)
                        nc.vector.tensor_copy(xsh[:, :, D // 2:D], bank["f0"][:, 0:4 * D // 2].rearrange(
                            "p (b d) -> p b d", b=4)).then_inc(dve_sh.sem, 1)
                    places = LN_ALONE if last and half else LN_JOINT
                    for k, place in places.items():
                        if (f, p) == place:
                            if k == 0:
                                dve_sh.done(dve, unit)
                            norm_ffn(k)
                    for c, place in enumerate(((6, 6), (7, 0), (7, 6))):
                        if (f, p) == place:
                            fn = FCH[c][1]
                            act_gelu.done(dve, unit)
                            pe_a.done(dve, unit * NF + c)
                            nc.vector.scalar_tensor_tensor(out=hT[0:fn, c, :], in0=bank["f1" if c == 1 else "f0"][0:fn, :],
                                                           scalar=lpar[0:fn, 2 + c:3 + c], in1=gact[0:fn, c, :],
                                                           op0=ALU.add, op1=ALU.mult).then_inc(dve_h.sem, 1)
                    if f == 8 and p == 6:
                        pool_b2.done(dve, unit)
                        pe_f.done(dve, unit)
                        xb = xres[:, 4 * half:4 * half + 4, :]
                        nc.vector.tensor_tensor(xb, by_head["f0"], xb, ALU.add).then_inc(x_half.sem, 1)

                def maxima():
                    n = at(4)
                    if n is not None:
                        g, r = base + n, n % 2
                        pe_S.done(dve, g)
                        act_exp.free(dve, g, 2)
                        nc.vector.tensor_reduce(negm[:, r, :], by_head["s"], AX.X, ALU.max, negate=True).then_inc(dve_max.sem, 1)

                ffn(0)
                n = at(0)
                if n is not None:
                    g, r = base + n, n % 2
                    pe_qk.done(dve, g)
                    act_qk.done(dve, g)
                    if not (last and n >= GPL):
                        if n % GPL == 0:
                            tab_ready.done(dve, l + n // GPL)
                        pool_add.free(dve, g, 2)
                        qk = bank["qk"][:, :].rearrange("p (m h d) -> p m h d", m=2, d=DH)
                        ra = rot_a[:, r, :].rearrange("p (m h d) -> p m h d", m=2, d=DH)
                        rb = rot_b[:, r, :].rearrange("p (m h d) -> p m h d", m=2, d=DH)
                        H = DH // 2

                        def table(t, a, b):
                            return t[:, :, a:b].unsqueeze(2).to_broadcast([T, 2, HG, b - a])

                        nc.vector.tensor_tensor(ra, qk, table(tab_cos, 0, DH), ALU.mult)
                        norms(1, 5)
                        ffn(1)
                        maxima()
                        norms(1, 6)
                        nc.vector.tensor_tensor(rb[:, :, :, 0:H], qk[:, :, :, H:DH], table(tab_sin, 0, H), ALU.mult)
                        norms(1, 7)
                        ffn(2)
                        nc.vector.tensor_tensor(rb[:, :, :, H:DH], qk[:, :, :, 0:H], table(tab_sin, H, DH),
                                                ALU.mult).then_inc(dve_qk.sem, 1)
                    else:
                        pe_T.free(dve, g, 4)
                        nc.vector.tensor_copy(k_n[:, n % 4, :], bank["qk"][:, GW:2 * GW]).then_inc(dve_qk.sem, 1)
                        norms(1, 5, 6, 7)
                        ffn(1)
                        maxima()
                        ffn(2)
                else:
                    norms(1, 5, 6, 7)
                    ffn(1)
                    maxima()
                    ffn(2)
                ffn(3)
                n = at(7)
                if n is not None and n % GPB == GPB - 1:
                    bs = n // GPB
                    pe_Y.done(dve, l * B + bs)
                    y = bank["f1" if f in (4, 8) else "f0"][:, 0:D]
                    if last and n >= GPL:
                        if n % (GPL // 2) == GPB - 1:
                            dve_x1.done(dve, 2 * (bs % B // 4) + 1)
                        xb = xbase[:, bs % B, :]
                        i = nc.vector.scalar_tensor_tensor(out=xb, in0=y, scalar=tg[:, 1:2], in1=xb,
                                                           op0=ALU.mult, op1=ALU.add)
                    else:
                        xb = xres[:, bs % B, :]
                        i = nc.vector.tensor_tensor(xb, y, xb, ALU.add)
                    i.then_inc(dve_y.sem, 1)
                n = at(0)
                if n is not None and not (last and n >= GPL):
                    r = n % 2
                    nc.vector.tensor_reduce(n2[:, r, 0:8], sq[:, r, :].rearrange("p (h d) -> p h d", d=DH), AX.X,
                                            ALU.add).then_inc(dve_n2.sem, 1)
                ffn(4)
                norms(0, -1, 0, 1)
                ffn(5)
                n = at(4)
                if n is not None:
                    g, r = base + n, n % 2
                    act_exp.done(dve, g)
                    nc.vector.reciprocal(rsum[:, r, :], sums[:, r, :]).then_inc(dve_rs.sem, 1)
                norms(0, 2, 3, 4)
                ffn(6)

            all_layers(stage_step)(dve)
            dve_y.done(dve, (DEPTH + 1) * B - 1)
            for k in range(LN_OPS + 1):
                layernorm_step(dve, k, xn[:, 4:8, :], xbase[:, 4:8, :], 4, LN_MOE + LN_OPS, x_ready)

            dve.wait_ge(moe_pe, 2)
            nc.vector.tensor_copy(sc[:, :, :], bank["s"][:, 0:B * E].rearrange("p (b e) -> p b e", e=E)).then_inc(moe_dve, 1)
            n = 1
            dve.wait_ge(moe_dve, n)
            nc.vector.tensor_reduce(scm[:, :], sc[:, :, :], AX.X, ALU.max).then_inc(moe_self, 1)
            dve.wait_ge(moe_self, 1)
            nc.vector.tensor_tensor(sc[:, :, :], sc[:, :, :], scm[:, :].unsqueeze(2).to_broadcast([T, B, E]),
                                    ALU.subtract).then_inc(moe_dve, 1)
            dve.wait_ge(moe_act, 2)
            nc.vector.tensor_reduce(scs[:, :], sc[:, :, :], AX.X, ALU.add).then_inc(moe_self, 1)
            dve.wait_ge(moe_self, 2)
            nc.vector.reciprocal(scm[:, :], scs[:, :]).then_inc(moe_self, 1)
            dve.wait_ge(moe_self, 3)
            nc.vector.tensor_tensor(sc[:, :, :], sc[:, :, :], scm[:, :].unsqueeze(2).to_broadcast([T, B, E]),
                                    ALU.mult).then_inc(moe_self, 1)
            dve.wait_ge(moe_self, 4)
            for b in range(B):
                i = nc.vector.max(top[:, b, :], sc[:, b, :])
            i.then_inc(moe_self, 1)
            dve.wait_ge(moe_self, 5)
            for b in range(B):
                i = nc.vector.max_index(tidx[:, b, :], top[:, b, :], sc[:, b, :])
            i.then_inc(moe_self, 1)
            dve.wait_ge(moe_self, 6)
            nc.vector.tensor_copy(tidf[:, :, :], tidx[:, :, 0:2]).then_inc(moe_self, 1)
            dve.wait_ge(moe_self, 7)
            experts = cst[:, C_IOTA:C_IOTA + E].unsqueeze(1).to_broadcast([T, B, E])
            for k, hot in enumerate((cw, sc2)):
                i = nc.vector.tensor_tensor(hot[:, :, :], experts, tidf[:, :, k:k + 1].to_broadcast([T, B, E]), ALU.is_equal)
            i.then_inc(moe_self, 1)
            dve.wait_ge(moe_self, 8)
            nc.vector.tensor_tensor(cw[:, :, :], cw[:, :, :], sc2[:, :, :], ALU.add).then_inc(moe_self, 1)
            dve.wait_ge(moe_self, 9)
            nc.vector.tensor_tensor(cw[:, :, :], cw[:, :, :], sc[:, :, :], ALU.mult).then_inc(moe_dve, 1)

            def gated(t, r):
                m_T.free(dve, t * 3 + 2, 6)
                for c in range(NCH):
                    m_silu.done(dve, t * NCH + c)
                    if c < NCH - 1:
                        i = nc.vector.tensor_tensor(mh[:, r, c, :].rearrange("p (e h) -> p e h", h=HE),
                                                    bank[H_BANKS[c]][:, :].rearrange("p (e u h) -> p e u h", u=2, h=HE)[:, :, 0, :],
                                                    sg[:, r, c, :].rearrange("p (e h) -> p e h", h=HE), ALU.mult)
                    else:
                        i = nc.vector.tensor_tensor(mh[:, r, c, 0:2 * HE], bank[H_BANKS[c]][:, 0:2 * HE], sg[:, r, c, 0:2 * HE],
                                                    ALU.mult)
                    i.then_inc(m_u.sem, 1)

            def add_out(t):
                m_y.done(dve, t)
                xb = xbase[:, t, :]
                nc.vector.scalar_tensor_tensor(out=xb, in0=bank["qkt"][:, 0:D], scalar=tg[:, 3:4], in1=xb,
                                               op0=ALU.mult, op1=ALU.add).then_inc(m_out.sem, 1)

            gated(0, 0)
            with dve.Fori(0, B // 2 - 1) as p:
                gated(p * 2 + 1, 1)
                add_out(p * 2)
                gated(p * 2 + 2, 0)
                add_out(p * 2 + 1)
            gated(B - 1, 1)
            add_out(B - 2)
            add_out(B - 1)

        @block.gpsimd
        def _(pool):
            for s in (pool_add, pool_norm):
                pool.sem_inc(s.sem, s.credit)
            nc.gpsimd.memset(kT[:, :, :, :], 0.0)
            pool.wait_ge(in_const, 16)
            pool.wait_ge(in_par, PAR)

            def tables(l):
                H = DH // 2
                nc.gpsimd.tensor_tensor(tab_cos[:, :, :], cst[:, C_COS:C_COS + 2 * DH].rearrange("p (m d) -> p m d", m=2),
                                        scales[:, l, :, :], ALU.mult)
                sin = cst[:, C_SIN:C_SIN + 2 * DH].rearrange("p (m d) -> p m d", m=2)
                nc.gpsimd.tensor_tensor(tab_sin[:, :, 0:H], sin[:, :, 0:H], scales[:, l, :, H:DH], ALU.mult)
                nc.gpsimd.tensor_tensor(tab_sin[:, :, H:DH], sin[:, :, H:DH], scales[:, l, :, 0:H], ALU.mult).then_inc(tab_ready.sem, 1)

            def stage_step(l, s, at, last):
                base = l * GPL
                half, f = ffn_step(s)
                unit = l * 2 + half if half is not None else None
                ch, cs = cross_step(s, last)
                ms = moe_step(s, last)
                n = at(1)
                if n is not None and not (last and n >= GPL):
                    g, r, r4 = base + n, n % 2, n % 4
                    pool.wait_ge(dve_rn, (g + 1) * (RS_OPS + 1))
                    pool_add.done(pool, g)
                    pe_T.free(pool, g, 4)
                    u = rot[:, :].rearrange("p (m h d) -> p m h d", m=2, d=DH)
                    rec = rn[:, r, 0:8].rearrange("p (m h) -> p m h", m=2).unsqueeze(3).to_broadcast([T, 2, HG, DH])
                    nc.gpsimd.tensor_tensor(q_n[:, r4, :].rearrange("p (h d) -> p h d", d=DH), u[:, 0], rec[:, 0], ALU.mult)
                    nc.gpsimd.tensor_tensor(k_n[:, r4, :].rearrange("p (h d) -> p h d", d=DH), u[:, 1], rec[:, 1],
                                            ALU.mult).then_inc(pool_norm.sem, 1)
                if f == 3:
                    if last:
                        dve_sh.done(pool, unit)
                    xb = xres[:, 4 * half:4 * half + 4, :]
                    nc.gpsimd.tensor_tensor(xb, xb, b2_all[:, l, :].unsqueeze(1).to_broadcast([T, 4, D]),
                                            ALU.add).then_inc(pool_b2.sem, 1)
                n = at(0)
                if n is not None and not (last and n >= GPL):
                    g, r = base + n, n % 2
                    dve_qk.done(pool, g)
                    pool_norm.free(pool, g, 1)
                    nc.gpsimd.tensor_tensor(rot[:, :], rot_a[:, r, :], rot_b[:, r, :], ALU.add).then_inc(pool_add.sem, 1)
                    if s == 20:
                        nc.gpsimd.tensor_copy(lpar[:, :], lpar_all[:, :, l]).then_inc(lpar_ready.sem, 1)
                    if s == GPL - 1 and not last:
                        tables(l + 1)
                n = at(4)
                if n is not None:
                    g, r = base + n, n % 2
                    dve_rs.done(pool, g)
                    nc.gpsimd.tensor_tensor(probs[:, r], probs[:, r], rsum[:, r, :].unsqueeze(2).to_broadcast([T, HG, T]),
                                            ALU.mult).then_inc(pool_pn.sem, 1)

            tables(0)
            pool.wait_ge(sim_act, 8)
            all_layers(stage_step)(pool)

            def weigh(t, r, half):
                m_u.done(pool, t * NCH + 2 * half + 1)
                part = mh[:, r, 2 * half:2 * half + 2, :].rearrange("p c (e h) -> p (c e) h", h=HE)
                i = nc.gpsimd.tensor_tensor(part, part, cw[:, t, E // 2 * half:E // 2 * (half + 1)].unsqueeze(2).to_broadcast(
                    [T, E // 2, HE]), ALU.mult)
                if half:
                    i.then_inc(m_w.sem, 1)

            def stage_tile(t, r):
                nc.gpsimd.tensor_copy(xcur[:, r, :], xfT[:, t, :]).then_inc(m_cur.sem, 1)

            xf_ready.done(pool, 1)
            stage_tile(0, 0)
            stage_tile(1, 1)
            xf_ready.done(pool, 2)
            pool.wait_ge(moe_dve, 3)
            weigh(0, 0, 0)
            weigh(0, 0, 1)
            with pool.Fori(0, B // 2 - 1) as p:
                weigh(p * 2 + 1, 1, 0)
                stage_tile(p * 2 + 2, 0)
                weigh(p * 2 + 1, 1, 1)
                weigh(p * 2 + 2, 0, 0)
                stage_tile(p * 2 + 3, 1)
                weigh(p * 2 + 2, 0, 1)
            weigh(B - 1, 1, 0)
            weigh(B - 1, 1, 1)


_IN = ['x', 'ctx_768', 'g_xattn', 'g_ffn', 'L0_xattn_Wv', 'L0_xattn_bv', 'L0_xattn_Wt', 'L0_xattn_bt', 'L0_ffn_Wqkv',
       'L0_ffn_q_scale', 'L0_ffn_k_scale', 'L0_ffn_Wo', 'L0_ffn_ln_g', 'L0_ffn_ln_b', 'L0_ffn_W1', 'L0_ffn_b1', 'L0_ffn_W2',
       'L0_ffn_b2', 'L1_xattn_Wq', 'L1_xattn_Wk', 'L1_xattn_Wv', 'L1_xattn_Wo', 'L1_xattn_bo', 'L1_ffn_Wg', 'L1_ffn_W1',
       'L1_ffn_W2', 'L1_ffn_Ws1', 'L1_ffn_Ws2']


def kernel(**inputs):
    import concourse.bacc as bacc
    from concourse.bass_utils import run_bass_kernel_spmd

    nc = bacc.Bacc("TRN2", target_bir_lowering=False, num_devices=1)
    arrays = {f"in_{n}": np.ascontiguousarray(inputs[n]) for n in _IN}
    arrays["in_consts"] = shape_constants()
    args = [nc.dram_tensor(n, a.shape, mybir.dt.from_np(a.dtype), kind="ExternalInput").ap() for n, a in arrays.items()]
    res = nc.dram_tensor("out", (B, T, D), F32, kind="ExternalOutput").ap()
    build(nc, *args, res)
    r = run_bass_kernel_spmd(nc, [arrays], core_ids=[0])
    return r.results[0]["out"]
```
